# Optimizing a Trainium2 kernel written in Bass

```python
import numpy as np
import jax
import jax.numpy as jnp

def _softmax(x, axis=-1):
    return jax.nn.softmax(x, axis=axis)

def _gelu(x):
    return jax.nn.gelu(x, approximate=True)

def _silu(x):
    return jax.nn.silu(x)

def _sigmoid(x):
    return jax.nn.sigmoid(x)

def _layernorm(x, axis=-1, eps=1e-05):
    m = jnp.mean(x, axis=axis, keepdims=True)
    v = jnp.var(x, axis=axis, keepdims=True)
    return (x - m) / jnp.sqrt(v + eps)

def _scatter_add(tgt, idx, src, axis=0):
    return tgt.at[idx].add(src)

def _segment_sum(src, seg, n):
    return jax.ops.segment_sum(src, seg, n)
kernel_name = 'mk_conv_attn_hybrid_d2_conv_nchw128_r2_0a0b21'

def setup_inputs(seed: int=0):
    np.random.seed(seed)
    _w = jnp.asarray

    def _rec_inputs():
        import jax
        import jax.numpy as jnp
        _gk = jax.random.key(seed)
        x = -0.0002928 + 1 * jax.random.normal(jax.random.fold_in(_gk, 1), (8, 64, 32, 32), jnp.float32)
        return x
    x = _rec_inputs()

    def _L0_conv_setup():
        import jax, jax.numpy as jnp
        import numpy as np
        EPS = 1e-05

        def conv2d(x, w, b, stride=1, pad=1):
            out = jax.lax.conv_general_dilated(x, w, (stride, stride), [(pad, pad), (pad, pad)], dimension_numbers=('NCHW', 'OIHW', 'NCHW'))
            return out + b[None, :, None, None]

        def bn_inf(x, gamma, beta, mean, var):
            inv = gamma / jnp.sqrt(var + EPS)
            return x * inv[None, :, None, None] + (beta - mean * inv)[None, :, None, None]

        def deform_conv(x, offset, weight, stride, pad, dil):
            B, Ci, H, W = x.shape
            Co, _, K, _ = weight.shape
            KK = K * K
            Ho = (H + 2 * pad - dil * (K - 1) - 1) // stride + 1
            Wo = (W + 2 * pad - dil * (K - 1) - 1) // stride + 1
            dy = offset[:, 0::2]
            dx = offset[:, 1::2]
            ky, kx = jnp.meshgrid(jnp.arange(K), jnp.arange(K), indexing='ij')
            ky = ky.reshape(KK).astype(x.dtype)
            kx = kx.reshape(KK).astype(x.dtype)
            base_y = (jnp.arange(Ho) * stride - pad).astype(x.dtype)
            base_x = (jnp.arange(Wo) * stride - pad).astype(x.dtype)
            ys = base_y[None, None, :, None] + (ky * dil)[None, :, None, None] + dy
            xs = base_x[None, None, None, :] + (kx * dil)[None, :, None, None] + dx
            y0 = jnp.floor(ys)
            x0 = jnp.floor(xs)
            fy = ys - y0
            fx = xs - x0

            def gather(img, iy, ix):
                valid = (iy >= 0) & (iy < H) & (ix >= 0) & (ix < W)
                iyc = jnp.clip(iy, 0, H - 1).astype(jnp.int32)
                ixc = jnp.clip(ix, 0, W - 1).astype(jnp.int32)
                v = img[:, iyc, ixc]
                return v * valid[None].astype(img.dtype)

            def sample_one(img, y0b, x0b, fyb, fxb):
                w00 = (1 - fyb) * (1 - fxb)
                w01 = (1 - fyb) * fxb
                w10 = fyb * (1 - fxb)
                w11 = fyb * fxb
                s = gather(img, y0b, x0b) * w00[None] + gather(img, y0b, x0b + 1) * w01[None] + gather(img, y0b + 1, x0b) * w10[None] + gather(img, y0b + 1, x0b + 1) * w11[None]
                return s
            sampled = jax.vmap(sample_one)(x, y0, x0, fy, fx)
            return jnp.einsum('oik,bikhw->bohw', weight.reshape(Co, Ci, KK), sampled)
        key = jax.random.key(seed)
        ks = jax.random.split(key, 16)
        B, C, H, W = (8, 64, 32, 32)
        d = dict(x=jax.random.normal(ks[0], (B, C, H, W), jnp.float32), w_off1=jax.random.normal(ks[1], (18, C, 3, 3), jnp.float32) * 0.01, b_off1=jnp.zeros((18,), jnp.float32), w_dc1=jax.random.normal(ks[2], (C, C, 3, 3), jnp.float32) * 0.05, g1=jnp.ones((C,), jnp.float32), beta1=jnp.zeros((C,), jnp.float32), m1=jax.random.normal(ks[3], (C,), jnp.float32) * 0.1, v1=jax.random.uniform(ks[4], (C,), jnp.float32) + 0.5, w_off2=jax.random.normal(ks[5], (18, C, 3, 3), jnp.float32) * 0.01, b_off2=jnp.zeros((18,), jnp.float32), w_dc2=jax.random.normal(ks[6], (C, C, 3, 3), jnp.float32) * 0.05, g2=jnp.ones((C,), jnp.float32), beta2=jnp.zeros((C,), jnp.float32), m2=jax.random.normal(ks[7], (C,), jnp.float32) * 0.1, v2=jax.random.uniform(ks[8], (C,), jnp.float32) + 0.5)
        return d
    _L0_conv_all = _L0_conv_setup()
    _L0_conv_in = {k: v for k, v in _L0_conv_all.items() if k in ('w_off1', 'b_off1', 'w_dc1', 'g1', 'beta1', 'm1', 'v1', 'w_off2', 'b_off2', 'w_dc2', 'g2', 'beta2', 'm2', 'v2')}
    del _L0_conv_all

    def _L1_attn_setup():
        import jax, jax.numpy as jnp
        import numpy as np
        EMB, HEADS, K = (64, 8, 32)
        key = jax.random.key(seed)
        ks = jax.random.split(key, 6)
        b, t, e, h = (2, 1024, EMB, HEADS)
        s = 1.0 / np.sqrt(e).astype(np.float32)
        x = jax.random.normal(ks[0], (b, t, e), jnp.float32)
        Wq = jax.random.normal(ks[1], (e * h, e), jnp.float32) * s
        Wk = jax.random.normal(ks[2], (e * h, e), jnp.float32) * s
        Wv = jax.random.normal(ks[3], (e * h, e), jnp.float32) * s
        Wu = jax.random.normal(ks[4], (e, h * e), jnp.float32) * (1.0 / np.sqrt(h * e).astype(np.float32))
        bu = jnp.zeros((e,), jnp.float32)
        return {'x': x, 'Wq': Wq, 'Wk': Wk, 'Wv': Wv, 'Wu': Wu, 'bu': bu}
    _L1_attn_all = _L1_attn_setup()
    _L1_attn_in = {k: v for k, v in _L1_attn_all.items() if k in ('Wq', 'Wk', 'Wv', 'Wu', 'bu')}
    del _L1_attn_all

    def _L1_ffn_setup():
        import jax, jax.numpy as jnp
        import numpy as np
        B, S, D, E, H, O, K = (256, 1024, 64, 32, 256, 64, 8)
        key = jax.random.key(seed)
        k0, k1, k2, k3 = jax.random.split(key, 4)
        x = jax.random.normal(k0, (B, S, D), dtype=jnp.float32)
        gate_w = jax.random.normal(k1, (E, D), dtype=jnp.float32) * (1.0 / np.sqrt(D))
        gate_b = jnp.zeros((E,), dtype=jnp.float32)
        weight1 = jax.random.uniform(k2, (E, D + 1, H), dtype=jnp.float32, minval=-1.0, maxval=1.0) * (1.0 / np.sqrt(D + 1))
        weight2 = jax.random.uniform(k3, (E, H + 1, O), dtype=jnp.float32, minval=-1.0, maxval=1.0) * (1.0 / np.sqrt(H + 1))
        return {'x': x, 'gate_w': gate_w, 'gate_b': gate_b, 'weight1': weight1, 'weight2': weight2}
    _L1_ffn_all = _L1_ffn_setup()
    _L1_ffn_in = {k: v for k, v in _L1_ffn_all.items() if k in ('gate_w', 'gate_b', 'weight1', 'weight2')}
    del _L1_ffn_all
    return {'x': x, 'L0_conv_w_off1': _L0_conv_in['w_off1'], 'L0_conv_b_off1': _L0_conv_in['b_off1'], 'L0_conv_w_dc1': _L0_conv_in['w_dc1'], 'L0_conv_g1': _L0_conv_in['g1'], 'L0_conv_beta1': _L0_conv_in['beta1'], 'L0_conv_m1': _L0_conv_in['m1'], 'L0_conv_v1': _L0_conv_in['v1'], 'L0_conv_w_off2': _L0_conv_in['w_off2'], 'L0_conv_b_off2': _L0_conv_in['b_off2'], 'L0_conv_w_dc2': _L0_conv_in['w_dc2'], 'L0_conv_g2': _L0_conv_in['g2'], 'L0_conv_beta2': _L0_conv_in['beta2'], 'L0_conv_m2': _L0_conv_in['m2'], 'L0_conv_v2': _L0_conv_in['v2'], 'L1_attn_Wq': _L1_attn_in['Wq'], 'L1_attn_Wk': _L1_attn_in['Wk'], 'L1_attn_Wv': _L1_attn_in['Wv'], 'L1_attn_Wu': _L1_attn_in['Wu'], 'L1_attn_bu': _L1_attn_in['bu'], 'L1_ffn_gate_w': _L1_ffn_in['gate_w'], 'L1_ffn_gate_b': _L1_ffn_in['gate_b'], 'L1_ffn_weight1': _L1_ffn_in['weight1'], 'L1_ffn_weight2': _L1_ffn_in['weight2']}

def reference(x, L0_conv_w_off1, L0_conv_b_off1, L0_conv_w_dc1, L0_conv_g1, L0_conv_beta1, L0_conv_m1, L0_conv_v1, L0_conv_w_off2, L0_conv_b_off2, L0_conv_w_dc2, L0_conv_g2, L0_conv_beta2, L0_conv_m2, L0_conv_v2, L1_attn_Wq, L1_attn_Wk, L1_attn_Wv, L1_attn_Wu, L1_attn_bu, L1_ffn_gate_w, L1_ffn_gate_b, L1_ffn_weight1, L1_ffn_weight2):
    import jax
    import jax.numpy as jnp

    def _L0_conv_ref(x, w_off1, b_off1, w_dc1, g1, beta1, m1, v1, w_off2, b_off2, w_dc2, g2, beta2, m2, v2):
        import jax, jax.numpy as jnp
        import numpy as np
        EPS = 1e-05

        def conv2d(x, w, b, stride=1, pad=1):
            out = jax.lax.conv_general_dilated(x, w, (stride, stride), [(pad, pad), (pad, pad)], dimension_numbers=('NCHW', 'OIHW', 'NCHW'))
            return out + b[None, :, None, None]

        def bn_inf(x, gamma, beta, mean, var):
            inv = gamma / jnp.sqrt(var + EPS)
            return x * inv[None, :, None, None] + (beta - mean * inv)[None, :, None, None]

        def deform_conv(x, offset, weight, stride, pad, dil):
            B, Ci, H, W = x.shape
            Co, _, K, _ = weight.shape
            KK = K * K
            Ho = (H + 2 * pad - dil * (K - 1) - 1) // stride + 1
            Wo = (W + 2 * pad - dil * (K - 1) - 1) // stride + 1
            dy = offset[:, 0::2]
            dx = offset[:, 1::2]
            ky, kx = jnp.meshgrid(jnp.arange(K), jnp.arange(K), indexing='ij')
            ky = ky.reshape(KK).astype(x.dtype)
            kx = kx.reshape(KK).astype(x.dtype)
            base_y = (jnp.arange(Ho) * stride - pad).astype(x.dtype)
            base_x = (jnp.arange(Wo) * stride - pad).astype(x.dtype)
            ys = base_y[None, None, :, None] + (ky * dil)[None, :, None, None] + dy
            xs = base_x[None, None, None, :] + (kx * dil)[None, :, None, None] + dx
            y0 = jnp.floor(ys)
            x0 = jnp.floor(xs)
            fy = ys - y0
            fx = xs - x0

            def gather(img, iy, ix):
                valid = (iy >= 0) & (iy < H) & (ix >= 0) & (ix < W)
                iyc = jnp.clip(iy, 0, H - 1).astype(jnp.int32)
                ixc = jnp.clip(ix, 0, W - 1).astype(jnp.int32)
                v = img[:, iyc, ixc]
                return v * valid[None].astype(img.dtype)

            def sample_one(img, y0b, x0b, fyb, fxb):
                w00 = (1 - fyb) * (1 - fxb)
                w01 = (1 - fyb) * fxb
                w10 = fyb * (1 - fxb)
                w11 = fyb * fxb
                s = gather(img, y0b, x0b) * w00[None] + gather(img, y0b, x0b + 1) * w01[None] + gather(img, y0b + 1, x0b) * w10[None] + gather(img, y0b + 1, x0b + 1) * w11[None]
                return s
            sampled = jax.vmap(sample_one)(x, y0, x0, fy, fx)
            return jnp.einsum('oik,bikhw->bohw', weight.reshape(Co, Ci, KK), sampled)
        off1 = conv2d(x, w_off1, b_off1, stride=1, pad=1)
        out = jax.nn.relu(bn_inf(deform_conv(x, off1, w_dc1, 1, 2, 2), g1, beta1, m1, v1))
        off2 = conv2d(out, w_off2, b_off2, stride=1, pad=1)
        out = bn_inf(deform_conv(out, off2, w_dc2, 1, 2, 2), g2, beta2, m2, v2)
        out = out + x
        return jax.nn.relu(out)

    def _L1_attn_ref(x, Wq, Wk, Wv, Wu, bu):
        import jax, jax.numpy as jnp
        import numpy as np
        EMB, HEADS, K = (64, 8, 32)
        b, t, e = x.shape
        h, k = (HEADS, K)
        tp = t + k - 1
        scale = e ** 0.25
        xp = jnp.pad(x, ((0, 0), (k - 1, 0), (0, 0)))
        q = (x @ Wq.T).reshape(b, t, h, e) / scale
        kk = (xp @ Wk.T).reshape(b, tp, h, e) / scale
        v = (xp @ Wv.T).reshape(b, tp, h, e)
        idx = jnp.arange(t)[:, None] + jnp.arange(k)[None, :]
        kw = kk[:, idx]
        vw = v[:, idx]
        dot = jnp.einsum('bthe,btkhe->bthk', q, kw)
        attn = jax.nn.softmax(dot, axis=-1)
        out = jnp.einsum('bthk,btkhe->bthe', attn, vw)
        out = out.reshape(b, t, h * e)
        return out @ Wu.T + bu

    def _L1_ffn_ref(x, gate_w, gate_b, weight1, weight2):
        import jax, jax.numpy as jnp
        import numpy as np
        B, S, D, E, H, O, K = (256, 1024, 64, 32, 256, 64, 8)
        Bn, Sn, Dn = x.shape
        logits = jnp.einsum('bsd,ed->bse', x, gate_w) + gate_b
        probs = jax.nn.softmax(logits, axis=1)
        vals, idx = jax.lax.top_k(probs.transpose(0, 2, 1), K)
        topv = vals.transpose(0, 2, 1)
        topi = idx.transpose(0, 2, 1)
        flat_idx = topi.reshape(Bn, K * E)
        gathered = jnp.take_along_axis(x, flat_idx[:, :, None], axis=1)
        gathered = gathered.reshape(Bn, K, E, Dn)
        pooled = jnp.einsum('bked,bke->bed', gathered, topv)
        ones = jnp.ones((E, Bn, 1), dtype=x.dtype)
        h = jnp.concatenate([pooled.transpose(1, 0, 2), ones], axis=-1)
        h = jax.nn.gelu(jnp.einsum('ebd,edh->ebh', h, weight1), approximate=False)
        h = jnp.concatenate([h, ones], axis=-1)
        out = jnp.einsum('ebh,eho->ebo', h, weight2)
        out = out.transpose(1, 0, 2)
        weighted = jnp.einsum('beo,bke->bkeo', out, topv).reshape(Bn, K * E, O)
        outputs = jnp.zeros((Bn, Sn, O), dtype=x.dtype)
        outputs = outputs.at[jnp.arange(Bn)[:, None], flat_idx].add(weighted)
        return outputs

    def _gn(v, G=32, eps=1e-05):
        B_, C_, H_, W_ = v.shape
        g = v.reshape(B_, G, C_ // G, H_, W_)
        m = jnp.mean(g, axis=(2, 3, 4), keepdims=True)
        s = jnp.var(g, axis=(2, 3, 4), keepdims=True)
        return ((g - m) / jnp.sqrt(s + eps)).reshape(v.shape)

    def _ln_c(v, eps=1e-06):
        m = jnp.mean(v, axis=1, keepdims=True)
        s = jnp.var(v, axis=1, keepdims=True)
        return (v - m) / jnp.sqrt(s + eps)

    def _ln_t(v, eps=1e-05):
        m = jnp.mean(v, axis=-1, keepdims=True)
        s = jnp.var(v, axis=-1, keepdims=True)
        return (v - m) / jnp.sqrt(s + eps)

    def _to_tokens(v):
        B_, C_, H_, W_ = v.shape
        return v.reshape(B_, C_, H_ * W_).transpose(0, 2, 1)

    def _from_tokens(t, like):
        B_, C_, H_, W_ = like.shape
        return t.transpose(0, 2, 1).reshape(B_, C_, H_, W_)
    x = _L0_conv_ref(x, L0_conv_w_off1, L0_conv_b_off1, L0_conv_w_dc1, L0_conv_g1, L0_conv_beta1, L0_conv_m1, L0_conv_v1, L0_conv_w_off2, L0_conv_b_off2, L0_conv_w_dc2, L0_conv_g2, L0_conv_beta2, L0_conv_m2, L0_conv_v2)
    t = _to_tokens(x)
    t = t + _L1_attn_ref(_ln_t(t), L1_attn_Wq, L1_attn_Wk, L1_attn_Wv, L1_attn_Wu, L1_attn_bu)
    t = t + _L1_ffn_ref(_ln_t(t), L1_ffn_gate_w, L1_ffn_gate_b, L1_ffn_weight1, L1_ffn_weight2)
    x = _from_tokens(t, x)
    return x

_drawn_inputs = setup_inputs


def setup_inputs(seed=0):
    import zlib

    import numpy as np

    out = dict(_drawn_inputs(seed))
    spreads = {'L0_conv_b_off1': (0.0, 0.1),
     'L0_conv_g1': (1.0, 0.2),
     'L0_conv_beta1': (0.0, 0.1),
     'L0_conv_b_off2': (0.0, 0.1),
     'L0_conv_g2': (1.0, 0.2),
     'L0_conv_beta2': (0.0, 0.1),
     'L1_attn_bu': (0.0, 0.1),
     'L1_ffn_gate_b': (0.0, 0.1)}
    factors = {'L1_ffn_gate_w': 8.0, 'L1_ffn_weight1': 8.0, 'L1_ffn_weight2': 8.0}
    for name, (base, spread) in spreads.items():
        noise = np.random.default_rng([zlib.crc32(name.encode()), seed]).standard_normal(out[name].shape)
        drawn = base * np.exp(spread * noise) if base else spread * noise
        out[name] = jnp.asarray(drawn.astype(out[name].dtype))
    for name, factor in factors.items():
        out[name] = (out[name] * factor).astype(out[name].dtype)
    return out
```

```python
import concourse.bass as bass
from concourse import mybir
from contextlib import ExitStack
import numpy as np

F32 = mybir.dt.float32
F16 = mybir.dt.float16
I32 = mybir.dt.int32
ALU = mybir.AluOpType
ACT = mybir.ActivationFunctionType
AX = mybir.AxisListType

NIMG, C, H, W = 8, 64, 32, 32
PAIRS = NIMG // 2
P = 128
PIX = H * W
TAPS = 9
NOFF = 2 * TAPS
PADR, PADC = 2, 1
HP, WP = H + 2 * PADR, W + 2 * PADC
BANK = 512
EPS_BN = 1e-5

CHUNK_ROWS = P // W
TILE = P
SPAN = 2 * TILE
REACH = 2.0
HAT_SCALE = 4096.0
ALIGNED = [CHUNK_ROWS * c for c in range(H // CHUNK_ROWS)]
SHIFTED = [CHUNK_ROWS * c - 2 for c in range(H // CHUNK_ROWS + 1)]
CHUNK_START = [ALIGNED, SHIFTED, ALIGNED]
CHUNK_BASE = [0, len(ALIGNED), len(ALIGNED) + len(SHIFTED)]
NCHUNK = 2 * len(ALIGNED) + len(SHIFTED)
SEL_BASE = [0, len(ALIGNED), 0]
NSEL = len(ALIGNED) + len(SHIFTED)
PX_ROW, PY_ROW, NCOORD = 64, 96, 97

HY_BANKS, S_SLOTS, TAP_SLOTS = 3, 6, 3


def near_steps():
    out = []
    for t in range(TAPS):
        ky = t // 3
        back = [0, 1, 1][ky]
        ranges = [(c, min(max(TILE * (c - back), 0), PIX - SPAN)) for c in range(len(CHUNK_START[ky]))]
        for k in range(0, len(ranges), 2):
            for image in range(2):
                out.append((t, image, ranges[k:k + 2]))
    return out


def all_steps():
    out = []
    for t in range(TAPS):
        for c in range(len(CHUNK_START[t // 3])):
            for p0 in range(0, PIX, 2 * SPAN):
                for image in range(2):
                    out.append((t, image, [(c, p0), (c, p0 + SPAN)]))
    return out


def y_pieces(g):
    n = len(CHUNK_START[g])
    return [(image, c, min(2, n - c)) for image in range(2) for c in range(0, n, 2)]


class Sampler:

    def __init__(self, sem, name, steps):
        self.steps = steps
        self.last_of_tap = [max(n for n, s in enumerate(steps) if s[0] == t) + 1 for t in range(TAPS)]
        self.first_of_tap = [min(n for n, s in enumerate(steps) if s[0] == t) for t in range(TAPS)]
        self.coord_in_psum = sem(name + "_coord_in_psum")
        self.coord_read = sem(name + "_coord_read")
        self.hat_ready = sem(name + "_hat_ready")
        self.hi_ready = sem(name + "_hi_ready")
        self.lo_ready = sem(name + "_lo_ready")
        self.stacked = [sem(f"{name}_stacked{s}") for s in range(TAP_SLOTS)]
        self.hx_in_psum = sem(name + "_hx_in_psum")
        self.hx_ready = sem(name + "_hx_ready")
        self.hy_in_psum = sem(name + "_hy_in_psum")
        self.s_ready = sem(name + "_s_ready")
        self.sampled = sem(name + "_sampled")
        self.y_in_psum = sem(name + "_y_in_psum")
        self.y_ready = sem(name + "_y_ready")
        self.source_ready = sem(name + "_source_ready")

    def y_count(self, g):
        return sum(len(y_pieces(k)) for k in range(g + 1))


class Conv:
    pass


def sampler_pe(nc, pe, m, cv, v, i):
    steps = v.steps
    nsteps = len(steps)
    ny = v.y_count(2)
    hx_seen = [0]
    coord_seen = [0]
    y_seen = [0]

    def coord(t):
        for half in range(2):
            n = coord_seen[0]
            if n >= 1:
                pe.wait_ge(v.coord_read, i * 2 * TAPS + n)
            nc.tensor.matmul(m.ps[:, m.COORD, :], m.sel_coord[0:NCOORD, t, :],
                             cv.off[0:NCOORD, bass.ds(i, 1), half * BANK:(half + 1) * BANK],
                             start=True, stop=True).then_inc(v.coord_in_psum, 1)
            coord_seen[0] += 1

    def columns(t):
        pe.wait_ge(v.stacked[t % TAP_SLOTS], i * (64 * TAPS // TAP_SLOTS) + 64 * (t // TAP_SLOTS + 1))
        for image in range(2):
            for half in range(2):
                n = hx_seen[0]
                if n >= 1:
                    pe.wait_ge(v.hx_ready, i * 4 * TAPS + n)
                nc.tensor.matmul(m.ps[:, m.HX, :], m.sel_x[:, :],
                                 m.stack[:, t % TAP_SLOTS, image, half * BANK:(half + 1) * BANK],
                                 start=True, stop=True).then_inc(v.hx_in_psum, 1)
                hx_seen[0] += 1

    def weighted(piece, g):
        image, c, k = piece
        n = y_seen[0]
        if n == 0:
            pe.wait_ge(v.source_ready, i + 1)
        else:
            pe.wait_ge(v.y_ready, i * ny + n)
        half = slice(C * image, C * image + C)
        for j in range(k):
            r0 = (CHUNK_START[g][c + j] + PADR) * W
            last = nc.tensor.matmul(m.ps[:, m.YB, j * 192:(j + 1) * 192], m.source[half, r0:r0 + P],
                                    cv.w_dc[half, 3 * g:3 * g + 3, :], start=True, stop=True)
        last.then_inc(v.y_in_psum, 1)
        y_seen[0] += 1

    def rows(n):
        t, image, parts = steps[n]
        if n >= HY_BANKS:
            pe.wait_ge(v.s_ready, i * nsteps + n - HY_BANKS + 1)
        for j, (c, p0) in enumerate(parts):
            last = nc.tensor.matmul(m.ps[:, m.HY + n % HY_BANKS, j * SPAN:(j + 1) * SPAN],
                                    m.sel_y[:, SEL_BASE[t // 3] + c, :],
                                    m.stack[:, t % TAP_SLOTS, image, p0:p0 + SPAN], start=True, stop=True)
        last.then_inc(v.hy_in_psum, 1)

    def sample(n):
        t = steps[n][0]
        pe.wait_ge(v.s_ready, i * nsteps + n + 2)
        if n == v.first_of_tap[3 * (t // 3)]:
            pe.wait_ge(v.y_ready, i * ny + v.y_count(t // 3))
        pieces = []
        for j, (c, p0) in enumerate(steps[n][2]):
            cuts = [p0, p0 + SPAN]
            if p0 < BANK < p0 + SPAN:
                cuts = [p0, BANK, p0 + SPAN]
            for a, b in zip(cuts[:-1], cuts[1:]):
                for image in range(2):
                    pieces.append((image, c, a, b, j * SPAN + a - p0))
        for image, c, a, b, at in pieces:
            last = nc.tensor.matmul(
                m.out[C * image:C * image + C, a:b],
                m.y[:, CHUNK_BASE[t // 3] + c, image, (t % 3) * C:(t % 3 + 1) * C],
                m.s[:, (n + image) % S_SLOTS, at:at + b - a], start=False, stop=True, skip_group_check=True)
        last.then_inc(v.sampled, 2)

    pe.wait_ge(cv.pair_free, i + 1)
    for half in range(2):
        nc.tensor.matmul(m.out[:, half * BANK:(half + 1) * BANK], m.zeros[:, 0:P], m.zeros[:, :],
                         start=True, stop=True, skip_group_check=True)
    coord(0)
    coord(1)
    for piece in y_pieces(0):
        weighted(piece, 0)
    columns(0)
    waiting = {t: [(p, t // 3 + 1) for p in y_pieces(t // 3 + 1)] for t in (0, 3)}
    rows(0)
    rows(1)
    pending = []
    for n in range(0, nsteps, 2):
        t = steps[n][0]
        if n == v.first_of_tap[t]:
            if t + 2 < TAPS:
                coord(t + 2)
            pending += waiting.get(t, [])
        if t + 1 < TAPS and n == v.last_of_tap[t] - 4:
            columns(t + 1)
        for k in (n + 2, n + 3):
            if k < nsteps:
                rows(k)
        sample(n)
        if pending:
            weighted(*pending.pop(0))


def sampler_act(nc, act, m, cv, v, i):
    nsteps = len(v.steps)
    ny = v.y_count(2)
    hx_seen = [0]
    coord_seen = [0]
    y_seen = [0]

    def hats(t):
        if t >= TAP_SLOTS:
            act.wait_ge(v.lo_ready, i * TAPS + t - TAP_SLOTS + 1)
        for half in range(2):
            coord_seen[0] += 1
            act.wait_ge(v.coord_in_psum, i * 2 * TAPS + coord_seen[0])
            nc.scalar.activation(m.hat[:, t % TAP_SLOTS, half * BANK:(half + 1) * BANK], m.ps[:, m.COORD, :],
                                 ACT.Abs, bias=m.coord_bias[:, t:t + 1]).then_inc(v.coord_read, 1)
        act.wait_ge(v.coord_read, i * 2 * TAPS + coord_seen[0])
        nc.scalar.activation(m.hat[:, t % TAP_SLOTS, :], m.hat[:, t % TAP_SLOTS, :], ACT.Relu,
                             bias=m.hat_scale[:, 0:1], scale=-HAT_SCALE).then_inc(v.hat_ready, 1)

    def columns(t):
        if t >= TAP_SLOTS:
            act.wait_ge(v.s_ready, i * nsteps + v.last_of_tap[t - TAP_SLOTS])
        for image in range(2):
            for half in range(2):
                hx_seen[0] += 1
                act.wait_ge(v.hx_in_psum, i * 4 * TAPS + hx_seen[0])
                nc.scalar.copy(m.hx[:, t % TAP_SLOTS, image, half * BANK:(half + 1) * BANK],
                               m.ps[:, m.HX, :]).then_inc(v.hx_ready, 1)

    def weighted(piece, g):
        image, c, k = piece
        y_seen[0] += 1
        act.wait_ge(v.y_in_psum, i * ny + y_seen[0])
        at = CHUNK_BASE[g] + c
        nc.scalar.copy(m.y[:, at:at + k, image, :],
                       m.ps[:, m.YB, 0:192 * k].rearrange("p (k n) -> p k n", k=k)).then_inc(v.y_ready, 1)

    act.wait_ge(cv.pair_free, i + 1)
    hats(0)
    hats(1)
    for piece in y_pieces(0):
        weighted(piece, 0)
    columns(0)
    waiting = {t: [(p, t // 3 + 1) for p in y_pieces(t // 3 + 1)] for t in (0, 3)}
    pending = []
    for n in range(0, nsteps, 2):
        t = v.steps[n][0]
        if n == v.first_of_tap[t]:
            if t + 2 < TAPS:
                hats(t + 2)
            pending += waiting.get(t, [])
        if t + 1 < TAPS and n == v.last_of_tap[t] - 4:
            columns(t + 1)
        if pending:
            weighted(*pending.pop(0))
    act.wait_ge(v.sampled, i * nsteps + nsteps)
    cv.finish(i).then_inc(cv.pair_free, 1)


def sampler_dve(nc, dve, m, cv, v, i):
    nsteps = len(v.steps)
    dve.wait_ge(cv.pair_free, i + 1)
    for n, (t, image, parts) in enumerate(v.steps):
        dve.wait_ge(v.hy_in_psum, i * nsteps + n + 1)
        if n - image == v.first_of_tap[t]:
            dve.wait_ge(v.hx_ready, i * 4 * TAPS + 4 * t + 2 * image + 2)
        if n >= S_SLOTS:
            dve.wait_ge(v.sampled, i * nsteps + 2 * ((n - S_SLOTS) // 2) + 2)
        width = SPAN * len(parts)
        p0 = parts[0][1]
        step = parts[-1][1] - p0
        hx = m.hx[:, t % TAP_SLOTS, image, p0:p0 + SPAN]
        if len(parts) == 2:
            hx = bass.AP(hx.tensor, hx.offset, [hx.ap[0], [step, 2], [1, SPAN]])
        nc.vector.tensor_tensor(m.s[:, n % S_SLOTS, 0:width].rearrange("p (k n) -> p k n", n=SPAN)
                                if len(parts) == 2 else m.s[:, n % S_SLOTS, 0:width],
                                hx,
                                m.ps[:, m.HY + n % HY_BANKS, 0:width].rearrange("p (k n) -> p k n", n=SPAN)
                                if len(parts) == 2 else m.ps[:, m.HY + n % HY_BANKS, 0:width],
                                ALU.mult).then_inc(v.s_ready, 1)


def sampler_pool(nc, pool, m, cv, v, i):
    pool.wait_ge(cv.pair_free, i + 1)
    nc.gpsimd.tensor_copy(m.source[:, :].rearrange("p (r c) -> p r c", c=W),
                          cv.src[:, i, :].rearrange("p (r c) -> p r c", c=WP)[:, :, PADC:PADC + W]
                          ).then_inc(v.source_ready, 1)
    for t in range(TAPS):
        slot = t % TAP_SLOTS
        pool.wait_ge(v.hat_ready, i * TAPS + t + 1)
        if t >= TAP_SLOTS:
            pool.wait_ge(v.stacked[slot], i * (64 * TAPS // TAP_SLOTS) + 64 * (t // TAP_SLOTS))
        nc.gpsimd.tensor_copy(m.hi[:, slot, :], m.hat[:, slot, :]).then_inc(v.hi_ready, 1)
        pool.wait_ge(v.hi_ready, i * TAPS + t + 1)
        nc.gpsimd.tensor_tensor(m.lo[:, slot, :], m.hat[:, slot, :], m.hi[:, slot, :],
                                ALU.subtract).then_inc(v.lo_ready, 1)


def sampler_sp(nc, sp, m, cv, v, i):
    nsteps = len(v.steps)
    sp.wait_ge(cv.pair_free, i + 1)
    for t in range(TAPS):
        slot = t % TAP_SLOTS
        if t >= TAP_SLOTS:
            sp.wait_ge(v.hy_in_psum, i * nsteps + v.last_of_tap[t - TAP_SLOTS])
        sp.wait_ge(v.hi_ready, i * TAPS + t + 1)
        for image in range(2):
            sp.dma_start(m.stack[0:C, slot, image, :], m.hi[C * image:C * image + C, slot, :]
                         ).then_inc(v.stacked[slot], 16)
        sp.wait_ge(v.lo_ready, i * TAPS + t + 1)
        for image in range(2):
            sp.dma_start(m.stack[C:P, slot, image, :], m.lo[C * image:C * image + C, slot, :]
                         ).then_inc(v.stacked[slot], 16)


HEADS, WINDOW, TQ = 8, 32, 32
HG = 2
H4 = HEADS // HG
KEYS = TQ + WINDOW
TILES = P // TQ
BLOCKS = PIX // P
UNITS = 2 * BLOCKS
EPS_LN = 1e-5
P_SLOTS = 3
MASK_SCALE, MASKED = 32768.0, -65504.0


class Attention:
    pass


class Experts:
    pass


def attention_pe(nc, pe, m, at, i):
    pe.wait_ge(at.pair_done, i + 1)
    for half in range(2):
        nc.tensor.matmul(m.ps[:, half, :], m.mean_of[:, :],
                         m.tokens[:, bass.ds(i, 1), half * BANK:(half + 1) * BANK],
                         start=True, stop=True).then_inc(at.mean_in_psum, 1)
    for half in range(2):
        pe.wait_ge(at.squared, i * 2 + half + 1)
        nc.tensor.matmul(m.ps[:, 2 + half, :], m.mean_of[:, :], at.square[:, half * BANK:(half + 1) * BANK],
                         start=True, stop=True).then_inc(at.var_in_psum, 1)
    pe.wait_ge(at.xh_ready, i + 1)

    def project_queries(b):
        if b >= 1:
            pe.wait_ge(at.g_ready, i * 2 * BLOCKS + 2 * b)
        for hg in range(HG):
            for h in range(H4):
                last = nc.tensor.matmul(m.ps[:, hg, h * P:(h + 1) * P], at.a_heads[:, hg * H4 + h, :],
                                        at.xh[:, WINDOW + b * P:WINDOW + (b + 1) * P], start=True, stop=True)
            last.then_inc(at.g_in_psum, 1)

    def turn_keys(b):
        if b >= 1:
            pe.wait_ge(at.xw_ready, i * 2 * BLOCKS + 2 * b)
        pe.wait_ge(at.windows_ready, i * BLOCKS + b + 1)
        for j in range(TILES):
            last = nc.tensor.transpose(m.ps[:, 5, j * P:(j + 1) * P], at.windows[:, b % 2, j, :], m.identity[:, :])
        last.then_inc(at.xw_in_psum, 1)

    def scores(v):
        b, image = divmod(v, 2)
        if image == 0:
            pe.wait_ge(at.g_ready, i * 2 * BLOCKS + 2 * b + 2)
        if v >= 2:
            pe.wait_ge(at.shifted, i * UNITS + v - 1)
        half = slice(C * image, C * image + C)
        nc.tensor.matmul(m.ps[:, 2 + image, :], m.identity16[:, :], m.mask[:, :], start=True, stop=False,
                         skip_group_check=True)
        for j in range(TILES):
            for hg in range(HG):
                last = nc.tensor.matmul(
                    m.ps[:, 2 + image, (j * HG + hg) * KEYS:(j * HG + hg + 1) * KEYS],
                    at.g[half, b % 2, hg, j, :],
                    at.xh[half, b * P + j * TQ:b * P + j * TQ + KEYS], start=False, stop=True, skip_group_check=True)
        last.then_inc(at.scores_in_psum, 1)

    def turn_probs(v):
        pe.wait_ge(at.probs_ready, i * UNITS + v + 1)
        if v >= 1:
            pe.wait_ge(at.pt_ready, i * UNITS + v)
        for j in range(TILES):
            last = nc.tensor.transpose(m.ps[:, 4, j * P:(j + 1) * P], at.pn[:, v % P_SLOTS, j * P:(j + 1) * P],
                                       m.identity[:, :])
        last.then_inc(at.pt_in_psum, 1)

    def values(v):
        b, image = divmod(v, 2)
        pe.wait_ge(at.pt_ready, i * UNITS + v + 1)
        if image == 0:
            pe.wait_ge(at.xw_ready, i * 2 * BLOCKS + 2 * b + 2)
        if v >= 1:
            pe.wait_ge(at.z_ready, i * UNITS + v)
        for j in range(TILES):
            last = nc.tensor.matmul(m.ps[:, 6, j * P:(j + 1) * P], at.xw[:, b % 2, image, j, :],
                                    at.pt[:, v % 2, j * P:(j + 1) * P], start=True, stop=True)
        last.then_inc(at.z_in_psum, 1)

    def project_values(v):
        b, image = divmod(v, 2)
        pe.wait_ge(at.z_ready, i * UNITS + v + 1)
        if b >= 2 and image == 0:
            pe.wait_ge(at.added, i * BLOCKS + b - 1)
        z = at.z[:, v % 2, :].rearrange("p (j h q) -> p h j q", j=TILES, h=H4)
        for h in range(H4):
            last = nc.tensor.matmul(m.ps[C * image:C * image + C, 7, (b % 2) * P:(b % 2 + 1) * P],
                                    at.b_heads[:, h, :], z[:, h, :, :], start=(h == 0), stop=(h == H4 - 1),
                                    skip_group_check=True)
        last.then_inc(at.projected, 1)

    project_queries(0)
    turn_keys(0)
    for v in range(UNITS + 2):
        if v < UNITS:
            scores(v)
        if v >= 2:
            values(v - 2)
        if v % 2 == 1 and v + 1 < UNITS:
            project_queries((v + 1) // 2)
        if v % 2 == 1 and 1 < v + 1 < UNITS:
            turn_keys((v + 1) // 2)
        if 1 <= v < UNITS + 1:
            turn_probs(v - 1)
        if v >= 2:
            project_values(v - 2)


def attention_act(nc, act, m, at, i):
    for half in range(2):
        act.wait_ge(at.centred, i * 2 + half + 1)
        cols = slice(half * BANK, (half + 1) * BANK)
        nc.scalar.activation(at.square[:, cols], at.xh[:, WINDOW + half * BANK:WINDOW + (half + 1) * BANK],
                             ACT.Square).then_inc(at.squared, 1)
    for half in range(2):
        act.wait_ge(at.var_in_psum, i * 2 + half + 1)
        nc.scalar.activation(at.std[:, half * BANK:(half + 1) * BANK], m.ps[:, 2 + half, :], ACT.Sqrt,
                             bias=m.eps_ln[:, 0:1]).then_inc(at.std_ready, 1)

    def queries(b):
        if b >= 2:
            act.wait_ge(at.scores_in_psum, i * UNITS + 2 * (b - 1))
        for hg in range(HG):
            act.wait_ge(at.g_in_psum, i * 2 * BLOCKS + 2 * b + hg + 1)
            nc.scalar.copy(at.g[:, b % 2, hg, :, :].rearrange("p j (h q) -> p h j q", h=H4),
                           m.ps[:, hg, :].rearrange("p (h j q) -> p h j q", h=H4, j=TILES)).then_inc(at.g_ready, 1)

    queries(0)
    for v in range(UNITS + 2):
        if v >= 2:
            act.wait_ge(at.z_in_psum, i * UNITS + v - 1)
            if v >= 4:
                act.wait_ge(at.projected, i * UNITS + v - 3)
            nc.scalar.copy(at.z[:, v % 2, :], m.ps[:, 6, :]).then_inc(at.z_ready, 1)
        if v < UNITS:
            act.wait_ge(at.shifted, i * UNITS + v + 1)
            nc.scalar.activation(at.p[:, v % P_SLOTS, :], at.p[:, v % P_SLOTS, :], ACT.Exp).then_inc(at.exp_ready, 1)
        if v % 2 == 1 and v + 1 < UNITS:
            queries((v + 1) // 2)
        if 1 <= v < UNITS + 1:
            act.wait_ge(at.pt_in_psum, i * UNITS + v)
            if v >= 3:
                act.wait_ge(at.z_in_psum, i * UNITS + v - 2)
            nc.scalar.copy(at.pt[:, (v - 1) % 2, :], m.ps[:, 4, :]).then_inc(at.pt_ready, 1)


def attention_dve(nc, dve, m, at, i):
    dve.wait_ge(at.pair_done, i + 1)
    for half in range(2):
        dve.wait_ge(at.mean_in_psum, i * 2 + half + 1)
        nc.vector.tensor_tensor(at.xh[:, WINDOW + half * BANK:WINDOW + (half + 1) * BANK],
                                m.tokens[:, bass.ds(i, 1), half * BANK:(half + 1) * BANK].rearrange("p a n -> p (a n)"),
                                m.ps[:, half, :], ALU.subtract).then_inc(at.centred, 1)
    dve.wait_ge(at.std_ready, i * 2 + 2)
    nc.vector.reciprocal(at.std[:, :], at.std[:, :]).then_inc(at.rstd_ready, 1)
    dve.wait_ge(at.rstd_ready, i + 1)
    nc.vector.tensor_tensor(at.xh[:, WINDOW:WINDOW + PIX], at.xh[:, WINDOW:WINDOW + PIX], at.std[:, :],
                            ALU.mult).then_inc(at.xh_ready, 1)

    def keys(b):
        dve.wait_ge(at.xw_in_psum, i * BLOCKS + b + 1)
        if b >= 2:
            dve.wait_ge(at.z_in_psum, i * UNITS + 2 * (b - 1))
        for hg in range(HG):
            rows = slice(KEYS * hg, KEYS * hg + KEYS)
            nc.vector.tensor_copy(at.xw[rows, b % 2, :, :, hg * C:(hg + 1) * C].rearrange("p a j c -> p j a c"),
                                  m.ps[rows, 5, :].rearrange("p (j a c) -> p j a c", j=TILES, a=2)
                                  ).then_inc(at.xw_ready, 1)

    keys(0)
    for v in range(UNITS + 2):
        if v < UNITS:
            image = v % 2
            bank = m.ps[:, 2 + image, :].rearrange("p (g k) -> p g k", k=KEYS)
            st = at.stats[:, v % P_SLOTS, :, :]
            dve.wait_ge(at.scores_in_psum, i * UNITS + v + 1)
            if v >= P_SLOTS:
                dve.wait_ge(at.probs_ready, i * UNITS + v - P_SLOTS + 1)
            nc.vector.tensor_reduce(st[:, 0, :], bank, AX.X, ALU.max).then_inc(at.max_ready, 1)
            dve.wait_ge(at.max_ready, i * UNITS + v + 1)
            nc.vector.tensor_tensor(at.p[:, v % P_SLOTS, :].rearrange("p (g k) -> p g k", k=KEYS), bank,
                                    st[:, 0, :].unsqueeze(2).to_broadcast([P, TILES * HG, KEYS]),
                                    ALU.subtract).then_inc(at.shifted, 1)
        if v % 2 == 1 and v >= 3:
            b = (v - 3) // 2
            dve.wait_ge(at.projected, i * UNITS + 2 * b + 2)
            tok = m.tokens[:, bass.ds(i, 1), b * P:(b + 1) * P].rearrange("p a n -> p (a n)")
            nc.vector.scalar_tensor_tensor(tok, m.ps[:, 7, (b % 2) * P:(b % 2 + 1) * P], m.bu[:, 0:1], tok,
                                           ALU.add, ALU.add).then_inc(at.added, 1)
        if v % 2 == 1 and v + 1 < UNITS:
            keys((v + 1) // 2)
        if v < UNITS:
            dve.wait_ge(at.exp_ready, i * UNITS + v + 1)
            nc.vector.tensor_reduce(st[:, 1, :], at.p[:, v % P_SLOTS, :].rearrange("p (g k) -> p g k", k=KEYS),
                                    AX.X, ALU.add).then_inc(at.sum_ready, 1)
            dve.wait_ge(at.sum_ready, i * UNITS + v + 1)
            nc.vector.reciprocal(st[:, 2, :], st[:, 1, :]).then_inc(at.rsum_ready, 1)
    dve.wait_ge(at.added, i * BLOCKS + BLOCKS)
    nc.vector.tensor_copy(at.mark[:, 0:1], m.bu[:, 0:1]).then_inc(at.pair_done, 1)


def attention_pool(nc, pool, m, at, i):
    def windows(b):
        if b >= 2:
            pool.wait_ge(at.xw_in_psum, i * BLOCKS + b - 1)
        first = at.xh[:, b * P:b * P + KEYS]
        nc.gpsimd.tensor_copy(at.windows[:, b % 2, :, :].rearrange("p j (a k) -> p j a k", a=2),
                              bass.AP(first.tensor, first.offset, [first.ap[0], [TQ, TILES], [0, 2], [1, KEYS]])
                              ).then_inc(at.windows_ready, 1)

    pool.wait_ge(at.xh_ready, i + 1)
    windows(0)
    windows(1)
    for v in range(UNITS):
        if v % 2 == 1 and (v + 3) // 2 < BLOCKS:
            windows((v + 3) // 2)
        pool.wait_ge(at.rsum_ready, i * UNITS + v + 1)
        if v >= P_SLOTS:
            pool.wait_ge(at.pt_in_psum, i * UNITS + v - P_SLOTS + 1)
        nc.gpsimd.tensor_tensor(at.pn[:, v % P_SLOTS, :].rearrange("p (g k) -> p g k", k=KEYS),
                                at.p[:, v % P_SLOTS, :].rearrange("p (g k) -> p g k", k=KEYS),
                                at.stats[:, v % P_SLOTS, 2, :].unsqueeze(2).to_broadcast([P, TILES * HG, KEYS]),
                                ALU.mult).then_inc(at.probs_ready, 1)


EXPERTS, TOPK, HID = 32, 8, 256
GROUPS = NIMG * EXPERTS // P
PER_GROUP = NIMG // GROUPS
CHUNKS = PIX // P
MH = HID // P


def experts_pe(nc, pe, m, ex):
    for pr in range(PAIRS):
        if pr:
            pe.wait_ge(ex.xh_ready, pr)
        for half in range(2):
            nc.tensor.matmul(m.ps[:, half, :], m.mean_of[:, :], m.tokens[:, pr, half * BANK:(half + 1) * BANK],
                             start=True, stop=True).then_inc(ex.mean_in_psum, 1)
        for half in range(2):
            pe.wait_ge(ex.squared, 2 * pr + half + 1)
            nc.tensor.matmul(m.ps[:, 2 + half, :], m.mean_of[:, :], ex.square[:, half * BANK:(half + 1) * BANK],
                             start=True, stop=True).then_inc(ex.var_in_psum, 1)
        pe.wait_ge(ex.xh_ready, pr + 1)
        for half in range(2):
            last = nc.tensor.matmul(m.ps[2 * EXPERTS * (pr % 2):2 * EXPERTS * (pr % 2 + 1), 4 + 2 * (pr // 2) + half, :],
                                    m.w_gate[:, :], ex.xh[:, pr, half * BANK:(half + 1) * BANK], start=True, stop=True)
        last.then_inc(ex.logits_in_psum, 1)
    for c in range(CHUNKS):
        if c >= 4:
            pe.wait_ge(ex.xt_ready, c - 3)
        for pr in range(PAIRS):
            last = nc.tensor.transpose(m.ps[:, c % 4, pr * P:(pr + 1) * P], ex.xh[:, pr, c * P:(c + 1) * P],
                                       m.identity[:, :])
        last.then_inc(ex.xt_in_psum, 1)
    for g in range(GROUPS):
        pe.wait_ge(ex.picked, g + 1)
        for q in range(2):
            for c in range(4):
                last = nc.tensor.transpose(m.ps[:, 4 + 2 * g + q, c * P:(c + 1) * P],
                                           ex.pick[:, g, (4 * q + c) * P:(4 * q + c + 1) * P], m.identity[:, :])
            last.then_inc(ex.pt_in_psum, 1)
    pe.wait_ge(ex.xt_ready, CHUNKS)
    pe.wait_ge(ex.pt_ready, 2 * GROUPS)
    for b in range(NIMG):
        for c in range(CHUNKS):
            last = nc.tensor.matmul(m.ps[0:C, 0, b * EXPERTS:(b + 1) * EXPERTS],
                                    ex.xt[:, c, b // 2, (b % 2) * C:(b % 2 + 1) * C],
                                    ex.pt[:, c, b * EXPERTS:(b + 1) * EXPERTS], start=(c == 0), stop=(c == CHUNKS - 1))
    last.then_inc(ex.pooled_in_psum, 1)
    pe.wait_ge(ex.pooled_ready, 1)
    pe.wait_ge(ex.ones_set, 1)
    pe.wait_ge(ex.w_loaded, 48)
    for e in range(EXPERTS):
        for k in range(MH):
            last = nc.tensor.matmul(m.ps[:, 1, (k * EXPERTS + e) * NIMG:(k * EXPERTS + e + 1) * NIMG],
                                    ex.w1[0:C + 1, e, k * P:(k + 1) * P], ex.pooled[0:C + 1, e, :],
                                    start=True, stop=True)
    last.then_inc(ex.hidden_in_psum, 1)
    pe.wait_ge(ex.hidden_ready, 1)
    for e in range(EXPERTS):
        dst = m.ps[0:C, 2, e * NIMG:(e + 1) * NIMG]
        nc.tensor.matmul(dst, ex.w2_bias[0:1, e, :], m.ones[0:1, 0:NIMG], start=True, stop=False)
        for k in range(MH):
            last = nc.tensor.matmul(dst, ex.w2[:, k, e, :], ex.hidden[:, k, e, :], start=False, stop=(k == MH - 1))
    last.then_inc(ex.answer_in_psum, 1)
    pe.wait_ge(ex.answer_ready, 1)
    for g in range(GROUPS):
        last = nc.tensor.transpose(m.ps[:, 3, g * C:(g + 1) * C], ex.answer[0:C, g * P:(g + 1) * P],
                                   m.identity[0:C, 0:C])
    last.then_inc(ex.answer_turned, 1)
    pe.wait_ge(ex.answer_sb, 1)
    for pr in range(PAIRS):
        if pr >= 2:
            pe.wait_ge(ex.joined, pr - 1)
        for image in range(2):
            b = 2 * pr + image
            rows = slice(EXPERTS * (b % PER_GROUP), EXPERTS * (b % PER_GROUP + 1))
            for half in range(2):
                last = nc.tensor.matmul(m.ps[C * image:C * image + C, 4 + 2 * (pr % 2) + half, :],
                                        ex.answers[rows, b // PER_GROUP, :],
                                        ex.pick[rows, b // PER_GROUP, half * BANK:(half + 1) * BANK],
                                        start=True, stop=True, skip_group_check=True)
        last.then_inc(ex.spread, 1)


def experts_act(nc, act, m, ex):
    for pr in range(PAIRS):
        for half in range(2):
            act.wait_ge(ex.centred, 2 * pr + half + 1)
            cols = slice(half * BANK, (half + 1) * BANK)
            nc.scalar.activation(ex.square[:, cols], ex.xh[:, pr, cols], ACT.Square).then_inc(ex.squared, 1)
        if pr:
            act.wait_ge(ex.xh_ready, pr)
        for half in range(2):
            act.wait_ge(ex.var_in_psum, 2 * pr + half + 1)
            nc.scalar.activation(ex.std[:, half * BANK:(half + 1) * BANK], m.ps[:, 2 + half, :], ACT.Sqrt,
                                 bias=m.eps_ln[:, 0:1]).then_inc(ex.std_ready, 1)
    for g in range(GROUPS):
        act.wait_ge(ex.logits_in_psum, 2 * g + 2)
        for half in range(2):
            nc.scalar.activation(ex.pick[:, g, half * BANK:(half + 1) * BANK], m.ps[:, 4 + 2 * g + half, :],
                                 ACT.Identity, bias=m.b_gate[:, 0:1]).then_inc(ex.logits_ready, 1)
    for g in range(GROUPS):
        act.wait_ge(ex.gate_max, g + 1)
        nc.scalar.activation(ex.pick[:, g, :], ex.pick[:, g, :], ACT.Exp, bias=ex.neg_max[:, g:g + 1],
                             accum_out=ex.gate_sum[:, g:g + 1]).then_inc(ex.gate_exp, 1)
    for c in range(CHUNKS):
        act.wait_ge(ex.xt_in_psum, c + 1)
        nc.scalar.copy(ex.xt[:, c, :, :], m.ps[:, c % 4, :].rearrange("p (r n) -> p r n", r=PAIRS)
                       ).then_inc(ex.xt_ready, 1)
    for g in range(GROUPS):
        for q in range(2):
            act.wait_ge(ex.pt_in_psum, 2 * g + q + 1)
            nc.scalar.copy(ex.pt[:, 4 * q:4 * q + 4, g * P:(g + 1) * P],
                           m.ps[:, 4 + 2 * g + q, :].rearrange("p (c n) -> p c n", c=4)).then_inc(ex.pt_ready, 1)
    act.wait_ge(ex.hidden_in_psum, 1)
    nc.scalar.activation(ex.hidden[:, :, :, :], m.ps[:, 1, :].rearrange("p (k e b) -> p k e b", k=MH, e=EXPERTS),
                         ACT.Gelu).then_inc(ex.hidden_ready, 1)


def experts_dve(nc, dve, m, ex):
    for pr in range(PAIRS):
        for half in range(2):
            cols = slice(half * BANK, (half + 1) * BANK)
            dve.wait_ge(ex.mean_in_psum, 2 * pr + half + 1)
            nc.vector.tensor_tensor(ex.xh[:, pr, cols], m.tokens[:, pr, cols], m.ps[:, half, :],
                                    ALU.subtract).then_inc(ex.centred, 1)
        dve.wait_ge(ex.std_ready, 2 * pr + 2)
        nc.vector.reciprocal(ex.std[:, :], ex.std[:, :]).then_inc(ex.rstd_ready, 1)
        dve.wait_ge(ex.rstd_ready, pr + 1)
        nc.vector.tensor_tensor(ex.xh[:, pr, :], ex.xh[:, pr, :], ex.std[:, :], ALU.mult).then_inc(ex.xh_ready, 1)
    for g in range(GROUPS):
        dve.wait_ge(ex.logits_ready, 2 * g + 2)
        nc.vector.max(ex.top[:, g, 0, :], ex.pick[:, g, :]).then_inc(ex.top_steps, 1)
        dve.wait_ge(ex.top_steps, g + 1)
        nc.vector.tensor_scalar(ex.neg_max[:, g:g + 1], ex.top[:, g, 0, 0:1], -1.0, None, ALU.mult
                                ).then_inc(ex.gate_max, 1)
    for g in range(GROUPS):
        dve.wait_ge(ex.gate_exp, g + 1)
        nc.vector.max(ex.top[:, g, 1, :], ex.pick[:, g, :]).then_inc(ex.pick_steps, 1)
        nc.vector.reciprocal(ex.gate_rsum[:, g:g + 1], ex.gate_sum[:, g:g + 1]).then_inc(ex.rsum_ready, 1)
        dve.wait_ge(ex.pick_steps, 3 * g + 1)
        nc.vector.match_replace(ex.rest[:, g, :], ex.top[:, g, 1, :], ex.pick[:, g, :], 0.0).then_inc(ex.pick_steps, 1)
        dve.wait_ge(ex.pick_steps, 3 * g + 2)
        nc.vector.tensor_tensor(ex.rest[:, g, :], ex.pick[:, g, :], ex.rest[:, g, :], ALU.subtract
                                ).then_inc(ex.pick_steps, 1)
        dve.wait_ge(ex.pick_steps, 3 * g + 3)
        dve.wait_ge(ex.rsum_ready, g + 1)
        nc.vector.tensor_scalar(ex.pick[:, g, :], ex.rest[:, g, :], ex.gate_rsum[:, g:g + 1], None, ALU.mult
                                ).then_inc(ex.picked, 1)
    dve.wait_ge(ex.pooled_in_psum, 1)
    nc.vector.tensor_copy(ex.pooled[0:C, :, :].rearrange("p e b -> p b e"),
                          m.ps[0:C, 0, 0:NIMG * EXPERTS].rearrange("p (b e) -> p b e", b=NIMG)
                          ).then_inc(ex.pooled_ready, 1)
    dve.wait_ge(ex.answer_in_psum, 1)
    nc.vector.tensor_copy(ex.answer[0:C, :].rearrange("p (b e) -> p e b", b=NIMG),
                          m.ps[0:C, 2, 0:NIMG * EXPERTS].rearrange("p (e b) -> p e b", b=NIMG)
                          ).then_inc(ex.answer_ready, 1)
    dve.wait_ge(ex.answer_turned, 1)
    nc.vector.tensor_copy(ex.answers[:, :, :], m.ps[:, 3, 0:GROUPS * C].rearrange("p (g c) -> p g c", g=GROUPS)
                          ).then_inc(ex.answer_sb, 1)
    for pr in range(PAIRS):
        dve.wait_ge(ex.spread, pr + 1)
        nc.vector.tensor_tensor(m.tokens[:, pr, :], m.tokens[:, pr, :],
                                m.ps[:, 4 + 2 * (pr % 2):6 + 2 * (pr % 2), :].rearrange("p a n -> p (a n)"),
                                ALU.add).then_inc(ex.joined, 1)


class Memory:
    pass


def program(nc, a, out):
    ctx = ExitStack()
    with ctx:
        def sb(name, shape, dt=F32):
            return ctx.enter_context(nc.sbuf_tensor(name, shape, dt))

        def sem(name):
            return ctx.enter_context(nc.semaphore(name))

        m = Memory()
        m.ps = ctx.enter_context(nc.psum_tensor("banks", [P, 8, BANK], F32))
        m.out = m.ps[:, 0:2, :].rearrange("p b n -> p (b n)")
        m.HY, m.HX, m.COORD, m.YB = 2, 5, 6, 7
        m.sel_coord = sb("sel_coord", [P, TAPS, P])
        m.coord_bias = sb("coord_bias", [P, TAPS])
        m.hat_scale = sb("hat_scale", [P, 1])
        m.sel_x = sb("sel_x", [P, P], F16)
        m.sel_y = sb("sel_y", [P, NSEL, P], F16)
        m.identity = sb("identity", [P, P])
        m.zeros = sb("zeros", [P, BANK], F16)
        m.source = sb("source", [P, HP * W])
        m.hat = sb("hat", [P, TAP_SLOTS, PIX])
        m.hi = sb("hi", [P, TAP_SLOTS, PIX], F16)
        m.lo = sb("lo", [P, TAP_SLOTS, PIX], F16)
        m.stack = sb("stack", [P, TAP_SLOTS, 2, PIX], F16)
        m.hx = sb("hx", [P, TAP_SLOTS, 2, PIX])
        m.y = sb("y", [P, NCHUNK, 2, 192])
        m.s = sb("s", [P, S_SLOTS, 2 * SPAN])
        m.tokens = sb("tokens", [P, PAIRS, PIX])
        bn = sb("bn", [P, 2, 4])
        bn_inv = sb("bn_inv", [P, 2])
        bn_shift = sb("bn_shift", [P, 2])
        bn_tmp = sb("bn_tmp", [P, 4])
        abs_max = sb("abs_max", [P, 2])
        far = sb("far", [1, 4])
        far_flag = sb("far_flag", [1, 2], I32)
        b_off = sb("b_off", [2 * NOFF, 2])
        eps_bn = sb("eps_bn", [P, 1])

        loaded = sem("loaded")
        prepared = sem("prepared")
        bn_sqrt = sem("bn_sqrt")
        bn_steps = sem("bn_steps")
        bn_ready = sem("bn_ready")

        convs = []
        off = sb("off", [P, PAIRS, PIX])
        for k in range(2):
            cv = Conv()
            cv.k = k
            cv.src = sb(f"src{k}", [P, PAIRS, HP * WP])
            cv.off = off
            cv.w_off = sb(f"w_off{k}", [P, TAPS, 2 * NOFF])
            cv.w_dc = sb(f"w_dc{k}", [P, TAPS, C])
            cv.off_in_psum = sem(f"c{k}_off_in_psum")
            cv.off_ready = sem(f"c{k}_off_ready")
            cv.max_ready = sem(f"c{k}_max_ready")
            cv.max_turned = sem(f"c{k}_max_turned")
            cv.max_steps = sem(f"c{k}_max_steps")
            cv.flag_ready = sem(f"c{k}_flag_ready")
            cv.pair_free = sem(f"c{k}_pair_free")
            cv.near = Sampler(sem, f"c{k}n", near_steps())
            cv.all = Sampler(sem, f"c{k}a", all_steps())
            convs.append(cv)

        def finish0(i):
            dst = convs[1].src[:, bass.ds(i, 1), :].rearrange("p a (r c) -> p (a r) c", c=WP)
            return nc.scalar.activation(dst[:, PADR:PADR + H, PADC:PADC + W],
                                        m.out.rearrange("p (r c) -> p r c", c=W), ACT.Relu,
                                        bias=bn_shift[:, 0:1], scale=bn_inv[:, 0:1])

        def finish1(i):
            return nc.scalar.activation(m.tokens[:, bass.ds(i, 1), :].rearrange("p a n -> p (a n)"), m.out,
                                        ACT.Identity, bias=bn_shift[:, 1:2], scale=bn_inv[:, 1:2])

        convs[0].finish, convs[1].finish = finish0, finish1

        at = Attention()
        hx_all = m.hx[:, :, :, :].rearrange("p a b n -> p (a b n)")
        hat_all = m.hat[:, :, :].rearrange("p a n -> p (a n)")
        s_all = m.s[:, :, :].rearrange("p a n -> p (a n)")
        y_all = m.y[:, :, :, :].rearrange("p a b n -> p (a b n)")
        src0 = convs[0].src[:, :, :].rearrange("p a n -> p (a n)")
        src1 = convs[1].src[:, :, :].rearrange("p a n -> p (a n)")
        at.xh = src1[:, 0:WINDOW + PIX]
        at.square = src1[:, 1056:1056 + PIX]
        at.std = src1[:, 2080:2080 + PIX]
        at.g = hx_all[:, 0:2048].rearrange("p (s g j n) -> p s g j n", s=2, g=HG, j=TILES)
        at.windows = src1[:, 3104:4128].rearrange("p (s j n) -> p s j n", s=2, j=TILES)
        at.p = hx_all[:, 2048:3584].rearrange("p (s n) -> p s n", s=P_SLOTS)
        at.pn = hx_all[:, 3584:5120].rearrange("p (s n) -> p s n", s=P_SLOTS)
        at.pt = hx_all[:, 5120:6144].rearrange("p (s n) -> p s n", s=2)
        at.xw = hat_all[:, 0:2048].rearrange("p (s a j n) -> p s a j n", s=2, a=2, j=TILES)
        at.z = hat_all[:, 2048:3072].rearrange("p (s n) -> p s n", s=2)
        at.a_heads = s_all[:, 0:1024].rearrange("p (h n) -> p h n", h=HEADS)
        at.b_heads = sb("b_heads", [P, H4, C])
        at.stats = sb("stats", [P, P_SLOTS, 3, TILES * HG])
        at.mark = sb("mark", [P, 1])
        at.pair_done = sem("at_pair_done")
        at.mean_in_psum = sem("at_mean_in_psum")
        at.squared = sem("at_squared")
        at.var_in_psum = sem("at_var_in_psum")
        at.xh_ready = sem("at_xh_ready")
        at.g_in_psum = sem("at_g_in_psum")
        at.g_ready = sem("at_g_ready")
        at.xw_in_psum = sem("at_xw_in_psum")
        at.xw_ready = sem("at_xw_ready")
        at.scores_in_psum = sem("at_scores_in_psum")
        at.shifted = sem("at_shifted")
        at.probs_ready = sem("at_probs_ready")
        at.pt_in_psum = sem("at_pt_in_psum")
        at.pt_ready = sem("at_pt_ready")
        at.z_in_psum = sem("at_z_in_psum")
        at.z_ready = sem("at_z_ready")
        at.projected = sem("at_projected")
        at.added = sem("at_added")
        at.centred = sem("at_centred")
        at.std_ready = sem("at_std_ready")
        at.rstd_ready = sem("at_rstd_ready")
        at.windows_ready = sem("at_windows_ready")
        at.exp_ready = sem("at_exp_ready")
        at.max_ready = sem("at_max_ready")
        at.sum_ready = sem("at_sum_ready")
        at.rsum_ready = sem("at_rsum_ready")
        w_attn = y_all[0:C, 0:4 * HEADS * C].rearrange("p (k n) -> p k n", k=4)
        m.mean_of = sb("mean_of", [P, P])
        m.identity16 = sb("identity16", [P, P], F16)
        m.mask = sb("mask", [P, BANK], F16)
        m.eps_ln = sb("eps_ln", [P, 1])
        m.bu = sb("bu", [P, 1])
        m.w_gate = sb("w_gate", [P, 2 * EXPERTS])
        m.b_gate = sb("b_gate", [P, 1])
        m.ones = sb("ones", [1, NIMG])

        ex = Experts()
        ex.w1 = y_all[:, 0:8192].rearrange("p (e n) -> p e n", e=EXPERTS)
        ex.w2 = off[:, :, :].rearrange("p a n -> p (a n)").rearrange("p (k e c) -> p k e c", k=MH, e=EXPERTS)
        ex.w2_bias = s_all[:, 1024:3072].rearrange("p (e c) -> p e c", e=EXPERTS)
        ex.xh = src0[:, 0:4096].rearrange("p (r n) -> p r n", r=PAIRS)
        ex.square = hat_all[:, 0:1024]
        ex.std = hat_all[:, 1024:2048]
        ex.xt = src1[:, 0:4096].rearrange("p (c r n) -> p c r n", c=CHUNKS, r=PAIRS)
        ex.pick = hx_all[:, 0:2048].rearrange("p (g n) -> p g n", g=GROUPS)
        ex.rest = hx_all[:, 2048:4096].rearrange("p (g n) -> p g n", g=GROUPS)
        ex.pt = hx_all[:, 4096:6144].rearrange("p (c n) -> p c n", c=CHUNKS)
        ex.pooled = hat_all[:, 2048:2304].rearrange("p (e b) -> p e b", e=EXPERTS)
        ex.hidden = hat_all[:, 2304:2816].rearrange("p (k e b) -> p k e b", k=MH, e=EXPERTS)
        ex.answer = hat_all[:, 2816:3072]
        ex.answers = sb("answers", [P, GROUPS, C])
        ex.top = sb("top", [P, GROUPS, 2, TOPK])
        ex.neg_max = sb("neg_max", [P, GROUPS])
        ex.gate_sum = sb("gate_sum", [P, GROUPS])
        ex.gate_rsum = sb("gate_rsum", [P, GROUPS])
        ex.mean_in_psum = sem("ex_mean_in_psum")
        ex.squared = sem("ex_squared")
        ex.var_in_psum = sem("ex_var_in_psum")
        ex.xh_ready = sem("ex_xh_ready")
        ex.logits_in_psum = sem("ex_logits_in_psum")
        ex.xt_in_psum = sem("ex_xt_in_psum")
        ex.xt_ready = sem("ex_xt_ready")
        ex.picked = sem("ex_picked")
        ex.pt_in_psum = sem("ex_pt_in_psum")
        ex.pt_ready = sem("ex_pt_ready")
        ex.pooled_in_psum = sem("ex_pooled_in_psum")
        ex.pooled_ready = sem("ex_pooled_ready")
        ex.w_loaded = sem("ex_w_loaded")
        ex.hidden_in_psum = sem("ex_hidden_in_psum")
        ex.hidden_ready = sem("ex_hidden_ready")
        ex.answer_in_psum = sem("ex_answer_in_psum")
        ex.answer_ready = sem("ex_answer_ready")
        ex.answer_turned = sem("ex_answer_turned")
        ex.answer_sb = sem("ex_answer_sb")
        ex.joined = sem("ex_joined")
        ex.spread = sem("ex_spread")
        ex.centred = sem("ex_centred")
        ex.std_ready = sem("ex_std_ready")
        ex.logits_ready = sem("ex_logits_ready")
        ex.gate_max = sem("ex_gate_max")
        ex.gate_exp = sem("ex_gate_exp")
        ex.rstd_ready = sem("ex_rstd_ready")
        ex.top_steps = sem("ex_top_steps")
        ex.pick_steps = sem("ex_pick_steps")
        ex.rsum_ready = sem("ex_rsum_ready")
        ex.ones_set = sem("ex_ones_set")

        heads_loaded = sem("heads_loaded")
        heads_in_psum, heads_ready, cleared = sem("heads_in_psum"), sem("heads_ready"), sem("cleared")
        out_done = sem("out_done")
        residual = sem("residual")

        block = ctx.enter_context(nc.Block())
        loads = [(m.sel_coord[:, :, :], a["sel_coord"]), (m.coord_bias[:, :], a["coord_bias"]),
                 (convs[0].src[:, :, :], a["x"]), (convs[0].w_off[:, :, :], a["w_off1"]),
                 (m.sel_x[:, :], a["sel_x"]), (m.sel_y[:, :, :], a["sel_y"]),
                 (convs[0].w_dc[:, :, :], a["w_dc1"]), (off[PX_ROW:PX_ROW + 1, :, :], a["px"]),
                 (off[PY_ROW:PY_ROW + 1, :, :], a["py"]), (b_off[:, :], a["b_off"]), (bn[:, :, :], a["bn"]),
                 (m.identity[:, :], a["identity"]),
                 (convs[1].w_off[:, :, :], a["w_off2"]), (convs[1].w_dc[:, :, :], a["w_dc2"]),
                 (m.mean_of[:, :], a["mean_of"]),
                 (m.identity16[:, :], a["identity16"]), (m.mask[:, :], a["mask"]), (m.bu[:, :], a["bu"]),
                 (m.w_gate[:, :], a["w_gate"]), (m.b_gate[:, :], a["b_gate"])]
        NLOAD = 16 * len(loads)

        @block.sync
        def _(sp):
            for dst, src in loads[:7] + loads[9:]:
                sp.dma_start(dst, src).then_inc(loaded, 16)
            sp.wait_ge(prepared, 1)
            for dst, src in loads[7:9]:
                sp.dma_start(dst, src).then_inc(loaded, 16)
            for cv in convs:
                sp.wait_ge(cv.flag_ready, 1)
                flag = nc.sync.value_load(far_flag[0:1, cv.k:cv.k + 1], min_val=0, max_val=1)
                with sp.If(flag == 0):
                    for i in range(PAIRS):
                        sampler_sp(nc, sp, m, cv, cv.near, i)
                with sp.Else():
                    for i in range(PAIRS):
                        sampler_sp(nc, sp, m, cv, cv.all, i)
            sp.wait_ge(convs[1].pair_free, 1 + PAIRS)
            sp.dma_start(w_attn, a["w_attn"]).then_inc(heads_loaded, 16)
            sp.wait_ge(heads_in_psum, 2)
            sp.dma_start(ex.w1[0:C + 1, :, :], a["w1"]).then_inc(ex.w_loaded, 16)
            sp.dma_start(ex.w2[:, :, :, :], a["w2"]).then_inc(ex.w_loaded, 16)
            sp.dma_start(ex.w2_bias[0:1, :, :], a["w2_bias"]).then_inc(ex.w_loaded, 16)
            for i in range(PAIRS):
                sp.wait_ge(ex.joined, i + 1)
                sp.dma_start(out[i], m.tokens[:, i, :]).then_inc(out_done, 16)
            sp.wait_ge(out_done, 16 * PAIRS)

        @block.gpsimd
        def _(pool):
            nc.gpsimd.memset(off[:, :, :], 0.0).then_inc(prepared, 1)
            nc.gpsimd.memset(m.zeros[:, :], 0.0).then_inc(prepared, 1)
            nc.gpsimd.memset(convs[1].src[:, :, :], 0.0).then_inc(prepared, 1)
            nc.gpsimd.memset(eps_bn[:, :], EPS_BN).then_inc(prepared, 1)
            nc.gpsimd.memset(m.hat_scale[:, :], HAT_SCALE).then_inc(prepared, 1)
            nc.gpsimd.memset(m.eps_ln[:, :], EPS_LN).then_inc(prepared, 1)
            nc.gpsimd.memset(m.ones[:, :], 1.0).then_inc(prepared, 1)
            pool.wait_ge(loaded, NLOAD)
            for cv in convs:
                pool.wait_ge(cv.flag_ready, 1)
                flag = nc.gpsimd.value_load(far_flag[0:1, cv.k:cv.k + 1], min_val=0, max_val=1)
                with pool.If(flag == 0):
                    for i in range(PAIRS):
                        sampler_pool(nc, pool, m, cv, cv.near, i)
                with pool.Else():
                    for i in range(PAIRS):
                        sampler_pool(nc, pool, m, cv, cv.all, i)
            pool.wait_ge(convs[1].pair_free, 1 + PAIRS)
            nc.gpsimd.memset(at.a_heads, 0.0).then_inc(cleared, 1)
            nc.gpsimd.memset(hat_all[:, 0:2048], 0.0).then_inc(cleared, 1)
            nc.gpsimd.memset(at.xh[:, 0:WINDOW], 0.0).then_inc(cleared, 1)
            for i in range(PAIRS):
                attention_pool(nc, pool, m, at, i)
            pool.wait_ge(at.pair_done, 1 + PAIRS)
            nc.gpsimd.memset(ex.pooled[C:C + 1, :, :], 1.0).then_inc(ex.ones_set, 1)

        @block.scalar
        def _(act):
            act.wait_ge(loaded, NLOAD)
            act.wait_ge(prepared, 7)
            for k in range(2):
                nc.scalar.activation(bn_tmp[:, k:k + 1], bn[:, k, 3:4], ACT.Sqrt, bias=eps_bn[:, 0:1]).then_inc(bn_sqrt, 1)
            act.wait_ge(bn_ready, 2)
            for cv in convs:
                for i in range(PAIRS):
                    for half in range(2):
                        act.wait_ge(cv.off_in_psum, 2 * i + half + 1)
                        nc.scalar.activation(off[0:2 * NOFF, i, half * BANK:(half + 1) * BANK],
                                             m.ps[0:2 * NOFF, half, :], ACT.Identity,
                                             bias=b_off[:, cv.k:cv.k + 1]).then_inc(cv.off_ready, 1)
                act.wait_ge(cv.flag_ready, 1)
                flag = nc.scalar.value_load(far_flag[0:1, cv.k:cv.k + 1], min_val=0, max_val=1)
                with act.If(flag == 0):
                    with act.Fori(0, PAIRS) as i:
                        sampler_act(nc, act, m, cv, cv.near, i)
                with act.Else():
                    with act.Fori(0, PAIRS) as i:
                        sampler_act(nc, act, m, cv, cv.all, i)
            act.wait_ge(cleared, 3)
            act.wait_ge(heads_in_psum, 2)
            for image in range(2):
                rows = slice(C * image, C * image + C)
                nc.scalar.activation(at.a_heads[rows, :, rows], m.ps[rows, 0, :].rearrange("p (h n) -> p h n", h=HEADS),
                                     ACT.Copy, scale=1.0 / 8.0).then_inc(heads_ready, 1)
            nc.scalar.copy(at.b_heads[:, :, :], m.ps[:, 1, 0:H4 * C].rearrange("p (h n) -> p h n", h=H4)
                           ).then_inc(heads_ready, 1)
            with act.Fori(0, PAIRS) as i:
                attention_act(nc, act, m, at, i)
            experts_act(nc, act, m, ex)

        @block.vector
        def _(dve):
            dve.wait_ge(loaded, NLOAD)
            dve.wait_ge(bn_sqrt, 2)
            nc.vector.reciprocal(bn_tmp[:, 2:4], bn_tmp[:, 0:2]).then_inc(bn_steps, 1)
            dve.wait_ge(bn_steps, 1)
            nc.vector.tensor_tensor(bn_inv[:, :], bn[:, :, 0], bn_tmp[:, 2:4], ALU.mult).then_inc(bn_steps, 1)
            dve.wait_ge(bn_steps, 2)
            nc.vector.tensor_tensor(bn_tmp[:, 0:2], bn[:, :, 2], bn_inv[:, :], ALU.mult).then_inc(bn_steps, 1)
            dve.wait_ge(bn_steps, 3)
            nc.vector.tensor_tensor(bn_shift[:, :], bn[:, :, 1], bn_tmp[:, 0:2], ALU.subtract).then_inc(bn_ready, 2)
            for cv in convs:
                dve.wait_ge(cv.off_ready, 2 * PAIRS)
                nc.vector.tensor_reduce(abs_max[0:2 * NOFF, cv.k:cv.k + 1], off[0:2 * NOFF, :, :], AX.XY, ALU.max,
                                        apply_absolute_value=True).then_inc(cv.max_ready, 1)
                dve.wait_ge(cv.max_turned, 1)
                nc.vector.tensor_reduce(far[0:1, cv.k:cv.k + 1], m.ps[0:1, 0, 0:2 * NOFF], AX.X, ALU.max
                                        ).then_inc(cv.max_steps, 1)
                dve.wait_ge(cv.max_steps, 1)
                nc.vector.tensor_scalar(far_flag[0:1, cv.k:cv.k + 1], far[0:1, cv.k:cv.k + 1], REACH, None,
                                        ALU.is_ge).then_inc(cv.flag_ready, 1)
                nc.vector.tensor_copy(far[0:1, 2 + cv.k:3 + cv.k], far[0:1, cv.k:cv.k + 1]).then_inc(cv.pair_free, 1)
                dve.wait_ge(cv.flag_ready, 1)
                flag = nc.vector.value_load(far_flag[0:1, cv.k:cv.k + 1], min_val=0, max_val=1)
                with dve.If(flag == 0):
                    with dve.Fori(0, PAIRS) as i:
                        sampler_dve(nc, dve, m, cv, cv.near, i)
                with dve.Else():
                    with dve.Fori(0, PAIRS) as i:
                        sampler_dve(nc, dve, m, cv, cv.all, i)
            dve.wait_ge(convs[1].pair_free, 1 + PAIRS)
            src = convs[0].src[:, :, :].rearrange("p a (r c) -> p a r c", c=WP)
            for i in range(PAIRS):
                last = nc.vector.tensor_tensor(m.tokens[:, i, :].rearrange("p (r c) -> p r c", c=W),
                                               m.tokens[:, i, :].rearrange("p (r c) -> p r c", c=W),
                                               src[:, i, PADR:PADR + H, PADC:PADC + W], ALU.add)
            last.then_inc(residual, 1)
            dve.wait_ge(residual, 1)
            nc.vector.tensor_scalar(m.tokens[:, :, :], m.tokens[:, :, :], 0.0, None, ALU.max).then_inc(residual, 1)
            dve.wait_ge(cleared, 3)
            nc.vector.tensor_copy(at.mark[:, 0:1], m.bu[:, 0:1]).then_inc(at.pair_done, 1)
            with dve.Fori(0, PAIRS) as i:
                attention_dve(nc, dve, m, at, i)
            experts_dve(nc, dve, m, ex)

        @block.tensor
        def _(pe):
            pe.wait_ge(loaded, NLOAD)
            pe.wait_ge(prepared, 7)
            for cv in convs:
                if cv.k:
                    pe.wait_ge(convs[0].pair_free, 1 + PAIRS)
                for i in range(PAIRS):
                    src = cv.src[:, i, :].rearrange("p (r c) -> p r c", c=WP)
                    for half in range(2):
                        if i:
                            pe.wait_ge(cv.off_ready, 2 * i + half - 1)
                        for t in range(TAPS):
                            r0 = PADR - 1 + t // 3 + half * (H // 2)
                            last = nc.tensor.matmul(m.ps[0:2 * NOFF, half, :], cv.w_off[:, t, :],
                                                    src[:, r0:r0 + H // 2, t % 3:t % 3 + W],
                                                    start=(t == 0), stop=(t == TAPS - 1))
                        last.then_inc(cv.off_in_psum, 1)
                pe.wait_ge(cv.max_ready, 1)
                nc.tensor.transpose(m.ps[0:1, 0, 0:2 * NOFF], abs_max[0:2 * NOFF, cv.k:cv.k + 1],
                                    m.identity[0:2 * NOFF, 0:2 * NOFF]).then_inc(cv.max_turned, 1)
                pe.wait_ge(cv.flag_ready, 1)
                flag = nc.tensor.value_load(far_flag[0:1, cv.k:cv.k + 1], min_val=0, max_val=1)
                with pe.If(flag == 0):
                    with pe.Fori(0, PAIRS) as i:
                        sampler_pe(nc, pe, m, cv, cv.near, i)
                with pe.Else():
                    with pe.Fori(0, PAIRS) as i:
                        sampler_pe(nc, pe, m, cv, cv.all, i)
            pe.wait_ge(heads_loaded, 16)
            for h in range(HEADS):
                for image in range(2):
                    last = nc.tensor.matmul(m.ps[C * image:C * image + C, 0, h * C:(h + 1) * C],
                                            w_attn[:, 0, h * C:(h + 1) * C],
                                            w_attn[:, 1, h * C:(h + 1) * C], start=True, stop=True)
            last.then_inc(heads_in_psum, 1)
            for h in range(HEADS):
                hg, h4 = divmod(h, H4)
                last = nc.tensor.matmul(m.ps[C * hg:C * hg + C, 1, h4 * C:(h4 + 1) * C],
                                        w_attn[:, 2, h * C:(h + 1) * C], w_attn[:, 3, h * C:(h + 1) * C],
                                        start=True, stop=True)
            last.then_inc(heads_in_psum, 1)
            pe.wait_ge(heads_ready, 3)
            pe.wait_ge(residual, 2)
            with pe.Fori(0, PAIRS) as i:
                attention_pe(nc, pe, m, at, i)
            pe.wait_ge(at.pair_done, 1 + PAIRS)
            experts_pe(nc, pe, m, ex)


def constants():
    f32, f16 = np.float32, np.float16
    c = {}
    sel = np.zeros((P, TAPS, P), f32)
    bias = np.zeros((P, TAPS), f32)
    q = np.arange(W)
    for t in range(TAPS):
        ky, kx = divmod(t, 3)
        for image in range(2):
            for axis in range(2):
                g = slice(64 * image + 32 * axis, 64 * image + 32 * axis + 32)
                sel[NOFF * image + 2 * t + (1 - axis), t, g] = 1
                sel[[PX_ROW, PY_ROW][axis], t, g] = 1
                bias[g, t] = 2 * [kx, ky][axis] - 2 - q
    c["sel_coord"], c["coord_bias"] = sel, bias
    r = np.arange(P)
    part = (r % 64) // 32
    c["sel_x"] = (((part == 0)[:, None]) & ((r % 32)[:, None] == (r % 32)[None, :])).astype(f16) * f16(1 / HAT_SCALE)
    starts = np.array(ALIGNED + SHIFTED)
    c["sel_y"] = ((part == 1)[:, None, None] &
                  ((r % 32)[:, None, None] == (starts[:, None] + (r // 32)[None, :])[None])).astype(f16) * f16(1 / HAT_SCALE)
    c["px"] = np.ascontiguousarray(np.broadcast_to(np.tile(np.arange(W), H), (1, PAIRS, PIX)).astype(f32))
    c["py"] = np.ascontiguousarray(np.broadcast_to(np.repeat(np.arange(H), W), (1, PAIRS, PIX)).astype(f32))
    c["identity"] = np.eye(P, dtype=f32)
    c["mean_of"] = np.kron(np.eye(2), np.full((C, C), 1.0 / C)).astype(f32)
    c["identity16"] = (np.eye(P) * MASK_SCALE).astype(f16)
    qq, kk = (np.arange(P) % TQ)[:, None], np.arange(KEYS)[None, :]
    c["mask"] = np.tile(np.where((kk > qq) & (kk <= qq + WINDOW), 0.0, MASKED), (1, TILES * HG)).astype(f16)
    return c


def layout(v):
    d = {}
    x = np.pad(v["x"], ((0, 0), (0, 0), (PADR, PADR), (PADC, PADC)))
    d["x"] = x.reshape(PAIRS, P, HP * WP).transpose(1, 0, 2)
    for k in (1, 2):
        w = v[f"L0_conv_w_off{k}"].transpose(1, 2, 3, 0).reshape(C, TAPS, NOFF)
        blocks = np.zeros((2, C, TAPS, 2, NOFF), w.dtype)
        blocks[0, :, :, 0] = w
        blocks[1, :, :, 1] = w
        d[f"w_off{k}"] = blocks.reshape(P, TAPS, 2 * NOFF)
        w = v[f"L0_conv_w_dc{k}"].transpose(1, 2, 3, 0).reshape(C, TAPS, C)
        d[f"w_dc{k}"] = np.concatenate([w, w])
    d["b_off"] = np.stack([np.tile(v[f"L0_conv_b_off{k}"], 2) for k in (1, 2)], 1)
    d["bn"] = np.stack([np.stack([np.tile(v[f"L0_conv_{n}{k}"], 2) for n in ("g", "beta", "m", "v")], 1)
                        for k in (1, 2)], 1)
    per_head = [v[f"L1_attn_W{n}"].reshape(HEADS, C, C).transpose(1, 0, 2) for n in "qkv"]
    per_head.append(v["L1_attn_Wu"].T.reshape(HEADS, C, C).transpose(1, 0, 2))
    d["w_attn"] = np.stack(per_head, 1).reshape(C, 4, HEADS * C)
    d["bu"] = np.tile(v["L1_attn_bu"], 2)[:, None]
    gate = v["L1_ffn_gate_w"].T
    blocks = np.zeros((2, C, 2, EXPERTS), gate.dtype)
    blocks[0, :, 0] = gate
    blocks[1, :, 1] = gate
    d["w_gate"] = blocks.reshape(P, 2 * EXPERTS)
    d["b_gate"] = np.tile(v["L1_ffn_gate_b"], PER_GROUP)[:, None]
    d["w1"] = v["L1_ffn_weight1"].transpose(1, 0, 2)
    w2 = v["L1_ffn_weight2"]
    d["w2"] = w2[:, :HID].reshape(EXPERTS, MH, P, C).transpose(2, 1, 0, 3)
    d["w2_bias"] = w2[:, HID][None]
    return d


def kernel(**inputs):
    import numpy as _np
    import concourse.bacc as _bacc
    from concourse import mybir as _mybir
    from concourse.bass_utils import run_bass_kernel_spmd as _run

    nc = _bacc.Bacc("TRN2", target_bir_lowering=False, num_devices=1)
    given = {n: _np.asarray(x) for n, x in inputs.items()}
    arrays, aps = {}, {}
    for name, x in {**layout(given), **constants()}.items():
        x = _np.ascontiguousarray(x)
        arrays[f"in_{name}_dram"] = x
        aps[name] = nc.dram_tensor(f"in_{name}_dram", x.shape, _mybir.dt.from_np(x.dtype), kind="ExternalInput").ap()
    out = nc.dram_tensor("out_dram", (PAIRS, P, PIX), F32, kind="ExternalOutput").ap()
    program(nc, aps, out)
    r = _run(nc, [arrays], core_ids=[0])
    return r.results[0]["out_dram"].reshape(NIMG, C, H, W)
```

```python
import concourse.bass as bass
from concourse import mybir
from contextlib import ExitStack
import numpy as np

F32 = mybir.dt.float32
F16 = mybir.dt.float16
BF16 = mybir.dt.bfloat16
I32 = mybir.dt.int32
ALU = mybir.AluOpType
ACT = mybir.ActivationFunctionType
AX = mybir.AxisListType

NIMG, C, H, W = 8, 64, 32, 32
PAIRS = NIMG // 2
P = 128
PIX = H * W
TAPS = 9
NOFF = 2 * TAPS
PADR, PADC = 2, 1
HP, WP = H + 2 * PADR, W + 2 * PADC
BANK = 512
EPS_BN = 1e-5

CHUNK_ROWS = P // W
TILE = P
SPAN = 2 * TILE
REACH = 2.0
HAT_SCALE = 4096.0
ALIGNED = [CHUNK_ROWS * c for c in range(H // CHUNK_ROWS)]
SHIFTED = [CHUNK_ROWS * c - 2 for c in range(H // CHUNK_ROWS + 1)]
CHUNK_START = [ALIGNED, SHIFTED, ALIGNED]
CHUNK_BASE = [0, len(ALIGNED), len(ALIGNED) + len(SHIFTED)]
NCHUNK = 2 * len(ALIGNED) + len(SHIFTED)
SEL_BASE = [0, len(ALIGNED), 0]
NSEL = len(ALIGNED) + len(SHIFTED)
PX_ROW, PY_ROW, NCOORD = 3 * NOFF * 2, 3 * NOFF * 2 + 1, 3 * NOFF * 2 + 2

HY_BANKS, S_SLOTS, TAP_SLOTS = 2, 6, 3


def near_steps():
    out = []
    for t in range(TAPS):
        ky = t // 3
        back = [0, 1, 1][ky]
        ranges = [(c, min(max(TILE * (c - back), 0), PIX - SPAN)) for c in range(len(CHUNK_START[ky]))]
        for k in range(0, len(ranges), 2):
            for image in range(2):
                out.append((t, image, ranges[k:k + 2]))
    return out


def all_steps():
    out = []
    for t in range(TAPS):
        for c in range(len(CHUNK_START[t // 3])):
            for p0 in range(0, PIX, 2 * SPAN):
                for image in range(2):
                    out.append((t, image, [(c, p0), (c, p0 + SPAN)]))
    return out


CONV1_LOADS = 16 * 4


class Signals:

    def __init__(self, sem, name):
        self.coord_in_psum = sem(name + "_coord_in_psum")
        self.coord_read = sem(name + "_coord_read")
        self.hat_ready = sem(name + "_hat_ready")
        self.hi_ready = sem(name + "_hi_ready")
        self.lo_ready = sem(name + "_lo_ready")
        self.stacked = [sem(f"{name}_stacked{s}") for s in range(TAP_SLOTS)]
        self.hx_in_psum = sem(name + "_hx_in_psum")
        self.hx_ready = sem(name + "_hx_ready")
        self.hy_in_psum = sem(name + "_hy_in_psum")
        self.s_ready = sem(name + "_s_ready")
        self.sampled = sem(name + "_sampled")
        self.y_in_psum = sem(name + "_y_in_psum")
        self.y_ready = sem(name + "_y_ready")
        self.source_ready = sem(name + "_source_ready")


class Sampler(Signals):

    def __init__(self, sem, name, steps):
        Signals.__init__(self, sem, name)
        self.steps = steps
        self.last_of_tap = [max(n for n, s in enumerate(steps) if s[0] == t) + 1 for t in range(TAPS)]
        self.first_of_tap = [min(n for n, s in enumerate(steps) if s[0] == t) for t in range(TAPS)]


class Conv:
    pass


def hx_piece(t, k):
    tap, piece = (t + 1, k + 1) if k < 3 else (t + 2, 0)
    return tap, piece // 2, piece % 2


def sampler_steps(v):
    todo = {0: [(c, 1) for c in range(len(CHUNK_START[1]))], 3: [(c, 2) for c in range(len(CHUNK_START[2]))],
            7: [(c, 0) for c in range(len(CHUNK_START[0]))]}
    out, pending = [], []
    for n in range(0, len(v.steps), 2):
        t = v.steps[n][0]
        k = (n - v.first_of_tap[t]) // 2
        if k == 0:
            pending += todo.get(t, [])
        out.append((n, t, hx_piece(t, k) if k < 4 else None,
                    (t + AHEAD, k) if k < 2 else None, pending.pop(0) if pending else None))
    assert not pending
    return out


AHEAD = 3
NY = NCHUNK
FIRST_HX, NHX = 5, 4 * TAPS
FIRST_COORD, NCOORDS = 2 * AHEAD, 2 * TAPS
FIRST_Y = len(ALIGNED)
PER_SLOT = 64 * TAPS // TAP_SLOTS
RUNS = PAIRS * TAPS + AHEAD
FIRST_WORK = {(1, c): ("source", c) for c in range(FIRST_Y)}
FIRST_WORK.update({(2, t): ("distance", t) for t in range(4)})
FIRST_WORK.update({(2, 5 + piece): ("columns", piece) for piece in range(4)})
FIRST_WORK.update({(3, 0): ("distance", 4), (3, 1): ("distance", 5), (3, 5): ("columns", 4)})


def sampler_pe(nc, pe, m, cv, v, start=None):
    steps = v.steps
    nsteps = len(steps)

    def coord(i, t, half, seen):
        if seen:
            pe.wait_ge(v.coord_read, i * NCOORDS + seen)
        nc.tensor.matmul(m.ps[:, m.COORD, :], m.sel_coord[0:NCOORD, t % TAPS, :],
                         cv.off[0:NCOORD, bass.ds(i + t // TAPS, 1), half * BANK:(half + 1) * BANK],
                         start=True, stop=True).then_inc(v.coord_in_psum, 1)

    def columns(i, t, image, half, seen):
        if image == 0 and half == 0:
            pe.wait_ge(v.stacked[t % TAP_SLOTS], i * PER_SLOT + 64 * (t // TAP_SLOTS + 1))
        if seen:
            pe.wait_ge(v.hx_ready, i * NHX + seen)
        nc.tensor.matmul(m.ps[:, m.HX, :], m.sel_x[:, :],
                         m.stack[:, t % TAP_SLOTS, image, half * BANK:(half + 1) * BANK],
                         start=True, stop=True).then_inc(v.hx_in_psum, 1)

    def weighted(c, g):
        r0 = (CHUNK_START[g][c] + PADR) * W
        for turn in range(2):
            for image in range(2):
                half, rows = slice(C * image, C * image + C), C * (image ^ turn)
                last = nc.tensor.matmul(m.ps[rows:rows + C, m.YB + image, 0:192], m.source[half, r0 + rows:r0 + rows + C],
                                        cv.w_dc[half, 3 * g:3 * g + 3, :], start=True, stop=True)
        last.then_inc(v.y_in_psum, 1)

    def rows(i, n):
        t, image, parts = steps[n % nsteps]
        if n >= HY_BANKS:
            pe.wait_ge(v.s_ready, i * nsteps + n - HY_BANKS + 1)
        for j, (c, p0) in enumerate(parts):
            last = nc.tensor.matmul(m.ps[:, m.HY + n % HY_BANKS, j * SPAN:(j + 1) * SPAN],
                                    m.sel_y[:, SEL_BASE[t // 3] + c, :],
                                    m.stack[:, t % TAP_SLOTS, image, p0:p0 + SPAN], start=True, stop=True)
        last.then_inc(v.hy_in_psum, 1)

    def sample(i, n):
        t = steps[n][0]
        if n == v.first_of_tap[3 * (t // 3)]:
            pe.wait_ge(v.y_ready, i * NY + CHUNK_BASE[t // 3] + len(CHUNK_START[t // 3]))
        pe.wait_ge(v.s_ready, i * nsteps + n + 2)
        for j, (c, p0) in enumerate(steps[n][2]):
            cuts = [p0, BANK, p0 + SPAN] if p0 < BANK < p0 + SPAN else [p0, p0 + SPAN]
            for a, b in zip(cuts[:-1], cuts[1:]):
                for image in range(2):
                    at = j * SPAN + a - p0
                    last = nc.tensor.matmul(
                        m.out[C * image:C * image + C, a:b],
                        m.y[:, CHUNK_BASE[t // 3] + c, image, (t % 3) * C:(t % 3 + 1) * C],
                        m.s[:, (n + image) % S_SLOTS, at:at + b - a], start=False, stop=True, skip_group_check=True)
        last.then_inc(v.sampled, 2)

    if start:
        kind, k = start
        if kind == "source":
            pe.wait_ge(*((v.y_ready, k) if k else (v.source_ready, 1)))
            weighted(k, 0)
        elif kind == "distance":
            if k == 0:
                pe.wait_ge(cv.moved[0], 96)
            coord(0, k // 2, k % 2, k)
        else:
            columns(0, k // 4, k % 4 // 2, k % 2, k)
        return
    rows(0, 0)
    rows(0, 1)
    with pe.Fori(0, PAIRS) as i:
        pe.wait_ge(cv.pair_free, i + 1)
        for half in range(2):
            nc.tensor.matmul(m.out[:, half * BANK:(half + 1) * BANK], m.zeros[:, 0:P], m.zeros[:, :],
                             start=True, stop=True, skip_group_check=True)
        hx_seen, coord_seen, y_seen = FIRST_HX, FIRST_COORD, FIRST_Y
        for n, t, hx, distance, source in sampler_steps(v):
            rows(i, n + 2)
            if source:
                pe.wait_ge(v.y_ready, i * NY + y_seen)
            rows(i, n + 3)
            if source == (0, 0):
                pe.wait_ge(v.source_ready, i + 2)
            if n == nsteps - 2:
                sample(i, n)
            if hx:
                columns(i, *hx, hx_seen)
                hx_seen += 1
            if source:
                weighted(*source)
                y_seen += 1
            if distance:
                coord(i, *distance, coord_seen)
                coord_seen += 1
            if n < nsteps - 2:
                sample(i, n)
    pe.wait_ge(v.y_ready, PAIRS * NY + FIRST_Y)
    pe.wait_ge(v.hx_ready, PAIRS * NHX + FIRST_HX)
    pe.wait_ge(v.coord_read, PAIRS * NCOORDS + FIRST_COORD)


def sampler_act(nc, act, m, cv, v, start=None):
    nsteps = len(v.steps)

    def distance(i, t, half, seen):
        slot, cols = t % TAP_SLOTS, slice(half * BANK, (half + 1) * BANK)
        if half == 0 and t >= TAP_SLOTS:
            act.wait_ge(v.lo_ready, i * TAPS + t - TAP_SLOTS + 1)
            act.wait_ge(v.stacked[slot], i * PER_SLOT + 64 * (t // TAP_SLOTS))
        act.wait_ge(v.coord_in_psum, i * NCOORDS + seen + 1)
        nc.scalar.activation(m.dist[:, seen % 2, :], m.ps[:, m.COORD, :],
                             ACT.Abs, bias=m.coord_bias[:, t % TAPS:t % TAPS + 1]).then_inc(v.coord_read, 1)
        act.wait_ge(v.coord_read, i * NCOORDS + seen + 1)
        nc.scalar.activation(m.hi[:, slot, cols], m.dist[:, seen % 2, :], ACT.Relu,
                             bias=m.hat_scale[:, 0:1], scale=-HAT_SCALE).then_inc(v.hi_ready, 1)
        nc.scalar.activation(m.hat[:, slot, cols], m.dist[:, seen % 2, :], ACT.Relu,
                             bias=m.hat_scale[:, 0:1], scale=-HAT_SCALE).then_inc(v.hat_ready, 1)

    def columns(i, t, image, half, seen):
        if t - TAP_SLOTS >= 0:
            act.wait_ge(v.s_ready, i * nsteps + v.last_of_tap[t - TAP_SLOTS])
        act.wait_ge(v.hx_in_psum, i * NHX + seen + 1)
        nc.scalar.copy(m.hx[:, t % TAP_SLOTS, image, half * BANK:(half + 1) * BANK],
                       m.ps[:, m.HX, :]).then_inc(v.hx_ready, 1)

    def weighted(i, c, g, seen):
        act.wait_ge(v.y_in_psum, i * NY + seen + 1)
        nc.scalar.copy(m.y[:, CHUNK_BASE[g] + c, :, :],
                       m.ps[:, m.YB:m.YB + 2, 0:192]).then_inc(v.y_ready, 1)

    if start:
        kind, k = start
        if kind == "source":
            weighted(0, k, 0, k)
        elif kind == "distance":
            distance(0, k // 2, k % 2, k)
        else:
            columns(0, k // 4, k % 4 // 2, k % 2, k)
        return
    with act.Fori(0, PAIRS) as i:
        hx_seen, coord_seen, y_seen = FIRST_HX, FIRST_COORD, FIRST_Y
        for n, t, hx, far, source in sampler_steps(v):
            if n == nsteps - 2:
                act.wait_ge(v.sampled, S_SLOTS + i * nsteps + nsteps)
                cv.finish(i).then_inc(cv.pair_free, 1)
            if hx:
                columns(i, *hx, hx_seen)
                hx_seen += 1
            if source:
                if source == (0, 0):
                    act.wait_ge(v.sampled, S_SLOTS + i * nsteps + v.last_of_tap[2])
                weighted(i, *source, y_seen)
                y_seen += 1
            if far:
                distance(i, *far, coord_seen)
                coord_seen += 1
    act.wait_ge(v.lo_ready, RUNS)
    for slot in range(TAP_SLOTS):
        act.wait_ge(v.stacked[slot], 64 * (RUNS // TAP_SLOTS))


def sampler_dve(nc, dve, m, cv, v):
    nsteps = len(v.steps)
    with dve.Fori(0, PAIRS) as i:
        for n, (t, image, parts) in enumerate(v.steps):
            dve.wait_ge(v.sampled, i * nsteps + 2 * (n // 2) + 2)
            if n - image == v.first_of_tap[t]:
                dve.wait_ge(v.hx_ready, i * NHX + 4 * t + 2 * image + 2)
            dve.wait_ge(v.hy_in_psum, i * nsteps + n + 1)
            p0 = parts[0][1]
            hx = m.hx[:, t % TAP_SLOTS, image, p0:p0 + SPAN]
            hx = bass.AP(hx.tensor, hx.offset, [hx.ap[0], [parts[-1][1] - p0, len(parts)], [1, SPAN]])
            dst = m.s[:, n % S_SLOTS, 0:SPAN * len(parts)].rearrange("p (k n) -> p k n", n=SPAN)
            hy = m.ps[:, m.HY + n % HY_BANKS, 0:SPAN * len(parts)].rearrange("p (k n) -> p k n", n=SPAN)
            nc.vector.tensor_tensor(dst, hx, hy, ALU.mult).then_inc(v.s_ready, 1)


def sampler_pool(nc, pool, m, cv, v, start=False):
    def source(i):
        nc.gpsimd.tensor_copy(m.source[:, :].rearrange("p (r c) -> p r c", c=W),
                              cv.src[:, i, :].rearrange("p (r c) -> p r c", c=WP)[:, :, PADC:PADC + W]
                              ).then_inc(v.source_ready, 1)

    if start:
        source(0)
    for run in range(0, AHEAD) if start else range(AHEAD, RUNS):
        slot = run % TAP_SLOTS
        if run >= TAP_SLOTS:
            pool.wait_ge(v.stacked[slot], 64 * (run // TAP_SLOTS))
        pool.wait_ge(v.hat_ready, 2 * run + 2)
        nc.gpsimd.tensor_tensor(m.lo[:, slot, :], m.hat[:, slot, :], m.hi[:, slot, :],
                                ALU.subtract).then_inc(v.lo_ready, 1)
        if run >= AHEAD and (run - AHEAD) % TAPS == 5 and not start:
            i = (run - AHEAD) // TAPS
            pool.wait_ge(v.y_in_psum, NY * (i + 1))
            source(min(i + 1, PAIRS - 1))
    if not start:
        for slot in range(TAP_SLOTS):
            pool.wait_ge(v.stacked[slot], 64 * (RUNS // TAP_SLOTS))
        pool.wait_ge(v.y_in_psum, PAIRS * NY + FIRST_Y)


def sampler_sp(nc, sp, m, cv, v, start=None):
    nsteps = len(v.steps)
    for run in range(AHEAD, RUNS) if start is None else [start]:
        slot = run % TAP_SLOTS
        if run >= TAP_SLOTS:
            i, t = divmod(run - TAP_SLOTS, TAPS)
            sp.wait_ge(v.hy_in_psum, i * nsteps + v.last_of_tap[t])
        sp.wait_ge(v.hi_ready, 2 * run + 2)
        for image in range(2):
            sp.dma_start(m.stack[0:C, slot, image, :], m.hi[C * image:C * image + C, slot, :]
                         ).then_inc(v.stacked[slot], 16)
        sp.wait_ge(v.lo_ready, run + 1)
        for image in range(2):
            sp.dma_start(m.stack[C:P, slot, image, :], m.lo[C * image:C * image + C, slot, :]
                         ).then_inc(v.stacked[slot], 16)


def offsets_pe(nc, pe, m, cv):
    for i in range(PAIRS):
        src = cv.src[:, i, :].rearrange("p (r c) -> p r c", c=WP)
        if cv.k == 0:
            pe.wait_ge(m.x_loaded[i], 16)
        else:
            pe.wait_ge(m.convs[0].pair_free, 1 + PAIRS)
        if i >= 2:
            pe.wait_ge(cv.off_read, 2 * i - 2)
        for t in range(TAPS):
            for half in range(2):
                r0 = PADR - 1 + t // 3 + half * (H // 2)
                last = nc.tensor.matmul(m.ps[C * half:C * half + 2 * NOFF, 2 * (i % 2) + half, :], cv.w_off[:, t, :],
                                        src[:, r0:r0 + H // 2, t % 3:t % 3 + W],
                                        start=(t == 0), stop=(t == TAPS - 1))
            if t == TAPS - 1:
                last.then_inc(cv.off_in_psum, 1)
            if (i, t) == (1, 0) and cv.k == 0:
                pe.wait_ge(m.conv1_loaded, CONV1_LOADS)
                pe.wait_ge(m.prepared, 7)
                pe.wait_ge(m.pxpy_placed, 16 * PAIRS)
            if (i, t) in FIRST_WORK:
                sampler_pe(nc, pe, m, cv, cv.near, start=FIRST_WORK[i, t])


def offsets_act(nc, act, m, cv):
    for i in range(PAIRS):
        if i == 1 and cv.k == 0:
            act.wait_ge(m.conv1_loaded, CONV1_LOADS)
        for t in range(TAPS):
            if (i, t) in FIRST_WORK:
                sampler_act(nc, act, m, cv, cv.near, start=FIRST_WORK[i, t])
        act.wait_ge(cv.off_in_psum, i + 1)
        if i >= 2:
            act.wait_ge(cv.split, 4 * (i - 1))
        for half in range(2):
            rows = slice(C * half, C * half + 2 * NOFF)
            nc.scalar.activation(m.off32[rows, i % 2, :], m.ps[rows, 2 * (i % 2) + half, :], ACT.Identity,
                                 bias=m.b_off[rows, cv.k:cv.k + 1]).then_inc(cv.off_read, 1)


def offsets_dve(nc, dve, m, cv):
    R = slice(0, C + 2 * NOFF)
    for i in range(PAIRS):
        o = m.off32[R, i % 2, :]
        dve.wait_ge(cv.off_read, 2 * i + 2)
        nc.vector.tensor_reduce(m.abs_max[R, i:i + 1], o, AX.X, ALU.max, apply_absolute_value=True
                                ).then_inc(cv.max_ready, 1)
        if i >= 2:
            dve.wait_ge(cv.moved[i % 2], 96)
        nc.vector.tensor_copy(m.parts[R, i % 2, 0, :], o).then_inc(cv.split, 1)
        dve.wait_ge(cv.split, 4 * i + 1)
        dve.wait_ge(cv.max_ready, i + 1)
        nc.vector.tensor_tensor(o, o, m.parts[R, i % 2, 0, :], ALU.subtract).then_inc(cv.split, 1)
        dve.wait_ge(cv.split, 4 * i + 2)
        nc.vector.tensor_copy(m.parts[R, i % 2, 1, :], o).then_inc(cv.split, 1)
        dve.wait_ge(cv.split, 4 * i + 3)
        nc.vector.tensor_tensor(m.parts[R, i % 2, 2, :], o, m.parts[R, i % 2, 1, :], ALU.subtract
                                ).then_inc(cv.split, 1)


def offsets_sp(nc, sp, m, cv):
    for i in range(PAIRS):
        for part in range(3):
            sp.wait_ge(cv.split, 4 * i + [1, 3, 4][part])
            for half in range(2):
                sp.dma_start(cv.off[2 * NOFF * part:2 * NOFF * (part + 1), i, half * BANK:(half + 1) * BANK],
                             m.parts[C * half:C * half + 2 * NOFF, i % 2, part, :]).then_inc(cv.moved[i % 2], 16)
        for run in [[], [0, 1], [2], []][i]:
            sampler_sp(nc, sp, m, cv, cv.near, start=run)


HEADS, WINDOW, TQ = 8, 32, 32
HG = 2
H4 = HEADS // HG
KEYS = TQ + WINDOW
TILES = P // TQ
BLOCKS = PIX // P
UNITS = 2 * BLOCKS
EPS_LN = 1e-5
P_SLOTS = 3
MASK_SCALE, MASKED = 32768.0, -65504.0


class Attention:
    pass


class Experts:
    pass


def attention_pe(nc, pe, m, at, i):
    pe.wait_ge(at.pair_done, i + 1)
    for half in range(2):
        nc.tensor.matmul(m.ps[:, half, :], m.mean_of[:, :],
                         m.tokens[:, bass.ds(i, 1), half * BANK:(half + 1) * BANK],
                         start=True, stop=True).then_inc(at.mean_in_psum, 1)
    for half in range(2):
        pe.wait_ge(at.squared, i * 2 + half + 1)
        nc.tensor.matmul(m.ps[:, 2 + half, :], m.mean_of[:, :], at.square[:, half * BANK:(half + 1) * BANK],
                         start=True, stop=True).then_inc(at.var_in_psum, 1)
    pe.wait_ge(at.xh_ready, i + 1)

    def project_queries(b):
        if b >= 1:
            pe.wait_ge(at.g_ready, i * 2 * BLOCKS + 2 * b)
        for hg in range(HG):
            for h in range(H4):
                last = nc.tensor.matmul(m.ps[:, hg, h * P:(h + 1) * P], at.a_heads[:, hg * H4 + h, :],
                                        at.xh[:, WINDOW + b * P:WINDOW + (b + 1) * P], start=True, stop=True)
            last.then_inc(at.g_in_psum, 1)

    def turn_keys(b):
        if b >= 1:
            pe.wait_ge(at.xw_ready, i * 2 * BLOCKS + 2 * b)
        pe.wait_ge(at.windows_ready, i * BLOCKS + b + 1)
        for j in range(TILES):
            last = nc.tensor.transpose(m.ps[:, 5, j * P:(j + 1) * P], at.windows[:, b % 2, j, :], m.identity[:, :])
        last.then_inc(at.xw_in_psum, 1)

    def scores(v):
        b, image = divmod(v, 2)
        if image == 0:
            pe.wait_ge(at.g_ready, i * 2 * BLOCKS + 2 * b + 2)
        if v >= 2:
            pe.wait_ge(at.shifted, i * UNITS + v - 1)
        half = slice(C * image, C * image + C)
        nc.tensor.matmul(m.ps[:, 2 + image, :], m.identity16[:, :], m.mask[:, :], start=True, stop=False,
                         skip_group_check=True)
        for j in range(TILES):
            for hg in range(HG):
                last = nc.tensor.matmul(
                    m.ps[:, 2 + image, (j * HG + hg) * KEYS:(j * HG + hg + 1) * KEYS],
                    at.g[half, b % 2, hg, j, :],
                    at.xh[half, b * P + j * TQ:b * P + j * TQ + KEYS], start=False, stop=True, skip_group_check=True)
        last.then_inc(at.scores_in_psum, 1)

    def turn_probs(v):
        pe.wait_ge(at.probs_ready, i * UNITS + v + 1)
        if v >= 1:
            pe.wait_ge(at.pt_ready, i * UNITS + v)
        for j in range(TILES):
            last = nc.tensor.transpose(m.ps[:, 4, j * P:(j + 1) * P], at.pn[:, v % P_SLOTS, j * P:(j + 1) * P],
                                       m.identity[:, :])
        last.then_inc(at.pt_in_psum, 1)

    def values(v):
        b, image = divmod(v, 2)
        pe.wait_ge(at.pt_ready, i * UNITS + v + 1)
        if image == 0:
            pe.wait_ge(at.xw_ready, i * 2 * BLOCKS + 2 * b + 2)
        if v >= 1:
            pe.wait_ge(at.z_ready, i * UNITS + v)
        for j in range(TILES):
            last = nc.tensor.matmul(m.ps[:, 6, j * P:(j + 1) * P], at.xw[:, b % 2, image, j, :],
                                    at.pt[:, v % 2, j * P:(j + 1) * P], start=True, stop=True)
        last.then_inc(at.z_in_psum, 1)

    def project_values(v):
        b, image = divmod(v, 2)
        pe.wait_ge(at.z_ready, i * UNITS + v + 1)
        if b >= 2 and image == 0:
            pe.wait_ge(at.added, i * BLOCKS + b - 1)
        z = at.z[:, v % 2, :].rearrange("p (j h q) -> p h j q", j=TILES, h=H4)
        for h in range(H4):
            last = nc.tensor.matmul(m.ps[C * image:C * image + C, 7, (b % 2) * P:(b % 2 + 1) * P],
                                    at.b_heads[:, h, :], z[:, h, :, :], start=(h == 0), stop=(h == H4 - 1),
                                    skip_group_check=True)
        last.then_inc(at.projected, 1)

    project_queries(0)
    turn_keys(0)
    for v in range(UNITS + 2):
        if v < UNITS:
            scores(v)
        if v >= 2:
            values(v - 2)
        if v % 2 == 1 and v + 1 < UNITS:
            project_queries((v + 1) // 2)
        if v % 2 == 1 and 1 < v + 1 < UNITS:
            turn_keys((v + 1) // 2)
        if 1 <= v < UNITS + 1:
            turn_probs(v - 1)
        if v >= 2:
            project_values(v - 2)


def attention_act(nc, act, m, at, i):
    for half in range(2):
        act.wait_ge(at.centred, i * 2 + half + 1)
        cols = slice(half * BANK, (half + 1) * BANK)
        nc.scalar.activation(at.square[:, cols], at.xh[:, WINDOW + half * BANK:WINDOW + (half + 1) * BANK],
                             ACT.Square).then_inc(at.squared, 1)
    for half in range(2):
        act.wait_ge(at.var_in_psum, i * 2 + half + 1)
        nc.scalar.activation(at.std[:, half * BANK:(half + 1) * BANK], m.ps[:, 2 + half, :], ACT.Sqrt,
                             bias=m.eps_ln[:, 0:1]).then_inc(at.std_ready, 1)

    def queries(b):
        if b >= 2:
            act.wait_ge(at.scores_in_psum, i * UNITS + 2 * (b - 1))
        for hg in range(HG):
            act.wait_ge(at.g_in_psum, i * 2 * BLOCKS + 2 * b + hg + 1)
            nc.scalar.copy(at.g[:, b % 2, hg, :, :].rearrange("p j (h q) -> p h j q", h=H4),
                           m.ps[:, hg, :].rearrange("p (h j q) -> p h j q", h=H4, j=TILES)).then_inc(at.g_ready, 1)

    queries(0)
    for v in range(UNITS + 2):
        if v >= 2:
            act.wait_ge(at.z_in_psum, i * UNITS + v - 1)
            if v >= 4:
                act.wait_ge(at.projected, i * UNITS + v - 3)
            nc.scalar.copy(at.z[:, v % 2, :], m.ps[:, 6, :]).then_inc(at.z_ready, 1)
        if v < UNITS:
            act.wait_ge(at.shifted, i * UNITS + v + 1)
            nc.scalar.activation(at.p[:, v % P_SLOTS, :], at.p[:, v % P_SLOTS, :], ACT.Exp).then_inc(at.exp_ready, 1)
        if v % 2 == 1 and v + 1 < UNITS:
            queries((v + 1) // 2)
        if 1 <= v < UNITS + 1:
            act.wait_ge(at.pt_in_psum, i * UNITS + v)
            if v >= 3:
                act.wait_ge(at.z_in_psum, i * UNITS + v - 2)
            nc.scalar.copy(at.pt[:, (v - 1) % 2, :], m.ps[:, 4, :]).then_inc(at.pt_ready, 1)


def attention_dve(nc, dve, m, at, i):
    dve.wait_ge(at.pair_done, i + 1)
    for half in range(2):
        dve.wait_ge(at.mean_in_psum, i * 2 + half + 1)
        nc.vector.tensor_tensor(at.xh[:, WINDOW + half * BANK:WINDOW + (half + 1) * BANK],
                                m.tokens[:, bass.ds(i, 1), half * BANK:(half + 1) * BANK].rearrange("p a n -> p (a n)"),
                                m.ps[:, half, :], ALU.subtract).then_inc(at.centred, 1)
    dve.wait_ge(at.std_ready, i * 2 + 2)
    nc.vector.reciprocal(at.std[:, :], at.std[:, :]).then_inc(at.rstd_ready, 1)
    dve.wait_ge(at.rstd_ready, i + 1)
    nc.vector.tensor_tensor(at.xh[:, WINDOW:WINDOW + PIX], at.xh[:, WINDOW:WINDOW + PIX], at.std[:, :],
                            ALU.mult).then_inc(at.xh_ready, 1)

    def keys(b):
        dve.wait_ge(at.xw_in_psum, i * BLOCKS + b + 1)
        if b >= 2:
            dve.wait_ge(at.z_in_psum, i * UNITS + 2 * (b - 1))
        for hg in range(HG):
            rows = slice(KEYS * hg, KEYS * hg + KEYS)
            nc.vector.tensor_copy(at.xw[rows, b % 2, :, :, hg * C:(hg + 1) * C].rearrange("p a j c -> p j a c"),
                                  m.ps[rows, 5, :].rearrange("p (j a c) -> p j a c", j=TILES, a=2)
                                  ).then_inc(at.xw_ready, 1)

    keys(0)
    for v in range(UNITS + 2):
        if v < UNITS:
            image = v % 2
            bank = m.ps[:, 2 + image, :].rearrange("p (g k) -> p g k", k=KEYS)
            st = at.stats[:, v % P_SLOTS, :, :]
            dve.wait_ge(at.scores_in_psum, i * UNITS + v + 1)
            if v >= P_SLOTS:
                dve.wait_ge(at.probs_ready, i * UNITS + v - P_SLOTS + 1)
            nc.vector.tensor_reduce(st[:, 0, :], bank, AX.X, ALU.max).then_inc(at.max_ready, 1)
            dve.wait_ge(at.max_ready, i * UNITS + v + 1)
            nc.vector.tensor_tensor(at.p[:, v % P_SLOTS, :].rearrange("p (g k) -> p g k", k=KEYS), bank,
                                    st[:, 0, :].unsqueeze(2).to_broadcast([P, TILES * HG, KEYS]),
                                    ALU.subtract).then_inc(at.shifted, 1)
        if v % 2 == 1 and v >= 3:
            b = (v - 3) // 2
            dve.wait_ge(at.projected, i * UNITS + 2 * b + 2)
            tok = m.tokens[:, bass.ds(i, 1), b * P:(b + 1) * P].rearrange("p a n -> p (a n)")
            nc.vector.scalar_tensor_tensor(tok, m.ps[:, 7, (b % 2) * P:(b % 2 + 1) * P], m.bu[:, 0:1], tok,
                                           ALU.add, ALU.add).then_inc(at.added, 1)
        if v % 2 == 1 and v + 1 < UNITS:
            keys((v + 1) // 2)
        if v < UNITS:
            dve.wait_ge(at.exp_ready, i * UNITS + v + 1)
            nc.vector.tensor_reduce(st[:, 1, :], at.p[:, v % P_SLOTS, :].rearrange("p (g k) -> p g k", k=KEYS),
                                    AX.X, ALU.add).then_inc(at.sum_ready, 1)
            dve.wait_ge(at.sum_ready, i * UNITS + v + 1)
            nc.vector.reciprocal(st[:, 2, :], st[:, 1, :]).then_inc(at.rsum_ready, 1)
    dve.wait_ge(at.added, i * BLOCKS + BLOCKS)
    nc.vector.tensor_copy(at.mark[:, 0:1], m.bu[:, 0:1]).then_inc(at.pair_done, 1)


def attention_pool(nc, pool, m, at, i):
    def windows(b):
        if b >= 2:
            pool.wait_ge(at.xw_in_psum, i * BLOCKS + b - 1)
        first = at.xh[:, b * P:b * P + KEYS]
        nc.gpsimd.tensor_copy(at.windows[:, b % 2, :, :].rearrange("p j (a k) -> p j a k", a=2),
                              bass.AP(first.tensor, first.offset, [first.ap[0], [TQ, TILES], [0, 2], [1, KEYS]])
                              ).then_inc(at.windows_ready, 1)

    pool.wait_ge(at.xh_ready, i + 1)
    windows(0)
    windows(1)
    for v in range(UNITS):
        if v % 2 == 1 and (v + 3) // 2 < BLOCKS:
            windows((v + 3) // 2)
        pool.wait_ge(at.rsum_ready, i * UNITS + v + 1)
        if v >= P_SLOTS:
            pool.wait_ge(at.pt_in_psum, i * UNITS + v - P_SLOTS + 1)
        nc.gpsimd.tensor_tensor(at.pn[:, v % P_SLOTS, :].rearrange("p (g k) -> p g k", k=KEYS),
                                at.p[:, v % P_SLOTS, :].rearrange("p (g k) -> p g k", k=KEYS),
                                at.stats[:, v % P_SLOTS, 2, :].unsqueeze(2).to_broadcast([P, TILES * HG, KEYS]),
                                ALU.mult).then_inc(at.probs_ready, 1)


EXPERTS, TOPK, HID = 32, 8, 256
GROUPS = NIMG * EXPERTS // P
PER_GROUP = NIMG // GROUPS
CHUNKS = PIX // P
MH = HID // P


def experts_pe(nc, pe, m, ex):
    for pr in range(PAIRS):
        if pr:
            pe.wait_ge(ex.xh_ready, pr)
        for half in range(2):
            nc.tensor.matmul(m.ps[:, half, :], m.mean_of[:, :], m.tokens[:, pr, half * BANK:(half + 1) * BANK],
                             start=True, stop=True).then_inc(ex.mean_in_psum, 1)
        for half in range(2):
            pe.wait_ge(ex.squared, 2 * pr + half + 1)
            nc.tensor.matmul(m.ps[:, 2 + half, :], m.mean_of[:, :], ex.square[:, half * BANK:(half + 1) * BANK],
                             start=True, stop=True).then_inc(ex.var_in_psum, 1)
        pe.wait_ge(ex.xh_ready, pr + 1)
        for half in range(2):
            last = nc.tensor.matmul(m.ps[2 * EXPERTS * (pr % 2):2 * EXPERTS * (pr % 2 + 1), 4 + 2 * (pr // 2) + half, :],
                                    m.w_gate[:, :], ex.xh[:, pr, half * BANK:(half + 1) * BANK], start=True, stop=True)
        last.then_inc(ex.logits_in_psum, 1)
    for c in range(CHUNKS):
        if c >= 4:
            pe.wait_ge(ex.xt_ready, c - 3)
        for pr in range(PAIRS):
            last = nc.tensor.transpose(m.ps[:, c % 4, pr * P:(pr + 1) * P], ex.xh[:, pr, c * P:(c + 1) * P],
                                       m.identity[:, :])
        last.then_inc(ex.xt_in_psum, 1)
    for g in range(GROUPS):
        pe.wait_ge(ex.picked, g + 1)
        for q in range(2):
            for c in range(4):
                last = nc.tensor.transpose(m.ps[:, 4 + 2 * g + q, c * P:(c + 1) * P],
                                           ex.pick[:, g, (4 * q + c) * P:(4 * q + c + 1) * P], m.identity[:, :])
            last.then_inc(ex.pt_in_psum, 1)
    pe.wait_ge(ex.xt_ready, CHUNKS)
    pe.wait_ge(ex.pt_ready, 2 * GROUPS)
    for b in range(NIMG):
        for c in range(CHUNKS):
            last = nc.tensor.matmul(m.ps[0:C, 0, b * EXPERTS:(b + 1) * EXPERTS],
                                    ex.xt[:, c, b // 2, (b % 2) * C:(b % 2 + 1) * C],
                                    ex.pt[:, c, b * EXPERTS:(b + 1) * EXPERTS], start=(c == 0), stop=(c == CHUNKS - 1))
    last.then_inc(ex.pooled_in_psum, 1)
    pe.wait_ge(ex.pooled_ready, 1)
    pe.wait_ge(ex.ones_set, 1)
    pe.wait_ge(ex.w_loaded, 64)
    for e in range(EXPERTS):
        for k in range(MH):
            last = nc.tensor.matmul(m.ps[:, 1, (k * EXPERTS + e) * NIMG:(k * EXPERTS + e + 1) * NIMG],
                                    ex.w1[0:C + 1, e, k * P:(k + 1) * P], ex.pooled[0:C + 1, e, :],
                                    start=True, stop=True)
    last.then_inc(ex.hidden_in_psum, 1)
    pe.wait_ge(ex.hidden_ready, 1)
    for e in range(EXPERTS):
        dst = m.ps[0:C, 2, e * NIMG:(e + 1) * NIMG]
        nc.tensor.matmul(dst, ex.w2_bias[0:1, e, :], m.ones[0:1, 0:NIMG], start=True, stop=False)
        for k in range(MH):
            last = nc.tensor.matmul(dst, ex.w2[k][:, e, :], ex.hidden[:, k, e, :], start=False, stop=(k == MH - 1))
    last.then_inc(ex.answer_in_psum, 1)
    pe.wait_ge(ex.answer_ready, 1)
    for g in range(GROUPS):
        last = nc.tensor.transpose(m.ps[:, 3, g * C:(g + 1) * C], ex.answer[0:C, g * P:(g + 1) * P],
                                   m.identity[0:C, 0:C])
    last.then_inc(ex.answer_turned, 1)
    pe.wait_ge(ex.answer_sb, 1)
    for pr in range(PAIRS):
        if pr >= 2:
            pe.wait_ge(ex.joined, pr - 1)
        for image in range(2):
            b = 2 * pr + image
            rows = slice(EXPERTS * (b % PER_GROUP), EXPERTS * (b % PER_GROUP + 1))
            for half in range(2):
                last = nc.tensor.matmul(m.ps[C * image:C * image + C, 4 + 2 * (pr % 2) + half, :],
                                        ex.answers[rows, b // PER_GROUP, :],
                                        ex.pick[rows, b // PER_GROUP, half * BANK:(half + 1) * BANK],
                                        start=True, stop=True, skip_group_check=True)
        last.then_inc(ex.spread, 1)


def experts_act(nc, act, m, ex):
    for pr in range(PAIRS):
        for half in range(2):
            act.wait_ge(ex.centred, 2 * pr + half + 1)
            cols = slice(half * BANK, (half + 1) * BANK)
            nc.scalar.activation(ex.square[:, cols], ex.xh[:, pr, cols], ACT.Square).then_inc(ex.squared, 1)
        if pr:
            act.wait_ge(ex.xh_ready, pr)
        for half in range(2):
            act.wait_ge(ex.var_in_psum, 2 * pr + half + 1)
            nc.scalar.activation(ex.std[:, half * BANK:(half + 1) * BANK], m.ps[:, 2 + half, :], ACT.Sqrt,
                                 bias=m.eps_ln[:, 0:1]).then_inc(ex.std_ready, 1)
    for g in range(GROUPS):
        act.wait_ge(ex.logits_in_psum, 2 * g + 2)
        for half in range(2):
            nc.scalar.activation(ex.pick[:, g, half * BANK:(half + 1) * BANK], m.ps[:, 4 + 2 * g + half, :],
                                 ACT.Identity, bias=m.b_gate[:, 0:1]).then_inc(ex.logits_ready, 1)
    for g in range(GROUPS):
        act.wait_ge(ex.gate_max, g + 1)
        nc.scalar.activation(ex.pick[:, g, :], ex.pick[:, g, :], ACT.Exp, bias=ex.neg_max[:, g:g + 1],
                             accum_out=ex.gate_sum[:, g:g + 1]).then_inc(ex.gate_exp, 1)
    for c in range(CHUNKS):
        act.wait_ge(ex.xt_in_psum, c + 1)
        nc.scalar.copy(ex.xt[:, c, :, :], m.ps[:, c % 4, :].rearrange("p (r n) -> p r n", r=PAIRS)
                       ).then_inc(ex.xt_ready, 1)
    for g in range(GROUPS):
        for q in range(2):
            act.wait_ge(ex.pt_in_psum, 2 * g + q + 1)
            nc.scalar.copy(ex.pt[:, 4 * q:4 * q + 4, g * P:(g + 1) * P],
                           m.ps[:, 4 + 2 * g + q, :].rearrange("p (c n) -> p c n", c=4)).then_inc(ex.pt_ready, 1)
    act.wait_ge(ex.hidden_in_psum, 1)
    nc.scalar.activation(ex.hidden[:, :, :, :], m.ps[:, 1, :].rearrange("p (k e b) -> p k e b", k=MH, e=EXPERTS),
                         ACT.Gelu).then_inc(ex.hidden_ready, 1)


def experts_dve(nc, dve, m, ex):
    for pr in range(PAIRS):
        for half in range(2):
            cols = slice(half * BANK, (half + 1) * BANK)
            dve.wait_ge(ex.mean_in_psum, 2 * pr + half + 1)
            nc.vector.tensor_tensor(ex.xh[:, pr, cols], m.tokens[:, pr, cols], m.ps[:, half, :],
                                    ALU.subtract).then_inc(ex.centred, 1)
        dve.wait_ge(ex.std_ready, 2 * pr + 2)
        nc.vector.reciprocal(ex.std[:, :], ex.std[:, :]).then_inc(ex.rstd_ready, 1)
        dve.wait_ge(ex.rstd_ready, pr + 1)
        nc.vector.tensor_tensor(ex.xh[:, pr, :], ex.xh[:, pr, :], ex.std[:, :], ALU.mult).then_inc(ex.xh_ready, 1)
    for g in range(GROUPS):
        dve.wait_ge(ex.logits_ready, 2 * g + 2)
        nc.vector.max(ex.top[:, g, 0, :], ex.pick[:, g, :]).then_inc(ex.top_steps, 1)
        dve.wait_ge(ex.top_steps, g + 1)
        nc.vector.tensor_scalar(ex.neg_max[:, g:g + 1], ex.top[:, g, 0, 0:1], -1.0, None, ALU.mult
                                ).then_inc(ex.gate_max, 1)
    for g in range(GROUPS):
        dve.wait_ge(ex.gate_exp, g + 1)
        nc.vector.max(ex.top[:, g, 1, :], ex.pick[:, g, :]).then_inc(ex.pick_steps, 1)
        nc.vector.reciprocal(ex.gate_rsum[:, g:g + 1], ex.gate_sum[:, g:g + 1]).then_inc(ex.rsum_ready, 1)
        dve.wait_ge(ex.pick_steps, 3 * g + 1)
        nc.vector.match_replace(ex.rest[:, g, :], ex.top[:, g, 1, :], ex.pick[:, g, :], 0.0).then_inc(ex.pick_steps, 1)
        dve.wait_ge(ex.pick_steps, 3 * g + 2)
        nc.vector.tensor_tensor(ex.rest[:, g, :], ex.pick[:, g, :], ex.rest[:, g, :], ALU.subtract
                                ).then_inc(ex.pick_steps, 1)
        dve.wait_ge(ex.pick_steps, 3 * g + 3)
        dve.wait_ge(ex.rsum_ready, g + 1)
        nc.vector.tensor_scalar(ex.pick[:, g, :], ex.rest[:, g, :], ex.gate_rsum[:, g:g + 1], None, ALU.mult
                                ).then_inc(ex.picked, 1)
    dve.wait_ge(ex.pooled_in_psum, 1)
    nc.vector.tensor_copy(ex.pooled[0:C, :, :].rearrange("p e b -> p b e"),
                          m.ps[0:C, 0, 0:NIMG * EXPERTS].rearrange("p (b e) -> p b e", b=NIMG)
                          ).then_inc(ex.pooled_ready, 1)
    dve.wait_ge(ex.answer_in_psum, 1)
    nc.vector.tensor_copy(ex.answer[0:C, :].rearrange("p (b e) -> p e b", b=NIMG),
                          m.ps[0:C, 2, 0:NIMG * EXPERTS].rearrange("p (e b) -> p e b", b=NIMG)
                          ).then_inc(ex.answer_ready, 1)
    dve.wait_ge(ex.answer_turned, 1)
    nc.vector.tensor_copy(ex.answers[:, :, :], m.ps[:, 3, 0:GROUPS * C].rearrange("p (g c) -> p g c", g=GROUPS)
                          ).then_inc(ex.answer_sb, 1)
    for pr in range(PAIRS):
        dve.wait_ge(ex.spread, pr + 1)
        nc.vector.tensor_tensor(m.tokens[:, pr, :], m.tokens[:, pr, :],
                                m.ps[:, 4 + 2 * (pr % 2):6 + 2 * (pr % 2), :].rearrange("p a n -> p (a n)"),
                                ALU.add).then_inc(ex.joined, 1)


class Memory:
    pass


def program(nc, a, out):
    ctx = ExitStack()
    with ctx:
        def sb(name, shape, dt=F32):
            return ctx.enter_context(nc.sbuf_tensor(name, shape, dt))

        def sem(name):
            return ctx.enter_context(nc.semaphore(name))

        m = Memory()
        m.ps = ctx.enter_context(nc.psum_tensor("banks", [P, 8, BANK], F32))
        m.out = m.ps[:, 0:2, :].rearrange("p b n -> p (b n)")
        m.HY, m.HX, m.COORD, m.YB = 2, 4, 5, 6
        m.sel_coord = sb("sel_coord", [P, TAPS, P], F16)
        m.coord_bias = sb("coord_bias", [P, TAPS])
        m.hat_scale = sb("hat_scale", [P, 1])
        m.sel_x = sb("sel_x", [P, P], F16)
        m.sel_y = sb("sel_y", [P, NSEL, P], F16)
        m.identity = sb("identity", [P, P])
        m.zeros = sb("zeros", [P, BANK], F16)
        m.source = sb("source", [P, HP * W])
        m.dist = sb("dist", [P, 2, BANK])
        m.hat = sb("hat", [P, TAP_SLOTS, PIX])
        hi_lo = sb("hi_lo", [P, 2, TAP_SLOTS, PIX], F16)
        m.hi, m.lo = hi_lo[:, 0, :, :], hi_lo[:, 1, :, :]
        m.stack = sb("stack", [P, TAP_SLOTS, 2, PIX], F16)
        m.hx = sb("hx", [P, TAP_SLOTS, 2, PIX])
        m.y = sb("y", [P, NCHUNK, 2, 192])
        m.s = sb("s", [P, S_SLOTS, 2 * SPAN])
        m.tokens = sb("tokens", [P, PAIRS, PIX])
        bn = sb("bn", [P, 2, 4])
        bn_inv = sb("bn_inv", [P, 2])
        bn_shift = sb("bn_shift", [P, 2])
        bn_tmp = sb("bn_tmp", [P, 4])
        m.abs_max = sb("abs_max", [P, PAIRS + 1])
        m.off32 = m.s[:, 0:2, :]
        m.parts = m.s[:, 2:5, :].bitcast(BF16).rearrange("p a (b n) -> p (a b) n", b=2).rearrange(
            "p (s k) n -> p s k n", s=2)
        far = sb("far", [1, 6])
        far_flag = sb("far_flag", [1, 2], I32)
        m.b_off = sb("b_off", [P, 2])
        eps_bn = sb("eps_bn", [P, 1])

        loaded = sem("loaded")
        prepared = sem("prepared")
        bn_sqrt = sem("bn_sqrt")
        bn_steps = sem("bn_steps")
        bn_ready = sem("bn_ready")

        convs = []
        off = sb("off", [P, PAIRS + 1, PIX], BF16)
        pxpy = m.source[0:2, 0:PIX]
        pxpy16 = m.s[0:2, 2, :].bitcast(BF16)
        m.convs = convs
        m.x_loaded = [sem(f"x_loaded{i}") for i in range(PAIRS)]
        m.conv1_loaded, m.prepared, m.pxpy_placed = sem("conv1_loaded"), prepared, sem("pxpy_placed")
        w_off_loaded, pxpy_loaded, pxpy_cast = sem("w_off_loaded"), sem("pxpy_loaded"), sem("pxpy_cast")
        for k in range(2):
            cv = Conv()
            cv.k = k
            cv.src = sb(f"src{k}", [P, PAIRS, HP * WP])
            cv.off = off
            cv.w_off = sb(f"w_off{k}", [P, TAPS, 2 * NOFF])
            cv.w_dc = sb(f"w_dc{k}", [P, TAPS, C])
            cv.off_in_psum = sem(f"c{k}_off_in_psum")
            cv.max_ready = sem(f"c{k}_max_ready")
            cv.max_turned = sem(f"c{k}_max_turned")
            cv.max_steps = sem(f"c{k}_max_steps")
            cv.flag_ready = sem(f"c{k}_flag_ready")
            cv.pair_free = sem(f"c{k}_pair_free")
            cv.off_read = sem(f"c{k}_off_read")
            cv.split = sem(f"c{k}_split")
            cv.moved = [sem(f"c{k}_moved{i}") for i in range(2)]
            made = {}

            def shared(name, made=made):
                if name not in made:
                    made[name] = sem(name)
                return made[name]

            cv.near = Sampler(shared, f"c{k}", near_steps())
            cv.all = Sampler(shared, f"c{k}", all_steps())
            convs.append(cv)

        def finish0(i):
            dst = convs[1].src[:, bass.ds(i, 1), :].rearrange("p a (r c) -> p (a r) c", c=WP)
            return nc.scalar.activation(dst[:, PADR:PADR + H, PADC:PADC + W],
                                        m.out.rearrange("p (r c) -> p r c", c=W), ACT.Relu,
                                        bias=bn_shift[:, 0:1], scale=bn_inv[:, 0:1])

        def finish1(i):
            return nc.scalar.activation(m.tokens[:, bass.ds(i, 1), :].rearrange("p a n -> p (a n)"), m.out,
                                        ACT.Identity, bias=bn_shift[:, 1:2], scale=bn_inv[:, 1:2])

        convs[0].finish, convs[1].finish = finish0, finish1

        at = Attention()
        hx_all = m.hx[:, :, :, :].rearrange("p a b n -> p (a b n)")
        hat_all = m.hat[:, :, :].rearrange("p a n -> p (a n)")
        s_all = m.s[:, :, :].rearrange("p a n -> p (a n)")
        y_all = m.y[:, :, :, :].rearrange("p a b n -> p (a b n)")
        src0 = convs[0].src[:, :, :].rearrange("p a n -> p (a n)")
        src1 = convs[1].src[:, :, :].rearrange("p a n -> p (a n)")
        at.xh = src1[:, 0:WINDOW + PIX]
        at.square = src1[:, 1056:1056 + PIX]
        at.std = src1[:, 2080:2080 + PIX]
        at.g = hx_all[:, 0:2048].rearrange("p (s g j n) -> p s g j n", s=2, g=HG, j=TILES)
        at.windows = src1[:, 3104:4128].rearrange("p (s j n) -> p s j n", s=2, j=TILES)
        at.p = hx_all[:, 2048:3584].rearrange("p (s n) -> p s n", s=P_SLOTS)
        at.pn = hx_all[:, 3584:5120].rearrange("p (s n) -> p s n", s=P_SLOTS)
        at.pt = hx_all[:, 5120:6144].rearrange("p (s n) -> p s n", s=2)
        at.xw = hat_all[:, 0:2048].rearrange("p (s a j n) -> p s a j n", s=2, a=2, j=TILES)
        at.z = hat_all[:, 2048:3072].rearrange("p (s n) -> p s n", s=2)
        at.a_heads = s_all[:, 0:1024].rearrange("p (h n) -> p h n", h=HEADS)
        at.b_heads = y_all[:, 8192:8448].rearrange("p (h n) -> p h n", h=H4)
        at.stats = sb("stats", [P, P_SLOTS, 3, TILES * HG])
        at.mark = sb("mark", [P, 1])
        at.pair_done = sem("at_pair_done")
        at.mean_in_psum = sem("at_mean_in_psum")
        at.squared = sem("at_squared")
        at.var_in_psum = sem("at_var_in_psum")
        at.xh_ready = sem("at_xh_ready")
        at.g_in_psum = sem("at_g_in_psum")
        at.g_ready = sem("at_g_ready")
        at.xw_in_psum = sem("at_xw_in_psum")
        at.xw_ready = sem("at_xw_ready")
        at.scores_in_psum = sem("at_scores_in_psum")
        at.shifted = sem("at_shifted")
        at.probs_ready = sem("at_probs_ready")
        at.pt_in_psum = sem("at_pt_in_psum")
        at.pt_ready = sem("at_pt_ready")
        at.z_in_psum = sem("at_z_in_psum")
        at.z_ready = sem("at_z_ready")
        at.projected = sem("at_projected")
        at.added = sem("at_added")
        at.centred = sem("at_centred")
        at.std_ready = sem("at_std_ready")
        at.rstd_ready = sem("at_rstd_ready")
        at.windows_ready = sem("at_windows_ready")
        at.exp_ready = sem("at_exp_ready")
        at.max_ready = sem("at_max_ready")
        at.sum_ready = sem("at_sum_ready")
        at.rsum_ready = sem("at_rsum_ready")
        w_attn = y_all[0:C, 0:4 * HEADS * C].rearrange("p (k n) -> p k n", k=4)
        m.mean_of = sb("mean_of", [P, P])
        m.identity16 = sb("identity16", [P, P], F16)
        m.mask = sb("mask", [P, BANK], F16)
        m.eps_ln = sb("eps_ln", [P, 1])
        m.bu = sb("bu", [P, 1])
        m.w_gate = sb("w_gate", [P, 2 * EXPERTS])
        m.b_gate = sb("b_gate", [P, 1])
        m.ones = sb("ones", [1, NIMG])

        ex = Experts()
        ex.w1 = y_all[:, 0:8192].rearrange("p (e n) -> p e n", e=EXPERTS)
        ex.w2 = [buffer.bitcast(F32)[:, 0:EXPERTS * C].rearrange("p (e c) -> p e c", e=EXPERTS)
                 for buffer in (m.stack[:, :, :, :].rearrange("p a b n -> p (a b n)"),
                                hi_lo[:, :, :, :].rearrange("p a b n -> p (a b n)"))]
        ex.w2_bias = s_all[:, 1024:3072].rearrange("p (e c) -> p e c", e=EXPERTS)
        ex.xh = src0[:, 0:4096].rearrange("p (r n) -> p r n", r=PAIRS)
        ex.square = hat_all[:, 0:1024]
        ex.std = hat_all[:, 1024:2048]
        ex.xt = src1[:, 0:4096].rearrange("p (c r n) -> p c r n", c=CHUNKS, r=PAIRS)
        ex.pick = hx_all[:, 0:2048].rearrange("p (g n) -> p g n", g=GROUPS)
        ex.rest = hx_all[:, 2048:4096].rearrange("p (g n) -> p g n", g=GROUPS)
        ex.pt = hx_all[:, 4096:6144].rearrange("p (c n) -> p c n", c=CHUNKS)
        ex.pooled = hat_all[:, 2048:2304].rearrange("p (e b) -> p e b", e=EXPERTS)
        ex.hidden = hat_all[:, 2304:2816].rearrange("p (k e b) -> p k e b", k=MH, e=EXPERTS)
        ex.answer = hat_all[:, 2816:3072]
        ex.answers = y_all[:, 8448:8576].rearrange("p (g n) -> p g n", g=GROUPS)
        ex.top = sb("top", [P, GROUPS, 2, TOPK])
        ex.neg_max = sb("neg_max", [P, GROUPS])
        ex.gate_sum = sb("gate_sum", [P, GROUPS])
        ex.gate_rsum = sb("gate_rsum", [P, GROUPS])
        ex.mean_in_psum = sem("ex_mean_in_psum")
        ex.squared = sem("ex_squared")
        ex.var_in_psum = sem("ex_var_in_psum")
        ex.xh_ready = sem("ex_xh_ready")
        ex.logits_in_psum = sem("ex_logits_in_psum")
        ex.xt_in_psum = sem("ex_xt_in_psum")
        ex.xt_ready = sem("ex_xt_ready")
        ex.picked = sem("ex_picked")
        ex.pt_in_psum = sem("ex_pt_in_psum")
        ex.pt_ready = sem("ex_pt_ready")
        ex.pooled_in_psum = sem("ex_pooled_in_psum")
        ex.pooled_ready = sem("ex_pooled_ready")
        ex.w_loaded = sem("ex_w_loaded")
        ex.hidden_in_psum = sem("ex_hidden_in_psum")
        ex.hidden_ready = sem("ex_hidden_ready")
        ex.answer_in_psum = sem("ex_answer_in_psum")
        ex.answer_ready = sem("ex_answer_ready")
        ex.answer_turned = sem("ex_answer_turned")
        ex.answer_sb = sem("ex_answer_sb")
        ex.joined = sem("ex_joined")
        ex.spread = sem("ex_spread")
        ex.centred = sem("ex_centred")
        ex.std_ready = sem("ex_std_ready")
        ex.logits_ready = sem("ex_logits_ready")
        ex.gate_max = sem("ex_gate_max")
        ex.gate_exp = sem("ex_gate_exp")
        ex.rstd_ready = sem("ex_rstd_ready")
        ex.top_steps = sem("ex_top_steps")
        ex.pick_steps = sem("ex_pick_steps")
        ex.rsum_ready = sem("ex_rsum_ready")
        ex.ones_set = sem("ex_ones_set")

        heads_loaded = sem("heads_loaded")
        heads_in_psum, heads_ready, cleared = sem("heads_in_psum"), sem("heads_ready"), sem("cleared")
        out_done = sem("out_done")
        residual = sem("residual")

        block = ctx.enter_context(nc.Block())
        conv1_loads = [(convs[0].w_dc[:, :, :], a["w_dc1"]), (m.coord_bias[:, :], a["coord_bias"]),
                       (m.sel_coord[:, :, :], a["sel_coord"]), (m.sel_x[:, :], a["sel_x"])]
        loads = [(m.sel_y[:, :, :], a["sel_y"]), (bn[:, :, :], a["bn"]), (m.identity[:, :], a["identity"]),
                 (convs[1].w_off[:, :, :], a["w_off2"]), (convs[1].w_dc[:, :, :], a["w_dc2"]),
                 (m.mean_of[:, :], a["mean_of"]),
                 (m.identity16[:, :], a["identity16"]), (m.mask[:, :], a["mask"]), (m.bu[:, :], a["bu"]),
                 (m.w_gate[:, :], a["w_gate"]), (m.b_gate[:, :], a["b_gate"])]
        NLOAD = 16 * len(loads)

        @block.sync
        def _(sp):
            sp.dma_start(convs[0].w_off[:, :, :], a["w_off1"]).then_inc(w_off_loaded, 16)
            sp.dma_start(m.b_off[:, :], a["b_off"]).then_inc(w_off_loaded, 16)
            sp.dma_start(pxpy, a["pxpy"]).then_inc(pxpy_loaded, 16)
            for i in range(2):
                sp.dma_start(convs[0].src[:, i, :], a["x"][:, i, :]).then_inc(m.x_loaded[i], 16)
            sp.wait_ge(pxpy_cast, 1)
            for i in range(PAIRS):
                sp.dma_start(off[PX_ROW:NCOORD, i, :], pxpy16).then_inc(m.pxpy_placed, 16)
            for dst, src in conv1_loads:
                sp.dma_start(dst, src).then_inc(m.conv1_loaded, 16)
            for i in range(2, PAIRS):
                sp.dma_start(convs[0].src[:, i, :], a["x"][:, i, :]).then_inc(m.x_loaded[i], 16)
            for dst, src in loads:
                sp.dma_start(dst, src).then_inc(loaded, 16)
            for cv in convs:
                offsets_sp(nc, sp, m, cv)
                sp.wait_ge(cv.flag_ready, 1)
                flag = nc.sync.value_load(far_flag[0:1, cv.k:cv.k + 1], min_val=0, max_val=1)
                with sp.If(flag == 0):
                    sampler_sp(nc, sp, m, cv, cv.near)
                with sp.Else():
                    sampler_sp(nc, sp, m, cv, cv.all)
            sp.wait_ge(convs[1].pair_free, 1 + PAIRS)
            sp.wait_ge(convs[1].near.y_ready, PAIRS * NY + FIRST_Y)
            sp.dma_start(w_attn, a["w_attn"]).then_inc(heads_loaded, 16)
            sp.wait_ge(heads_in_psum, 2)
            sp.dma_start(ex.w1[0:C + 1, :, :], a["w1"]).then_inc(ex.w_loaded, 16)
            for k in range(MH):
                sp.dma_start(ex.w2[k], a["w2"][:, k, :, :]).then_inc(ex.w_loaded, 16)
            sp.dma_start(ex.w2_bias[0:1, :, :], a["w2_bias"]).then_inc(ex.w_loaded, 16)
            for i in range(PAIRS):
                sp.wait_ge(ex.joined, i + 1)
                sp.dma_start(out[i], m.tokens[:, i, :]).then_inc(out_done, 16)
            sp.wait_ge(out_done, 16 * PAIRS)

        @block.gpsimd
        def _(pool):
            nc.gpsimd.memset(m.off32[:, :, :], 0.0).then_inc(prepared, 1)
            nc.gpsimd.memset(eps_bn[:, :], EPS_BN).then_inc(prepared, 1)
            nc.gpsimd.memset(m.hat_scale[:, :], HAT_SCALE).then_inc(prepared, 1)
            nc.gpsimd.memset(m.eps_ln[:, :], EPS_LN).then_inc(prepared, 1)
            nc.gpsimd.memset(m.ones[:, :], 1.0).then_inc(prepared, 1)
            pool.wait_ge(pxpy_loaded, 16)
            nc.gpsimd.tensor_copy(pxpy16, pxpy).then_inc(pxpy_cast, 1)
            nc.gpsimd.memset(m.zeros[:, :], 0.0).then_inc(prepared, 1)
            nc.gpsimd.memset(off[:, PAIRS, :], 0.0).then_inc(prepared, 1)
            pool.wait_ge(pxpy_cast, 1)
            pool.wait_ge(m.x_loaded[0], 16)
            for cv in convs:
                if cv.k:
                    pool.wait_ge(convs[0].pair_free, 1 + PAIRS)
                sampler_pool(nc, pool, m, cv, cv.near, start=True)
                if cv.k == 0:
                    nc.gpsimd.memset(convs[1].src[:, :, :], 0.0).then_inc(prepared, 1)
                pool.wait_ge(cv.flag_ready, 1)
                flag = nc.gpsimd.value_load(far_flag[0:1, cv.k:cv.k + 1], min_val=0, max_val=1)
                with pool.If(flag == 0):
                    sampler_pool(nc, pool, m, cv, cv.near)
                with pool.Else():
                    sampler_pool(nc, pool, m, cv, cv.all)
            pool.wait_ge(convs[1].pair_free, 1 + PAIRS)
            pool.wait_ge(convs[1].pair_free, 1 + PAIRS)
            nc.gpsimd.memset(at.a_heads, 0.0).then_inc(cleared, 1)
            nc.gpsimd.memset(hat_all[:, 0:2048], 0.0).then_inc(cleared, 1)
            nc.gpsimd.memset(at.xh[:, 0:WINDOW], 0.0).then_inc(cleared, 1)
            for i in range(PAIRS):
                attention_pool(nc, pool, m, at, i)
            pool.wait_ge(at.pair_done, 1 + PAIRS)
            nc.gpsimd.memset(ex.pooled[C:C + 1, :, :], 1.0).then_inc(ex.ones_set, 1)

        @block.scalar
        def _(act):
            act.wait_ge(w_off_loaded, 32)
            act.wait_ge(prepared, 5)
            for cv in convs:
                offsets_act(nc, act, m, cv)
                if cv.k == 0:
                    act.wait_ge(loaded, NLOAD)
                    act.wait_ge(prepared, 8)
                    for k in range(2):
                        nc.scalar.activation(bn_tmp[:, k:k + 1], bn[:, k, 3:4], ACT.Sqrt, bias=eps_bn[:, 0:1]
                                             ).then_inc(bn_sqrt, 1)
                    act.wait_ge(bn_ready, 2)
                act.wait_ge(cv.flag_ready, 1)
                flag = nc.scalar.value_load(far_flag[0:1, cv.k:cv.k + 1], min_val=0, max_val=1)
                with act.If(flag == 0):
                    sampler_act(nc, act, m, cv, cv.near)
                with act.Else():
                    sampler_act(nc, act, m, cv, cv.all)
            act.wait_ge(cleared, 3)
            act.wait_ge(heads_in_psum, 2)
            for image in range(2):
                rows = slice(C * image, C * image + C)
                nc.scalar.activation(at.a_heads[rows, :, rows], m.ps[rows, 0, :].rearrange("p (h n) -> p h n", h=HEADS),
                                     ACT.Copy, scale=1.0 / 8.0).then_inc(heads_ready, 1)
            nc.scalar.copy(at.b_heads[:, :, :], m.ps[:, 1, 0:H4 * C].rearrange("p (h n) -> p h n", h=H4)
                           ).then_inc(heads_ready, 1)
            with act.Fori(0, PAIRS) as i:
                attention_act(nc, act, m, at, i)
            experts_act(nc, act, m, ex)

        @block.vector
        def _(dve):
            dve.wait_ge(prepared, 5)
            dve.wait_ge(m.pxpy_placed, 16 * PAIRS)
            for cv in convs:
                offsets_dve(nc, dve, m, cv)
                if cv.k == 0:
                    dve.wait_ge(bn_sqrt, 2)
                    nc.vector.reciprocal(bn_tmp[:, 2:4], bn_tmp[:, 0:2]).then_inc(bn_steps, 1)
                    dve.wait_ge(bn_steps, 1)
                    nc.vector.tensor_tensor(bn_inv[:, :], bn[:, :, 0], bn_tmp[:, 2:4], ALU.mult).then_inc(bn_steps, 1)
                    dve.wait_ge(bn_steps, 2)
                    nc.vector.tensor_tensor(bn_tmp[:, 0:2], bn[:, :, 2], bn_inv[:, :], ALU.mult).then_inc(bn_steps, 1)
                    dve.wait_ge(bn_steps, 3)
                    nc.vector.tensor_tensor(bn_shift[:, :], bn[:, :, 1], bn_tmp[:, 0:2], ALU.subtract
                                            ).then_inc(bn_ready, 2)
                R = slice(0, C + 2 * NOFF)
                dve.wait_ge(cv.max_ready, PAIRS)
                nc.vector.tensor_reduce(m.abs_max[R, PAIRS:PAIRS + 1], m.abs_max[R, 0:PAIRS], AX.X, ALU.max
                                        ).then_inc(cv.max_ready, 1)
                dve.wait_ge(cv.max_turned, 1)
                nc.vector.tensor_reduce(far[0:1, cv.k:cv.k + 1], m.ps[0:1, 0, 0:C + 2 * NOFF], AX.X, ALU.max
                                        ).then_inc(cv.max_steps, 1)
                dve.wait_ge(cv.max_steps, 1)
                nc.vector.tensor_scalar(far_flag[0:1, cv.k:cv.k + 1], far[0:1, cv.k:cv.k + 1], REACH, None,
                                        ALU.is_ge).then_inc(cv.flag_ready, 1)
                nc.vector.tensor_copy(far[0:1, 2 + cv.k:3 + cv.k], far[0:1, cv.k:cv.k + 1]).then_inc(cv.pair_free, 1)
                nc.vector.tensor_copy(far[0:1, 4 + cv.k:5 + cv.k], far[0:1, cv.k:cv.k + 1]
                                      ).then_inc(cv.near.sampled, S_SLOTS)
                dve.wait_ge(cv.flag_ready, 1)
                flag = nc.vector.value_load(far_flag[0:1, cv.k:cv.k + 1], min_val=0, max_val=1)
                with dve.If(flag == 0):
                    sampler_dve(nc, dve, m, cv, cv.near)
                with dve.Else():
                    sampler_dve(nc, dve, m, cv, cv.all)
            dve.wait_ge(convs[1].pair_free, 1 + PAIRS)
            src = convs[0].src[:, :, :].rearrange("p a (r c) -> p a r c", c=WP)
            for i in range(PAIRS):
                last = nc.vector.tensor_tensor(m.tokens[:, i, :].rearrange("p (r c) -> p r c", c=W),
                                               m.tokens[:, i, :].rearrange("p (r c) -> p r c", c=W),
                                               src[:, i, PADR:PADR + H, PADC:PADC + W], ALU.add)
            last.then_inc(residual, 1)
            dve.wait_ge(residual, 1)
            nc.vector.tensor_scalar(m.tokens[:, :, :], m.tokens[:, :, :], 0.0, None, ALU.max).then_inc(residual, 1)
            dve.wait_ge(cleared, 3)
            nc.vector.tensor_copy(at.mark[:, 0:1], m.bu[:, 0:1]).then_inc(at.pair_done, 1)
            with dve.Fori(0, PAIRS) as i:
                attention_dve(nc, dve, m, at, i)
            experts_dve(nc, dve, m, ex)

        @block.tensor
        def _(pe):
            pe.wait_ge(w_off_loaded, 32)
            for cv in convs:
                offsets_pe(nc, pe, m, cv)
                if cv.k == 0:
                    pe.wait_ge(loaded, NLOAD)
                for slot in range(2):
                    pe.wait_ge(cv.moved[slot], 96 * PAIRS // 2)
                pe.wait_ge(cv.max_ready, PAIRS + 1)
                nc.tensor.transpose(m.ps[0:1, 0, 0:C + 2 * NOFF], m.abs_max[0:C + 2 * NOFF, PAIRS:PAIRS + 1],
                                    m.identity[0:C + 2 * NOFF, 0:C + 2 * NOFF]).then_inc(cv.max_turned, 1)
                pe.wait_ge(cv.flag_ready, 1)
                flag = nc.tensor.value_load(far_flag[0:1, cv.k:cv.k + 1], min_val=0, max_val=1)
                with pe.If(flag == 0):
                    sampler_pe(nc, pe, m, cv, cv.near)
                with pe.Else():
                    sampler_pe(nc, pe, m, cv, cv.all)
            pe.wait_ge(heads_loaded, 16)
            for h in range(HEADS):
                for image in range(2):
                    last = nc.tensor.matmul(m.ps[C * image:C * image + C, 0, h * C:(h + 1) * C],
                                            w_attn[:, 0, h * C:(h + 1) * C],
                                            w_attn[:, 1, h * C:(h + 1) * C], start=True, stop=True)
            last.then_inc(heads_in_psum, 1)
            for h in range(HEADS):
                hg, h4 = divmod(h, H4)
                last = nc.tensor.matmul(m.ps[C * hg:C * hg + C, 1, h4 * C:(h4 + 1) * C],
                                        w_attn[:, 2, h * C:(h + 1) * C], w_attn[:, 3, h * C:(h + 1) * C],
                                        start=True, stop=True)
            last.then_inc(heads_in_psum, 1)
            pe.wait_ge(heads_ready, 3)
            pe.wait_ge(residual, 2)
            with pe.Fori(0, PAIRS) as i:
                attention_pe(nc, pe, m, at, i)
            pe.wait_ge(at.pair_done, 1 + PAIRS)
            experts_pe(nc, pe, m, ex)


def constants():
    f32, f16 = np.float32, np.float16
    c = {}
    sel = np.zeros((P, TAPS, P), f16)
    bias = np.zeros((P, TAPS), f32)
    q = np.arange(W)
    for t in range(TAPS):
        ky, kx = divmod(t, 3)
        for image in range(2):
            for axis in range(2):
                g = slice(64 * image + 32 * axis, 64 * image + 32 * axis + 32)
                for part in range(3):
                    sel[2 * NOFF * part + NOFF * image + 2 * t + (1 - axis), t, g] = 1
                sel[[PX_ROW, PY_ROW][axis], t, g] = 1
                bias[g, t] = 2 * [kx, ky][axis] - 2 - q
    c["sel_coord"], c["coord_bias"] = sel, bias
    r = np.arange(P)
    part = (r % 64) // 32
    c["sel_x"] = (((part == 0)[:, None]) & ((r % 32)[:, None] == (r % 32)[None, :])).astype(f16) * f16(1 / HAT_SCALE)
    starts = np.array(ALIGNED + SHIFTED)
    c["sel_y"] = ((part == 1)[:, None, None] &
                  ((r % 32)[:, None, None] == (starts[:, None] + (r // 32)[None, :])[None])).astype(f16) * f16(1 / HAT_SCALE)
    c["pxpy"] = np.stack([np.tile(np.arange(W), H), np.repeat(np.arange(H), W)]).astype(f32)
    c["identity"] = np.eye(P, dtype=f32)
    c["mean_of"] = np.kron(np.eye(2), np.full((C, C), 1.0 / C)).astype(f32)
    c["identity16"] = (np.eye(P) * MASK_SCALE).astype(f16)
    qq, kk = (np.arange(P) % TQ)[:, None], np.arange(KEYS)[None, :]
    c["mask"] = np.tile(np.where((kk > qq) & (kk <= qq + WINDOW), 0.0, MASKED), (1, TILES * HG)).astype(f16)
    return c


def layout(v):
    d = {}
    x = np.pad(v["x"], ((0, 0), (0, 0), (PADR, PADR), (PADC, PADC)))
    d["x"] = x.reshape(PAIRS, P, HP * WP).transpose(1, 0, 2)
    for k in (1, 2):
        w = v[f"L0_conv_w_off{k}"].transpose(1, 2, 3, 0).reshape(C, TAPS, NOFF)
        blocks = np.zeros((2, C, TAPS, 2, NOFF), w.dtype)
        blocks[0, :, :, 0] = w
        blocks[1, :, :, 1] = w
        d[f"w_off{k}"] = blocks.reshape(P, TAPS, 2 * NOFF)
        w = v[f"L0_conv_w_dc{k}"].transpose(1, 2, 3, 0).reshape(C, TAPS, C)
        d[f"w_dc{k}"] = np.concatenate([w, w])
    b_off = np.stack([np.tile(v[f"L0_conv_b_off{k}"], 2) for k in (1, 2)], 1)
    d["b_off"] = np.zeros((P, 2), b_off.dtype)
    d["b_off"][0:2 * NOFF] = d["b_off"][C:C + 2 * NOFF] = b_off
    d["bn"] = np.stack([np.stack([np.tile(v[f"L0_conv_{n}{k}"], 2) for n in ("g", "beta", "m", "v")], 1)
                        for k in (1, 2)], 1)
    per_head = [v[f"L1_attn_W{n}"].reshape(HEADS, C, C).transpose(1, 0, 2) for n in "qkv"]
    per_head.append(v["L1_attn_Wu"].T.reshape(HEADS, C, C).transpose(1, 0, 2))
    d["w_attn"] = np.stack(per_head, 1).reshape(C, 4, HEADS * C)
    d["bu"] = np.tile(v["L1_attn_bu"], 2)[:, None]
    gate = v["L1_ffn_gate_w"].T
    blocks = np.zeros((2, C, 2, EXPERTS), gate.dtype)
    blocks[0, :, 0] = gate
    blocks[1, :, 1] = gate
    d["w_gate"] = blocks.reshape(P, 2 * EXPERTS)
    d["b_gate"] = np.tile(v["L1_ffn_gate_b"], PER_GROUP)[:, None]
    d["w1"] = v["L1_ffn_weight1"].transpose(1, 0, 2)
    w2 = v["L1_ffn_weight2"]
    d["w2"] = w2[:, :HID].reshape(EXPERTS, MH, P, C).transpose(2, 1, 0, 3)
    d["w2_bias"] = w2[:, HID][None]
    return d


def kernel(**inputs):
    import numpy as _np
    import concourse.bacc as _bacc
    from concourse import mybir as _mybir
    from concourse.bass_utils import run_bass_kernel_spmd as _run

    nc = _bacc.Bacc("TRN2", target_bir_lowering=False, num_devices=1)
    given = {n: _np.asarray(x) for n, x in inputs.items()}
    arrays, aps = {}, {}
    for name, x in {**layout(given), **constants()}.items():
        x = _np.ascontiguousarray(x)
        arrays[f"in_{name}_dram"] = x
        aps[name] = nc.dram_tensor(f"in_{name}_dram", x.shape, _mybir.dt.from_np(x.dtype), kind="ExternalInput").ap()
    out = nc.dram_tensor("out_dram", (PAIRS, P, PIX), F32, kind="ExternalOutput").ap()
    program(nc, aps, out)
    r = _run(nc, [arrays], core_ids=[0])
    return r.results[0]["out_dram"].reshape(NIMG, C, H, W)
```

```python
import concourse.bass as bass
from concourse import mybir
from contextlib import ExitStack
import numpy as np

F32 = mybir.dt.float32
F16 = mybir.dt.float16
BF16 = mybir.dt.bfloat16
I32 = mybir.dt.int32
ALU = mybir.AluOpType
ACT = mybir.ActivationFunctionType
AX = mybir.AxisListType

NIMG, C, H, W = 8, 64, 32, 32
PAIRS = NIMG // 2
P = 128
PIX = H * W
TAPS = 9
NOFF = 2 * TAPS
PADR, PADC = 2, 1
HP, WP = H + 2 * PADR, W + 2 * PADC
BANK = 512
EPS_BN = 1e-5

CHUNK_ROWS = P // W
TILE = P
SPAN = 2 * TILE
REACH = 2.0
HAT_SCALE = 4096.0
ALIGNED = [CHUNK_ROWS * c for c in range(H // CHUNK_ROWS)]
SHIFTED = [CHUNK_ROWS * c - 2 for c in range(H // CHUNK_ROWS + 1)]
CHUNK_START = [ALIGNED, SHIFTED, ALIGNED]
CHUNK_BASE = [0, len(ALIGNED), len(ALIGNED) + len(SHIFTED)]
NCHUNK = 2 * len(ALIGNED) + len(SHIFTED)
SEL_BASE = [0, len(ALIGNED), 0]
NSEL = len(ALIGNED) + len(SHIFTED)
PX_ROW, PY_ROW, NCOORD = 3 * NOFF * 2, 3 * NOFF * 2 + 1, 3 * NOFF * 2 + 2

HY_BANKS, S_SLOTS, TAP_SLOTS = 2, 6, 3


def near_steps():
    out = []
    for t in range(TAPS):
        ky = t // 3
        back = [0, 1, 1][ky]
        ranges = [(c, min(max(TILE * (c - back), 0), PIX - SPAN)) for c in range(len(CHUNK_START[ky]))]
        for k in range(0, len(ranges), 2):
            for image in range(2):
                out.append((t, image, ranges[k:k + 2]))
    return out


def all_steps():
    out = []
    for t in range(TAPS):
        for c in range(len(CHUNK_START[t // 3])):
            for p0 in range(0, PIX, 2 * SPAN):
                for image in range(2):
                    out.append((t, image, [(c, p0), (c, p0 + SPAN)]))
    return out


CONV1_LOADS = 16 * 4


class Signals:

    def __init__(self, sem, name):
        self.coord_in_psum = sem(name + "_coord_in_psum")
        self.coord_read = sem(name + "_coord_read")
        self.hat_ready = sem(name + "_hat_ready")
        self.hi_ready = sem(name + "_hi_ready")
        self.lo_ready = sem(name + "_lo_ready")
        self.stacked = [sem(f"{name}_stacked{s}") for s in range(TAP_SLOTS)]
        self.hx_in_psum = sem(name + "_hx_in_psum")
        self.hx_ready = sem(name + "_hx_ready")
        self.hy_in_psum = sem(name + "_hy_in_psum")
        self.s_ready = sem(name + "_s_ready")
        self.sampled = sem(name + "_sampled")
        self.y_in_psum = sem(name + "_y_in_psum")
        self.y_ready = sem(name + "_y_ready")
        self.source_ready = sem(name + "_source_ready")


class Sampler(Signals):

    def __init__(self, sem, name, steps):
        Signals.__init__(self, sem, name)
        self.steps = steps
        self.last_of_tap = [max(n for n, s in enumerate(steps) if s[0] == t) + 1 for t in range(TAPS)]
        self.first_of_tap = [min(n for n, s in enumerate(steps) if s[0] == t) for t in range(TAPS)]


class Conv:
    pass


def hx_piece(t, k):
    tap, piece = (t + 1, k + 1) if k < 3 else (t + 2, 0)
    return tap, piece // 2, piece % 2


def sampler_steps(v):
    todo = {0: [(c, 1) for c in range(len(CHUNK_START[1]))], 3: [(c, 2) for c in range(len(CHUNK_START[2]))],
            7: [(c, 0) for c in range(len(CHUNK_START[0]))]}
    out, pending = [], []
    for n in range(0, len(v.steps), 2):
        t = v.steps[n][0]
        k = (n - v.first_of_tap[t]) // 2
        if k == 0:
            pending += todo.get(t, [])
        out.append((n, t, hx_piece(t, k) if k < 4 else None,
                    (t + AHEAD, k) if k < 2 else None, pending.pop(0) if pending else None))
    assert not pending
    return out


AHEAD = 3
NY = NCHUNK
FIRST_HX, NHX = 5, 4 * TAPS
FIRST_COORD, NCOORDS = 2 * AHEAD, 2 * TAPS
FIRST_Y = len(ALIGNED)
PER_SLOT = 64 * TAPS // TAP_SLOTS
RUNS = PAIRS * TAPS + AHEAD
FIRST_WORK = {(1, c): ("source", c) for c in range(FIRST_Y)}
FIRST_WORK.update({(2, 2 * k): ("distance", k) for k in range(5)})
FIRST_WORK.update({(3, 1): ("distance", 5), (3, 2): ("columns", 0), (3, 4): ("columns", 1), (3, 5): ("columns", 2),
                   (3, 6): ("columns", 3), (3, 8): ("columns", 4)})


def sampler_pe(nc, pe, m, cv, v, start=None):
    steps = v.steps
    nsteps = len(steps)

    def coord(i, t, half, seen):
        if seen:
            pe.wait_ge(v.coord_read, i * NCOORDS + seen)
        nc.tensor.matmul(m.ps[:, m.COORD, :], m.sel_coord[0:NCOORD, t % TAPS, :],
                         cv.off[0:NCOORD, bass.ds(i + t // TAPS, 1), half * BANK:(half + 1) * BANK],
                         start=True, stop=True).then_inc(v.coord_in_psum, 1)

    def columns(i, t, image, half, seen):
        if image == 0 and half == 0:
            pe.wait_ge(v.stacked[t % TAP_SLOTS], i * PER_SLOT + 64 * (t // TAP_SLOTS + 1))
        if seen:
            pe.wait_ge(v.hx_ready, i * NHX + seen)
        nc.tensor.matmul(m.ps[:, m.HX, :], m.sel_x[:, :],
                         m.stack[:, t % TAP_SLOTS, image, half * BANK:(half + 1) * BANK],
                         start=True, stop=True).then_inc(v.hx_in_psum, 1)

    def weighted(c, g):
        r0 = (CHUNK_START[g][c] + PADR) * W
        for image in range(2):
            half = slice(C * image, C * image + C)
            last = nc.tensor.matmul(m.ps[:, m.YB + image, 0:192], m.source[half, r0:r0 + P],
                                    cv.w_dc[half, 3 * g:3 * g + 3, :], start=True, stop=True)
        last.then_inc(v.y_in_psum, 1)

    def rows(i, n):
        t, image, parts = steps[n % nsteps]
        if n >= HY_BANKS:
            pe.wait_ge(v.s_ready, i * nsteps + n - HY_BANKS + 1)
        for j, (c, p0) in enumerate(parts):
            last = nc.tensor.matmul(m.ps[:, m.HY + n % HY_BANKS, j * SPAN:(j + 1) * SPAN],
                                    m.sel_y[:, SEL_BASE[t // 3] + c, :],
                                    m.stack[:, t % TAP_SLOTS, image, p0:p0 + SPAN], start=True, stop=True)
        last.then_inc(v.hy_in_psum, 1)

    def sample(i, n):
        t = steps[n][0]
        if n == v.first_of_tap[3 * (t // 3)]:
            pe.wait_ge(v.y_ready, i * NY + CHUNK_BASE[t // 3] + len(CHUNK_START[t // 3]))
        pe.wait_ge(v.s_ready, i * nsteps + n + 2)
        for j, (c, p0) in enumerate(steps[n][2]):
            cuts = [p0, BANK, p0 + SPAN] if p0 < BANK < p0 + SPAN else [p0, p0 + SPAN]
            for a, b in zip(cuts[:-1], cuts[1:]):
                for image in range(2):
                    at = j * SPAN + a - p0
                    last = nc.tensor.matmul(
                        m.out[C * image:C * image + C, a:b],
                        m.y[:, CHUNK_BASE[t // 3] + c, image, (t % 3) * C:(t % 3 + 1) * C],
                        m.s[:, (n + image) % S_SLOTS, at:at + b - a], start=False, stop=True, skip_group_check=True)
        last.then_inc(v.sampled, 2)

    if start:
        kind, k = start
        if kind == "source":
            pe.wait_ge(*((v.y_ready, k) if k else (v.source_ready, 1)))
            weighted(k, 0)
        elif kind == "distance":
            if k == 0:
                pe.wait_ge(cv.moved[0], 96)
            coord(0, k // 2, k % 2, k)
        else:
            columns(0, k // 4, k % 4 // 2, k % 2, k)
        return
    rows(0, 0)
    rows(0, 1)
    with pe.Fori(0, PAIRS) as i:
        pe.wait_ge(cv.pair_free, i + 1)
        for half in range(2):
            nc.tensor.matmul(m.out[:, half * BANK:(half + 1) * BANK], m.zeros[:, 0:P], m.zeros[:, :],
                             start=True, stop=True, skip_group_check=True)
        hx_seen, coord_seen, y_seen = FIRST_HX, FIRST_COORD, FIRST_Y
        for n, t, hx, distance, source in sampler_steps(v):
            rows(i, n + 2)
            if source:
                pe.wait_ge(v.y_ready, i * NY + y_seen)
            rows(i, n + 3)
            if source == (0, 0):
                pe.wait_ge(v.source_ready, i + 2)
            if n == nsteps - 2:
                sample(i, n)
            if hx:
                columns(i, *hx, hx_seen)
                hx_seen += 1
            if source:
                weighted(*source)
                y_seen += 1
            if distance:
                coord(i, *distance, coord_seen)
                coord_seen += 1
            if n < nsteps - 2:
                sample(i, n)
    pe.wait_ge(v.y_ready, PAIRS * NY + FIRST_Y)
    pe.wait_ge(v.hx_ready, PAIRS * NHX + FIRST_HX)
    pe.wait_ge(v.coord_read, PAIRS * NCOORDS + FIRST_COORD)


def sampler_act(nc, act, m, cv, v, start=None):
    nsteps = len(v.steps)

    def distance(i, t, half, seen):
        slot, cols = t % TAP_SLOTS, slice(half * BANK, (half + 1) * BANK)
        if half == 0 and t >= TAP_SLOTS:
            act.wait_ge(v.lo_ready, i * TAPS + t - TAP_SLOTS + 1)
            act.wait_ge(v.stacked[slot], i * PER_SLOT + 64 * (t // TAP_SLOTS))
        act.wait_ge(v.coord_in_psum, i * NCOORDS + seen + 1)
        nc.scalar.activation(m.dist[:, seen % 2, :], m.ps[:, m.COORD, :],
                             ACT.Abs, bias=m.coord_bias[:, t % TAPS:t % TAPS + 1]).then_inc(v.coord_read, 1)
        act.wait_ge(v.coord_read, i * NCOORDS + seen + 1)
        nc.scalar.activation(m.hi[:, slot, cols], m.dist[:, seen % 2, :], ACT.Relu,
                             bias=m.hat_scale[:, 0:1], scale=-HAT_SCALE).then_inc(v.hi_ready, 1)
        nc.scalar.activation(m.hat[:, slot, cols], m.dist[:, seen % 2, :], ACT.Relu,
                             bias=m.hat_scale[:, 0:1], scale=-HAT_SCALE).then_inc(v.hat_ready, 1)

    def columns(i, t, image, half, seen):
        if t - TAP_SLOTS >= 0:
            act.wait_ge(v.s_ready, i * nsteps + v.last_of_tap[t - TAP_SLOTS])
        act.wait_ge(v.hx_in_psum, i * NHX + seen + 1)
        nc.scalar.copy(m.hx[:, t % TAP_SLOTS, image, half * BANK:(half + 1) * BANK],
                       m.ps[:, m.HX, :]).then_inc(v.hx_ready, 1)

    def weighted(i, c, g, seen):
        act.wait_ge(v.y_in_psum, i * NY + seen + 1)
        nc.scalar.copy(m.y[:, CHUNK_BASE[g] + c, :, :],
                       m.ps[:, m.YB:m.YB + 2, 0:192]).then_inc(v.y_ready, 1)

    if start:
        kind, k = start
        if kind == "source":
            weighted(0, k, 0, k)
        elif kind == "distance":
            distance(0, k // 2, k % 2, k)
        else:
            columns(0, k // 4, k % 4 // 2, k % 2, k)
        return
    with act.Fori(0, PAIRS) as i:
        hx_seen, coord_seen, y_seen = FIRST_HX, FIRST_COORD, FIRST_Y
        for n, t, hx, far, source in sampler_steps(v):
            if n == nsteps - 2:
                act.wait_ge(v.sampled, S_SLOTS + i * nsteps + nsteps)
                cv.finish(i).then_inc(cv.pair_free, 1)
            if hx:
                columns(i, *hx, hx_seen)
                hx_seen += 1
            if source:
                if source == (0, 0):
                    act.wait_ge(v.sampled, S_SLOTS + i * nsteps + v.last_of_tap[2])
                weighted(i, *source, y_seen)
                y_seen += 1
            if far:
                distance(i, *far, coord_seen)
                coord_seen += 1
    act.wait_ge(v.lo_ready, RUNS)
    for slot in range(TAP_SLOTS):
        act.wait_ge(v.stacked[slot], 64 * (RUNS // TAP_SLOTS))


def sampler_dve(nc, dve, m, cv, v):
    nsteps = len(v.steps)
    with dve.Fori(0, PAIRS) as i:
        for n, (t, image, parts) in enumerate(v.steps):
            dve.wait_ge(v.sampled, i * nsteps + 2 * (n // 2) + 2)
            if n - image == v.first_of_tap[t]:
                dve.wait_ge(v.hx_ready, i * NHX + 4 * t + 2 * image + 2)
            dve.wait_ge(v.hy_in_psum, i * nsteps + n + 1)
            p0 = parts[0][1]
            hx = m.hx[:, t % TAP_SLOTS, image, p0:p0 + SPAN]
            hx = bass.AP(hx.tensor, hx.offset, [hx.ap[0], [parts[-1][1] - p0, len(parts)], [1, SPAN]])
            dst = m.s[:, n % S_SLOTS, 0:SPAN * len(parts)].rearrange("p (k n) -> p k n", n=SPAN)
            hy = m.ps[:, m.HY + n % HY_BANKS, 0:SPAN * len(parts)].rearrange("p (k n) -> p k n", n=SPAN)
            nc.vector.tensor_tensor(dst, hx, hy, ALU.mult).then_inc(v.s_ready, 1)


def sampler_pool(nc, pool, m, cv, v, start=False):
    def source(i):
        nc.gpsimd.tensor_copy(m.source[:, :].rearrange("p (r c) -> p r c", c=W),
                              cv.src[:, i, :].rearrange("p (r c) -> p r c", c=WP)[:, :, PADC:PADC + W]
                              ).then_inc(v.source_ready, 1)

    if start:
        source(0)
    for run in range(0, AHEAD) if start else range(AHEAD, RUNS):
        slot = run % TAP_SLOTS
        if run >= TAP_SLOTS:
            pool.wait_ge(v.stacked[slot], 64 * (run // TAP_SLOTS))
        pool.wait_ge(v.hat_ready, 2 * run + 2)
        nc.gpsimd.tensor_tensor(m.lo[:, slot, :], m.hat[:, slot, :], m.hi[:, slot, :],
                                ALU.subtract).then_inc(v.lo_ready, 1)
        if run >= AHEAD and (run - AHEAD) % TAPS == 5 and not start:
            i = (run - AHEAD) // TAPS
            pool.wait_ge(v.y_in_psum, NY * (i + 1))
            source(min(i + 1, PAIRS - 1))
        if cv.k == 1 and run >= AHEAD + TAPS and (run - AHEAD) % TAPS == 2 and not start:
            residual(nc, pool, m, cv, (run - AHEAD) // TAPS - 1)
    if not start:
        for slot in range(TAP_SLOTS):
            pool.wait_ge(v.stacked[slot], 64 * (RUNS // TAP_SLOTS))
        pool.wait_ge(v.y_in_psum, PAIRS * NY + FIRST_Y)


def residual(nc, pool, m, cv, i):
    tok = m.tokens[:, i, :].rearrange("p (r c) -> p r c", c=W)
    src = m.convs[0].src[:, i, :].rearrange("p (r c) -> p r c", c=WP)
    pool.wait_ge(cv.pair_free, i + 2)
    nc.gpsimd.tensor_tensor(tok, tok, src[:, PADR:PADR + H, PADC:PADC + W], ALU.add).then_inc(m.residual, 1)
    pool.wait_ge(m.residual, i + 1)
    nc.gpsimd.tensor_scalar(tok, tok, 0.0, None, ALU.max).then_inc(m.tokens_ready, 1)


def sampler_sp(nc, sp, m, cv, v, start=None):
    nsteps = len(v.steps)
    for run in range(AHEAD, RUNS) if start is None else [start]:
        slot = run % TAP_SLOTS
        if run >= TAP_SLOTS:
            i, t = divmod(run - TAP_SLOTS, TAPS)
            sp.wait_ge(v.hy_in_psum, i * nsteps + v.last_of_tap[t])
        sp.wait_ge(v.hi_ready, 2 * run + 2)
        for image in range(2):
            sp.dma_start(m.stack[0:C, slot, image, :], m.hi[C * image:C * image + C, slot, :]
                         ).then_inc(v.stacked[slot], 16)
        sp.wait_ge(v.lo_ready, run + 1)
        for image in range(2):
            sp.dma_start(m.stack[C:P, slot, image, :], m.lo[C * image:C * image + C, slot, :]
                         ).then_inc(v.stacked[slot], 16)


def offsets_pe(nc, pe, m, cv):
    for i in range(PAIRS):
        src = cv.src[:, i, :].rearrange("p (r c) -> p r c", c=WP)
        if cv.k == 0:
            pe.wait_ge(m.x_loaded[i], 16)
        else:
            pe.wait_ge(m.convs[0].pair_free, 1 + PAIRS)
        if i >= 2:
            pe.wait_ge(cv.off_read, 2 * i - 2)
        for t in range(TAPS):
            for half in range(2):
                r0 = PADR - 1 + t // 3 + half * (H // 2)
                last = nc.tensor.matmul(m.ps[C * half:C * half + 2 * NOFF, 2 * (i % 2) + half, :], cv.w_off[:, t, :],
                                        src[:, r0:r0 + H // 2, t % 3:t % 3 + W],
                                        start=(t == 0), stop=(t == TAPS - 1))
            if t == TAPS - 1:
                last.then_inc(cv.off_in_psum, 1)
            if (i, t) == (1, 0) and cv.k == 0:
                pe.wait_ge(m.conv1_loaded, CONV1_LOADS)
                pe.wait_ge(m.prepared, 6)
                pe.wait_ge(m.pxpy_placed, 16 * PAIRS)
            if (i, t) in FIRST_WORK:
                sampler_pe(nc, pe, m, cv, cv.near, start=FIRST_WORK[i, t])


def offsets_act(nc, act, m, cv):
    for i in range(PAIRS):
        if i == 1 and cv.k == 0:
            act.wait_ge(m.conv1_loaded, CONV1_LOADS)
        for t in range(TAPS):
            if (i, t) in FIRST_WORK:
                sampler_act(nc, act, m, cv, cv.near, start=FIRST_WORK[i, t])
        act.wait_ge(cv.off_in_psum, i + 1)
        if i >= 2:
            act.wait_ge(cv.split, 4 * (i - 1))
        for half in range(2):
            rows = slice(C * half, C * half + 2 * NOFF)
            nc.scalar.activation(m.off32[rows, i % 2, :], m.ps[rows, 2 * (i % 2) + half, :], ACT.Identity,
                                 bias=m.b_off[rows, cv.k:cv.k + 1]).then_inc(cv.off_read, 1)


def offsets_dve(nc, dve, m, cv):
    R = slice(0, C + 2 * NOFF)
    for i in range(PAIRS):
        o = m.off32[R, i % 2, :]
        dve.wait_ge(cv.off_read, 2 * i + 2)
        nc.vector.tensor_reduce(m.abs_max[R, i:i + 1], o, AX.X, ALU.max, apply_absolute_value=True
                                ).then_inc(cv.max_ready, 1)
        if i == PAIRS - 1:
            dve.wait_ge(cv.max_ready, PAIRS)
            nc.vector.tensor_reduce(m.abs_max[R, PAIRS:PAIRS + 1], m.abs_max[R, 0:PAIRS], AX.X, ALU.max
                                    ).then_inc(cv.max_ready, 1)
        if i >= 2:
            dve.wait_ge(cv.moved[i % 2], 96)
        nc.vector.tensor_copy(m.parts[R, i % 2, 0, :], o).then_inc(cv.split, 1)
        dve.wait_ge(cv.split, 4 * i + 1)
        dve.wait_ge(cv.max_ready, i + 1)
        nc.vector.tensor_tensor(o, o, m.parts[R, i % 2, 0, :], ALU.subtract).then_inc(cv.split, 1)
        dve.wait_ge(cv.split, 4 * i + 2)
        nc.vector.tensor_copy(m.parts[R, i % 2, 1, :], o).then_inc(cv.split, 1)
        dve.wait_ge(cv.split, 4 * i + 3)
        nc.vector.tensor_tensor(m.parts[R, i % 2, 2, :], o, m.parts[R, i % 2, 1, :], ALU.subtract
                                ).then_inc(cv.split, 1)


def offsets_sp(nc, sp, m, cv):
    for i in range(PAIRS):
        for part in range(3):
            sp.wait_ge(cv.split, 4 * i + [1, 3, 4][part])
            for half in range(2):
                sp.dma_start(cv.off[2 * NOFF * part:2 * NOFF * (part + 1), i, half * BANK:(half + 1) * BANK],
                             m.parts[C * half:C * half + 2 * NOFF, i % 2, part, :]).then_inc(cv.moved[i % 2], 16)
        for run in [[], [0, 1], [2], []][i]:
            sampler_sp(nc, sp, m, cv, cv.near, start=run)


HEADS, WINDOW, TQ = 8, 32, 32
HG = 2
H4 = HEADS // HG
KEYS = TQ + WINDOW
TILES = P // TQ
BLOCKS = PIX // P
EPS_LN = 1e-5
STATS = 2 * PIX // P
MASK_SCALE, MASKED = 32768.0, -65504.0


class Attention:
    pass


class Experts:
    pass


class LayerNorm:
    pass


def norm_pe(nc, pe, m, ln, beside):
    for pr in range(PAIRS):
        if ("turn", pr) in beside:
            beside["turn", pr]()
        pe.wait_ge(ln.tokens_ready, pr + 1)
        if pr >= 2:
            pe.wait_ge(ln.centred, pr - 1)
        for b in range(PIX // P):
            last = nc.tensor.transpose(m.ps[:, 4 * (pr % 2) + b // 4, b % 4 * P:(b % 4 + 1) * P],
                                       m.tokens[:, pr, b * P:(b + 1) * P], m.identity[:, :])
        last.then_inc(ln.turned, 1)
    for pr in range(PAIRS):
        if ("back", pr) in beside:
            beside["back", pr]()
        pe.wait_ge(ln.scaled, pr + 1)
        if pr >= 2:
            pe.wait_ge(ln.normed, pr - 1)
        for b in range(PIX // P):
            last = nc.tensor.transpose(m.ps[:, 4 * (pr % 2) + 2 + b // 4, b % 4 * P:(b % 4 + 1) * P],
                                       ln.xt[pr][:, b, :], m.identity[:, :])
        last.then_inc(ln.back_in_psum, 1)


def norm_act(nc, act, m, ln, beside):
    def square(pr):
        act.wait_ge(ln.centred, pr + 1)
        if pr >= 2:
            act.wait_ge(ln.squares_summed, pr - 1)
        nc.scalar.activation(ln.square[:, pr % 2, :, :], ln.xt[pr], ACT.Square).then_inc(ln.squared, 1)

    square(0)
    square(1)
    for stage in range(PAIRS + 1):
        if stage in beside:
            beside[stage]()
        pr = stage
        if pr < PAIRS:
            act.wait_ge(ln.squares_summed, pr + 1)
            nc.scalar.activation(ln.rstd[:, pr, :], ln.squares[:, pr, :], ACT.Sqrt, bias=m.eps_ln[:, 0:1],
                                 scale=1.0 / C).then_inc(ln.std_ready, 1)
            if pr + 2 < PAIRS:
                square(pr + 2)
        pr = stage - 1
        if pr >= 0:
            act.wait_ge(ln.back_in_psum, pr + 1)
            nc.scalar.copy(ln.xh[pr].rearrange("p (a n) -> p a n", a=2), m.ps[:, 4 * (pr % 2) + 2:4 * (pr % 2) + 4, :]
                           ).then_inc(ln.normed, 1)


def norm_dve(nc, dve, m, ln):
    def over_channels(stat):
        return stat.rearrange("p (b a) -> p b a", a=2).unsqueeze(3).to_broadcast([P, PIX // P, 2, C])

    def centre(pr):
        turned = m.ps[:, 4 * (pr % 2):4 * (pr % 2) + 2, :].rearrange("p a n -> p (a n)").rearrange(
            "p (b a c) -> p b a c", a=2, c=C)
        dve.wait_ge(ln.turned, pr + 1)
        nc.vector.tensor_reduce(ln.mean[:, pr, :].rearrange("p (b a) -> p b a", a=2), turned, AX.X, ALU.add
                                ).then_inc(ln.summed, 1)
        dve.wait_ge(ln.summed, pr + 1)
        nc.vector.tensor_scalar(ln.mean[:, pr, :], ln.mean[:, pr, :], 1.0 / C, None, ALU.mult
                                ).then_inc(ln.mean_ready, 1)
        dve.wait_ge(ln.mean_ready, pr + 1)
        nc.vector.tensor_tensor(ln.xt[pr].rearrange("p b (a c) -> p b a c", a=2), turned,
                                over_channels(ln.mean[:, pr, :]), ALU.subtract).then_inc(ln.centred, 1)

    def variance(pr):
        dve.wait_ge(ln.squared, pr + 1)
        nc.vector.tensor_reduce(ln.squares[:, pr, :].rearrange("p (b a) -> p b a", a=2),
                                ln.square[:, pr % 2, :, :].rearrange("p b (a c) -> p b a c", a=2), AX.X, ALU.add
                                ).then_inc(ln.squares_summed, 1)

    def invert(pr):
        dve.wait_ge(ln.std_ready, pr + 1)
        nc.vector.reciprocal(ln.rstd[:, pr, :], ln.rstd[:, pr, :]).then_inc(ln.rstd_ready, 1)

    centre(0)
    for pr in range(PAIRS):
        if pr + 1 < PAIRS:
            centre(pr + 1)
        if pr:
            invert(pr - 1)
        variance(pr)
    invert(PAIRS - 1)


def norm_pool(nc, pool, m, ln):
    for pr in range(PAIRS):
        pool.wait_ge(ln.rstd_ready, pr + 1)
        x = ln.xt[pr].rearrange("p b (a c) -> p b a c", a=2)
        nc.gpsimd.tensor_tensor(x, x, ln.rstd[:, pr, :].rearrange("p (b a) -> p b a", a=2).unsqueeze(3).to_broadcast(
            [P, PIX // P, 2, C]), ALU.mult).then_inc(ln.scaled, 1)


TURN_AHEAD, SCORES_AHEAD, QUERIES_AHEAD = 1, 2, 3
ALL_BLOCKS = PAIRS * BLOCKS


def attention_pe(nc, pe, m, at):
    def queries(i, b, hg):
        if b:
            pe.wait_ge(at.g_ready, (i * BLOCKS + b - 1) * 2 + hg + 1)
        first = WINDOW + b % BLOCKS * P
        for h in range(H4):
            last = nc.tensor.matmul(m.ps[:, hg, h * P:(h + 1) * P], at.a_heads[:, hg * H4 + h, :],
                                    at.xh[:, bass.ds(i + b // BLOCKS, 1), first:first + P], start=True, stop=True)
        last.then_inc(at.g_in_psum, 1)

    def scores(i, b):
        pe.wait_ge(at.g_ready, (i * BLOCKS + b) * 2 + 2)
        pe.wait_ge(at.pair_windows_ready, i * BLOCKS + b + 1)
        if b:
            pe.wait_ge(at.shifted, i * BLOCKS + b)
        for bank in range(2):
            nc.tensor.matmul(m.ps[:, 2 + bank, :], m.identity16[:, :], m.mask[:, :], start=True, stop=False,
                             skip_group_check=True)
        for j in range(TILES):
            for hg in range(HG):
                bank, first = divmod((j * HG + hg) * 2 * KEYS, BANK)
                last = nc.tensor.matmul(m.ps[:, 2 + bank, first:first + 2 * KEYS], at.g[:, b % 2, hg, j, :],
                                        at.pair_windows[:, b % 2, j, :, :], start=False, stop=True,
                                        skip_group_check=True)
        last.then_inc(at.scores_in_psum, 1)

    def turn_keys(i, b):
        if b:
            pe.wait_ge(at.xw_ready, (i * BLOCKS + b) * 2)
        pe.wait_ge(at.windows_ready, i * BLOCKS + b + 1)
        for j in range(TILES):
            last = nc.tensor.transpose(m.ps[:, 5, j * P:(j + 1) * P], at.windows[:, b % 4, j, :], m.identity[:, :])
        last.then_inc(at.xw_in_psum, 1)

    def turn_probs(i, b, image):
        if image == 0:
            pe.wait_ge(at.probs_ready, i * BLOCKS + b + 1)
        if b or image:
            pe.wait_ge(at.pt_ready, (i * BLOCKS + b) * 2 + image)
        for j in range(TILES):
            last = nc.tensor.transpose(m.ps[:, 4, j * P:(j + 1) * P], at.p[:, b % 2, image, j * P:(j + 1) * P],
                                       m.identity[:, :])
        last.then_inc(at.pt_in_psum, 1)

    def values(i, b, image):
        pe.wait_ge(at.pt_ready, (i * BLOCKS + b) * 2 + image + 1)
        if image == 0:
            pe.wait_ge(at.xw_ready, (i * BLOCKS + b) * 2 + 2)
        pe.wait_ge(at.z_ready, (i * BLOCKS + b) * 2 + image + 1)
        for j in range(TILES):
            last = nc.tensor.matmul(m.ps[:, 6, j * P:(j + 1) * P], at.xw[:, b % 2, image, j, :],
                                    at.pt[:, image, j * P:(j + 1) * P], start=True, stop=True)
        last.then_inc(at.z_in_psum, 1)

    def project_values(i, b):
        pe.wait_ge(at.z_ready, (i * BLOCKS + b) * 2 + 3)
        pe.wait_ge(at.added, i * BLOCKS + b + 1)
        z = at.z[:, :, :].rearrange("p a (j h q) -> p a h j q", j=TILES, h=H4)
        for h in range(H4):
            for image in range(2):
                last = nc.tensor.matmul(m.ps[C * image:C * image + C, 7, (b % 2) * P:(b % 2 + 1) * P],
                                        at.b_heads[:, h, :], z[:, image, h, :, :], start=(h == 0), stop=(h == H4 - 1),
                                        skip_group_check=True)
        last.then_inc(at.projected, 1)

    for hg in range(HG):
        queries(0, 0, hg)
    scores(0, 0)
    turn_keys(0, 0)
    for hg in range(HG):
        queries(0, 1, hg)
    scores(0, 1)
    for hg in range(HG):
        queries(0, 2, hg)
    for image in range(2):
        turn_probs(0, 0, image)
    with pe.Fori(0, PAIRS) as i:
        for b in range(BLOCKS):
            scores(i, b + SCORES_AHEAD)
            values(i, b, 0)
            turn_probs(i, b + TURN_AHEAD, 0)
            queries(i, b + QUERIES_AHEAD, 0)
            values(i, b, 1)
            turn_probs(i, b + TURN_AHEAD, 1)
            queries(i, b + QUERIES_AHEAD, 1)
            turn_keys(i, b + TURN_AHEAD)
            project_values(i, b)
    pe.wait_ge(at.g_ready, (ALL_BLOCKS + QUERIES_AHEAD) * 2)
    pe.wait_ge(at.shifted, ALL_BLOCKS + SCORES_AHEAD)
    pe.wait_ge(at.pt_ready, (ALL_BLOCKS + TURN_AHEAD) * 2)
    pe.wait_ge(at.xw_ready, (ALL_BLOCKS + TURN_AHEAD) * 2)


def attention_act(nc, act, m, at):
    def queries(i, b, hg):
        if b >= 2:
            act.wait_ge(at.scores_in_psum, i * BLOCKS + b - 1)
        act.wait_ge(at.g_in_psum, (i * BLOCKS + b) * 2 + hg + 1)
        nc.scalar.copy(at.g[:, b % 2, hg, :, :].rearrange("p j (h q) -> p h j q", h=H4),
                       m.ps[:, hg, :].rearrange("p (h j q) -> p h j q", h=H4, j=TILES)).then_inc(at.g_ready, 1)

    def exponentials(i, b):
        act.wait_ge(at.shifted, i * BLOCKS + b + 1)
        nc.scalar.activation(at.p[:, b % 2, :, :], at.p[:, b % 2, :, :], ACT.Exp).then_inc(at.exp_ready, 1)

    def probs(i, b, image):
        if b:
            act.wait_ge(at.z_in_psum, (i * BLOCKS + b - 1) * 2 + image + 1)
        act.wait_ge(at.pt_in_psum, (i * BLOCKS + b) * 2 + image + 1)
        nc.scalar.copy(at.pt[:, image, :], m.ps[:, 4, :]).then_inc(at.pt_ready, 1)

    def values(i, b, image):
        if image == 0:
            act.wait_ge(at.projected, i * BLOCKS + b + 1)
        act.wait_ge(at.z_in_psum, (i * BLOCKS + b) * 2 + image + 1)
        nc.scalar.copy(at.z[:, image, :], m.ps[:, 6, :]).then_inc(at.z_ready, 1)

    for hg in range(HG):
        queries(0, 0, hg)
    for hg in range(HG):
        queries(0, 1, hg)
    exponentials(0, 0)
    exponentials(0, 1)
    for hg in range(HG):
        queries(0, 2, hg)
    for image in range(2):
        probs(0, 0, image)
    with act.Fori(0, PAIRS) as i:
        for b in range(BLOCKS):
            values(i, b, 0)
            probs(i, b + TURN_AHEAD, 0)
            exponentials(i, b + SCORES_AHEAD)
            queries(i, b + QUERIES_AHEAD, 0)
            values(i, b, 1)
            probs(i, b + TURN_AHEAD, 1)
            queries(i, b + QUERIES_AHEAD, 1)


def attention_dve(nc, dve, m, at):
    bank = m.ps[:, 2:4, :].rearrange("p a n -> p (a n)").rearrange("p (g a k) -> p a g k", a=2, k=KEYS)

    def block(b):
        return at.p[:, b % 2, :, :].rearrange("p a (g k) -> p a g k", k=KEYS)

    def less_max(i, b):
        st = at.stats[:, b % 2, :, :, :]
        dve.wait_ge(at.scores_in_psum, i * BLOCKS + b + 1)
        if b >= 2:
            dve.wait_ge(at.pt_in_psum, (i * BLOCKS + b - 1) * 2)
        nc.vector.tensor_reduce(st[:, 0, :, :], bank, AX.X, ALU.max).then_inc(at.max_ready, 1)
        dve.wait_ge(at.max_ready, i * BLOCKS + b + 1)
        nc.vector.tensor_tensor(block(b), bank, st[:, 0, :, :].unsqueeze(3).to_broadcast([P, 2, TILES * HG, KEYS]),
                                ALU.subtract).then_inc(at.shifted, 1)

    def sums(i, b):
        st = at.stats[:, b % 2, :, :, :]
        dve.wait_ge(at.exp_ready, i * BLOCKS + b + 1)
        nc.vector.tensor_reduce(st[:, 1, :, :], block(b), AX.X, ALU.add).then_inc(at.sum_ready, 1)
        dve.wait_ge(at.sum_ready, i * BLOCKS + b + 1)
        nc.vector.reciprocal(st[:, 2, :, :], st[:, 1, :, :]).then_inc(at.rsum_ready, 1)

    def keys(i, b):
        dve.wait_ge(at.xw_in_psum, i * BLOCKS + b + 1)
        if b:
            dve.wait_ge(at.projected, i * BLOCKS + b)
        for hg in range(HG):
            rows = slice(KEYS * hg, KEYS * hg + KEYS)
            nc.vector.tensor_copy(at.xw[rows, b % 2, :, :, hg * C:(hg + 1) * C].rearrange("p a j c -> p j a c"),
                                  m.ps[rows, 5, :].rearrange("p (j a c) -> p j a c", j=TILES, a=2)
                                  ).then_inc(at.xw_ready, 1)

    def join(i, b):
        dve.wait_ge(at.projected, i * BLOCKS + b + 2)
        tok = m.tokens[:, bass.ds(i, 1), b * P:(b + 1) * P].rearrange("p a n -> p (a n)")
        nc.vector.scalar_tensor_tensor(tok, m.ps[:, 7, (b % 2) * P:(b % 2 + 1) * P], m.bu[:, 0:1], tok,
                                       ALU.add, ALU.add).then_inc(at.added, 1)

    nc.vector.tensor_copy(at.mark[:, 0:1], m.bu[:, 0:1]).then_inc(at.z_ready, 1)
    nc.vector.tensor_copy(at.mark[:, 1:2], m.bu[:, 0:1]).then_inc(at.projected, 1)
    nc.vector.tensor_copy(at.mark[:, 2:3], m.bu[:, 0:1]).then_inc(at.added, 2)
    keys(0, 0)
    less_max(0, 0)
    less_max(0, 1)
    sums(0, 0)
    sums(0, 1)
    with dve.Fori(0, PAIRS) as i:
        for b in range(BLOCKS):
            less_max(i, b + SCORES_AHEAD)
            sums(i, b + SCORES_AHEAD)
            keys(i, b + TURN_AHEAD)
            join(i, b)


def attention_pool(nc, pool, m, at):
    def windows(b):
        if b >= 4:
            pool.wait_ge(at.xw_in_psum, b - 3)
        if b % BLOCKS == 0 and b < ALL_BLOCKS:
            pool.wait_ge(at.ln.normed, b // BLOCKS + 1)
        first = at.xh[:, b // BLOCKS, b % BLOCKS * P:b % BLOCKS * P + KEYS]
        nc.gpsimd.tensor_copy(at.windows[:, b % 4, :, :].rearrange("p j (a k) -> p j a k", a=2),
                              bass.AP(first.tensor, first.offset, [first.ap[0], [TQ, TILES], [0, 2], [1, KEYS]])
                              ).then_inc(at.windows_ready, 1)
        if b >= 2:
            pool.wait_ge(at.scores_in_psum, b - 1)
        nc.gpsimd.tensor_tensor(at.pair_windows[:, b % 2, :, :, :],
                                bass.AP(first.tensor, first.offset, [first.ap[0], [TQ, TILES], [0, 2], [1, KEYS]]),
                                m.image_of[:, :].unsqueeze(1).unsqueeze(3).to_broadcast([P, TILES, 2, KEYS]),
                                ALU.mult).then_inc(at.pair_windows_ready, 1)

    def probs(b):
        p = at.p[:, b % 2, :, :].rearrange("p a (g k) -> p (a g) k", k=KEYS)
        pool.wait_ge(at.rsum_ready, b + 1)
        scale = at.stats[:, b % 2, 2, :, :].rearrange("p a g -> p (a g)")
        nc.gpsimd.tensor_tensor(p, p, scale.unsqueeze(2).to_broadcast([P, 2 * TILES * HG, KEYS]),
                                ALU.mult).then_inc(at.probs_ready, 1)

    for b in range(QUERIES_AHEAD):
        windows(b)
    for b in range(ALL_BLOCKS + TURN_AHEAD):
        probs(b)
        if b + QUERIES_AHEAD < ALL_BLOCKS + SCORES_AHEAD:
            windows(b + QUERIES_AHEAD)


EXPERTS, TOPK, HID = 32, 8, 256
GROUPS = NIMG * EXPERTS // P
PER_GROUP = NIMG // GROUPS
CHUNKS = PIX // P
MH = HID // P
HIDDEN_TURNED = [2, 3, 6, 7]
POOLED, POOLED_TURNED, ANSWER, ANSWERS = 2, 3, 0, 3
HIDDEN_BANKS, ANSWER_TURNED = [0, 1, 4, 5], [4, 5]
SIDE, ROWS = 4, 32


def experts_pe(nc, pe, m, ex):
    def logits(group):
        pe.wait_ge(ex.ln.normed, 2 * group + 2)
        pe.wait_ge(ex.ln.centred, 3 + group)
        for half in range(2):
            for pr in (2 * group, 2 * group + 1):
                last = nc.tensor.matmul(m.ps[2 * EXPERTS * (pr % 2):2 * EXPERTS * (pr % 2 + 1), 4 * group + half, :],
                                        m.w_gate[:, :], ex.ln.xh[pr][:, half * BANK:(half + 1) * BANK],
                                        start=True, stop=True)
        last.then_inc(ex.logits_in_psum, 1)

    norm_pe(nc, pe, m, ex.ln, {("back", PAIRS - 1): lambda: logits(0)})
    logits(1)
    for g in range(GROUPS):
        pe.wait_ge(ex.picked, g + 1)
        for q in range(2):
            for c in range(4):
                last = nc.tensor.transpose(m.ps[:, 4 * g + q, c * P:(c + 1) * P],
                                           ex.pick[:, g, (4 * q + c) * P:(4 * q + c + 1) * P], m.identity[:, :])
            last.then_inc(ex.pt_in_psum, 1)
    pe.wait_ge(ex.ln.scaled, PAIRS)
    pe.wait_ge(ex.pt_ready, 2 * GROUPS)
    for g in range(GROUPS):
        for c in range(CHUNKS):
            for k in range(PER_GROUP):
                b = PER_GROUP * g + k
                last = nc.tensor.matmul(m.ps[EXPERTS * k:EXPERTS * (k + 1), POOLED, g * C:(g + 1) * C],
                                        ex.pt[:, c, b * EXPERTS:(b + 1) * EXPERTS],
                                        ex.xt[:, c, b // 2, (b % 2) * C:(b % 2 + 1) * C],
                                        start=(c == 0), stop=(c == CHUNKS - 1), skip_group_check=True)
    last.then_inc(ex.pooled_in_psum, 1)
    pe.wait_ge(ex.pooled_copied, 1)
    for g in range(GROUPS):
        last = nc.tensor.transpose(m.ps[0:C, POOLED_TURNED, g * P:(g + 1) * P], ex.pooled_rows[:, g * C:(g + 1) * C],
                                   m.identity[:, :])
    last.then_inc(ex.pooled_turned, 1)
    pe.wait_ge(ex.pooled_ready, 1)
    pe.wait_ge(ex.w_loaded, 64)
    for e in range(EXPERTS):
        q, k = divmod(e, SIDE)
        last = nc.tensor.matmul(m.ps[ROWS * k:ROWS * (k + 1), HIDDEN_BANKS[q // 2], q % 2 * HID:(q % 2 + 1) * HID],
                                ex.pooled[0:C + 1, e, :], ex.w1[0:C + 1, e, :], start=True, stop=True,
                                skip_group_check=True)
        if e % (2 * SIDE) == 2 * SIDE - 1:
            last.then_inc(ex.hidden_in_psum, 1)
    for r in range(EXPERTS // (2 * SIDE)):
        pe.wait_ge(ex.hidden_copied[r % 2], r // 2 + 1)
        for part in range(2 * MH):
            last = nc.tensor.transpose(m.ps[:, HIDDEN_TURNED[r], part * P:(part + 1) * P],
                                       ex.hidden_rows[:, r, part * P:(part + 1) * P], m.identity[:, :])
        last.then_inc(ex.hidden_turned, 1)
    for e in range(EXPERTS):
        q, k = divmod(e, SIDE)
        if e % (2 * SIDE) == 0:
            pe.wait_ge(ex.hidden_ready, q // 2 + 1)
        for part in range(MH):
            last = nc.tensor.matmul(m.ps[ROWS * k:ROWS * (k + 1), ANSWER, q * C:(q + 1) * C],
                                    ex.hidden[:, q // 2, q % 2 * MH + part, k, :], ex.w2[part][:, e, :],
                                    start=(part == 0), stop=(part == MH - 1), skip_group_check=True)
    last.then_inc(ex.answer_in_psum, 1)
    pe.wait_ge(ex.answer_copied, 1)
    for q in range(EXPERTS // SIDE):
        last = nc.tensor.transpose(m.ps[0:C, ANSWER_TURNED[q // 4], q % 4 * P:(q % 4 + 1) * P],
                                   ex.answer_rows[:, q * C:(q + 1) * C], m.identity[:, :])
    last.then_inc(ex.answer_turned, 1)
    pe.wait_ge(ex.answer_ready, 1)
    for g in range(GROUPS):
        last = nc.tensor.transpose(m.ps[:, ANSWERS, g * C:(g + 1) * C], ex.answer[0:C, g * P:(g + 1) * P],
                                   m.identity[0:C, 0:C])
    last.then_inc(ex.answers_in_psum, 1)
    pe.wait_ge(ex.answer_sb, 1)
    for pr in range(PAIRS):
        if pr >= 2:
            pe.wait_ge(ex.joined, 2 * (pr - 1))
        for half in range(2):
            for image in range(2):
                b = 2 * pr + image
                rows = slice(EXPERTS * (b % PER_GROUP), EXPERTS * (b % PER_GROUP + 1))
                last = nc.tensor.matmul(m.ps[C * image:C * image + C, 4 + 2 * (pr % 2) + half, :],
                                        ex.answers[rows, b // PER_GROUP, :],
                                        ex.pick[rows, b // PER_GROUP, half * BANK:(half + 1) * BANK],
                                        start=True, stop=True, skip_group_check=True)
            last.then_inc(ex.spread, 1)


def experts_act(nc, act, m, ex):
    def logits(g):
        act.wait_ge(ex.logits_in_psum, g + 1)
        for half in range(2):
            nc.scalar.activation(ex.pick[:, g, half * BANK:(half + 1) * BANK], m.ps[:, 4 * g + half, :],
                                 ACT.Identity, bias=m.b_gate[:, 0:1]).then_inc(ex.logits_ready, 1)

    def exponentials(g):
        act.wait_ge(ex.gate_max, g + 1)
        nc.scalar.activation(ex.pick[:, g, :], ex.pick[:, g, :], ACT.Exp, bias=ex.neg_max[:, g:g + 1],
                             accum_out=ex.gate_sum[:, g:g + 1]).then_inc(ex.gate_exp, 1)

    norm_act(nc, act, m, ex.ln, {PAIRS: lambda: logits(0)})
    exponentials(0)
    logits(1)
    exponentials(1)
    for g in range(GROUPS):
        for q in range(2):
            act.wait_ge(ex.pt_in_psum, 2 * g + q + 1)
            nc.scalar.copy(ex.pt[:, 4 * q:4 * q + 4, g * P:(g + 1) * P],
                           m.ps[:, 4 * g + q, :].rearrange("p (c n) -> p c n", c=4)).then_inc(ex.pt_ready, 1)
    for r in range(0, EXPERTS // (2 * SIDE), 2):
        act.wait_ge(ex.hidden_in_psum, r + 1)
        nc.scalar.copy(ex.hidden_rows[:, r, :], m.ps[:, HIDDEN_BANKS[r], :]).then_inc(ex.hidden_copied[0], 1)
    for r in range(EXPERTS // (2 * SIDE)):
        act.wait_ge(ex.hidden_turned, r + 1)
        nc.scalar.activation(ex.hidden[:, r, :, :, :].rearrange("p a k b -> p (a k b)"), m.ps[:, HIDDEN_TURNED[r], :],
                             ACT.Gelu).then_inc(ex.hidden_ready, 1)


def experts_dve(nc, dve, m, ex):
    norm_dve(nc, dve, m, ex.ln)
    for g in range(GROUPS):
        dve.wait_ge(ex.logits_ready, 2 * g + 2)
        nc.vector.max(ex.top[:, g, 0, :], ex.pick[:, g, :]).then_inc(ex.top_steps, 1)
        dve.wait_ge(ex.top_steps, g + 1)
        nc.vector.tensor_scalar(ex.neg_max[:, g:g + 1], ex.top[:, g, 0, 0:1], -1.0, None, ALU.mult
                                ).then_inc(ex.gate_max, 1)
        dve.wait_ge(ex.gate_exp, g + 1)
        nc.vector.max(ex.top[:, g, 1, :], ex.pick[:, g, :]).then_inc(ex.pick_steps, 1)
        nc.vector.reciprocal(ex.gate_rsum[:, g:g + 1], ex.gate_sum[:, g:g + 1]).then_inc(ex.rsum_ready, 1)
        dve.wait_ge(ex.pick_steps, 3 * g + 1)
        nc.vector.match_replace(ex.rest[:, g, :], ex.top[:, g, 1, :], ex.pick[:, g, :], 0.0).then_inc(ex.pick_steps, 1)
        dve.wait_ge(ex.pick_steps, 3 * g + 2)
        nc.vector.tensor_tensor(ex.rest[:, g, :], ex.pick[:, g, :], ex.rest[:, g, :], ALU.subtract
                                ).then_inc(ex.pick_steps, 1)
        dve.wait_ge(ex.pick_steps, 3 * g + 3)
        dve.wait_ge(ex.rsum_ready, g + 1)
        nc.vector.tensor_scalar(ex.pick[:, g, :], ex.rest[:, g, :], ex.gate_rsum[:, g:g + 1], None, ALU.mult
                                ).then_inc(ex.picked, 1)
    dve.wait_ge(ex.pooled_in_psum, 1)
    nc.vector.tensor_copy(ex.pooled_rows, m.ps[:, POOLED, 0:GROUPS * C]).then_inc(ex.pooled_copied, 1)
    dve.wait_ge(ex.pooled_turned, 1)
    dve.wait_ge(ex.pooled_set, 2)
    nc.vector.tensor_copy(ex.pooled[0:C, :, 0:NIMG].rearrange("p e b -> p b e"),
                          m.ps[0:C, POOLED_TURNED, 0:NIMG * EXPERTS].rearrange("p (b e) -> p b e", b=NIMG)
                          ).then_inc(ex.pooled_ready, 1)
    for r in range(1, EXPERTS // (2 * SIDE), 2):
        dve.wait_ge(ex.hidden_in_psum, r + 1)
        nc.vector.tensor_copy(ex.hidden_rows[:, r, :], m.ps[:, HIDDEN_BANKS[r], :]).then_inc(ex.hidden_copied[1], 1)
    dve.wait_ge(ex.answer_in_psum, 1)
    nc.vector.tensor_copy(ex.answer_rows, m.ps[:, ANSWER, :]).then_inc(ex.answer_copied, 1)
    dve.wait_ge(ex.answer_turned, 1)
    nc.vector.tensor_copy(ex.answer[0:C, :].rearrange("p (b e) -> p e b", b=NIMG),
                          m.ps[0:C, ANSWER_TURNED[0]:ANSWER_TURNED[1] + 1, :].rearrange("p a n -> p (a n)").rearrange(
                              "p (e b) -> p e b", b=ROWS)[:, :, 0:NIMG]).then_inc(ex.answer_ready, 1)
    dve.wait_ge(ex.answers_in_psum, 1)
    nc.vector.tensor_tensor(ex.answers[:, :, :], m.ps[:, ANSWERS, 0:GROUPS * C].rearrange("p (g c) -> p g c", g=GROUPS),
                            ex.w2_bias.unsqueeze(1).to_broadcast([P, GROUPS, C]), ALU.add).then_inc(ex.answer_sb, 1)
    for pr in range(PAIRS):
        for half in range(2):
            cols = slice(half * BANK, (half + 1) * BANK)
            dve.wait_ge(ex.spread, 2 * pr + half + 1)
            nc.vector.tensor_tensor(m.tokens[:, pr, cols], m.tokens[:, pr, cols],
                                    m.ps[:, 4 + 2 * (pr % 2) + half, :], ALU.add).then_inc(ex.joined, 1)


class Memory:
    pass


def program(nc, a, out):
    ctx = ExitStack()
    with ctx:
        def sb(name, shape, dt=F32):
            return ctx.enter_context(nc.sbuf_tensor(name, shape, dt))

        def sem(name):
            return ctx.enter_context(nc.semaphore(name))

        m = Memory()
        m.ps = ctx.enter_context(nc.psum_tensor("banks", [P, 8, BANK], F32))
        m.out = m.ps[:, 0:2, :].rearrange("p b n -> p (b n)")
        m.HY, m.HX, m.COORD, m.YB = 2, 4, 5, 6
        m.sel_coord = sb("sel_coord", [P, TAPS, P], F16)
        m.coord_bias = sb("coord_bias", [P, TAPS])
        m.hat_scale = sb("hat_scale", [P, 1])
        m.sel_x = sb("sel_x", [P, P], F16)
        m.sel_y = sb("sel_y", [P, NSEL, P], F16)
        m.identity = sb("identity", [P, P])
        m.zeros = sb("zeros", [P, BANK], F16)
        m.source = sb("source", [P, HP * W])
        m.dist = sb("dist", [P, 2, BANK])
        m.hat = sb("hat", [P, TAP_SLOTS, PIX])
        hi_lo = sb("hi_lo", [P, 2, TAP_SLOTS, PIX], F16)
        m.hi, m.lo = hi_lo[:, 0, :, :], hi_lo[:, 1, :, :]
        m.stack = sb("stack", [P, TAP_SLOTS, 2, PIX], F16)
        m.hx = sb("hx", [P, TAP_SLOTS, 2, PIX])
        m.y = sb("y", [P, NCHUNK, 2, 192])
        m.s = sb("s", [P, S_SLOTS, 2 * SPAN])
        m.tokens = sb("tokens", [P, PAIRS, PIX])
        bn = sb("bn", [P, 2, 4])
        bn_inv = sb("bn_inv", [P, 2])
        bn_shift = sb("bn_shift", [P, 2])
        bn_tmp = sb("bn_tmp", [P, 4])
        m.abs_max = sb("abs_max", [P, PAIRS + 1])
        m.off32 = m.s[:, 0:2, :]
        m.parts = m.s[:, 2:5, :].bitcast(BF16).rearrange("p a (b n) -> p (a b) n", b=2).rearrange(
            "p (s k) n -> p s k n", s=2)
        far = sb("far", [1, 6])
        far_flag = sb("far_flag", [1, 2], I32)
        m.b_off = sb("b_off", [P, 2])
        eps_bn = sb("eps_bn", [P, 1])

        loaded = sem("loaded")
        prepared = sem("prepared")
        bn_sqrt = sem("bn_sqrt")
        bn_steps = sem("bn_steps")
        bn_ready = sem("bn_ready")

        convs, places = [], []
        off = sb("off", [P, PAIRS + 1, PIX], BF16)
        pxpy = m.source[0:2, 0:PIX]
        pxpy16 = m.s[0:2, 2, :].bitcast(BF16)
        m.convs = convs
        m.x_loaded = [sem(f"x_loaded{i}") for i in range(PAIRS)]
        m.conv1_loaded, m.prepared, m.pxpy_placed = sem("conv1_loaded"), prepared, sem("pxpy_placed")
        w_off_loaded, pxpy_loaded, pxpy_cast = sem("w_off_loaded"), sem("pxpy_loaded"), sem("pxpy_cast")
        for k in range(2):
            cv = Conv()
            cv.k = k
            spare = k * ((PAIRS + 1) * (WINDOW + PIX) - PAIRS * HP * WP)
            place = sb(f"src{k}", [P, PAIRS * HP * WP + spare])
            places.append(place)
            cv.src = place[:, 0:PAIRS * HP * WP].rearrange("p (i n) -> p i n", i=PAIRS)
            cv.off = off
            cv.w_off = sb(f"w_off{k}", [P, TAPS, 2 * NOFF])
            cv.w_dc = sb(f"w_dc{k}", [P, TAPS, C])
            cv.off_in_psum = sem(f"c{k}_off_in_psum")
            cv.max_ready = sem(f"c{k}_max_ready")
            cv.max_turned = sem(f"c{k}_max_turned")
            cv.max_steps = sem(f"c{k}_max_steps")
            cv.flag_ready = sem(f"c{k}_flag_ready")
            cv.pair_free = sem(f"c{k}_pair_free")
            cv.off_read = sem(f"c{k}_off_read")
            cv.split = sem(f"c{k}_split")
            cv.moved = [sem(f"c{k}_moved{i}") for i in range(2)]
            made = {}

            def shared(name, made=made):
                if name not in made:
                    made[name] = sem(name)
                return made[name]

            cv.near = Sampler(shared, f"c{k}", near_steps())
            cv.all = Sampler(shared, f"c{k}", all_steps())
            convs.append(cv)

        def finish0(i):
            dst = convs[1].src[:, bass.ds(i, 1), :].rearrange("p a (r c) -> p (a r) c", c=WP)
            return nc.scalar.activation(dst[:, PADR:PADR + H, PADC:PADC + W],
                                        m.out.rearrange("p (r c) -> p r c", c=W), ACT.Relu,
                                        bias=bn_shift[:, 0:1], scale=bn_inv[:, 0:1])

        def finish1(i):
            return nc.scalar.activation(m.tokens[:, bass.ds(i, 1), :].rearrange("p a n -> p (a n)"), m.out,
                                        ACT.Identity, bias=bn_shift[:, 1:2], scale=bn_inv[:, 1:2])

        convs[0].finish, convs[1].finish = finish0, finish1

        at = Attention()
        hx_all = m.hx[:, :, :, :].rearrange("p a b n -> p (a b n)")
        hat_all = m.hat[:, :, :].rearrange("p a n -> p (a n)")
        s_all = m.s[:, :, :].rearrange("p a n -> p (a n)")
        y_all = m.y[:, :, :, :].rearrange("p a b n -> p (a b n)")
        src0, src1 = places
        at.xh = src1[:, :].rearrange("p (i n) -> p i n", i=PAIRS + 1)
        at.windows = src0[:, 0:2048].rearrange("p (s j n) -> p s j n", s=4, j=TILES)
        at.pair_windows = src0[:, 2048:3072].rearrange("p (s j a k) -> p s j a k", s=2, j=TILES, a=2)
        at.g = hx_all[:, 0:2048].rearrange("p (s g j n) -> p s g j n", s=2, g=HG, j=TILES)
        at.p = hx_all[:, 2048:4096].rearrange("p (s a n) -> p s a n", s=2, a=2)
        at.pt = hx_all[:, 4096:5120].rearrange("p (a n) -> p a n", a=2)
        at.xw = hat_all[:, 0:2048].rearrange("p (s a j n) -> p s a j n", s=2, a=2, j=TILES)
        at.z = hat_all[:, 2048:3072].rearrange("p (a n) -> p a n", a=2)
        at.a_heads = s_all[:, 0:1024].rearrange("p (h n) -> p h n", h=HEADS)
        at.b_heads = y_all[:, 8192:8448].rearrange("p (h n) -> p h n", h=H4)
        at.stats = sb("stats", [P, 2, 3, 2, TILES * HG])
        at.mark = sb("mark", [P, 3])
        at.ln, ex = LayerNorm(), Experts()
        ex.ln = LayerNorm()
        at.ln.xh = [at.xh[:, pr, WINDOW:WINDOW + PIX] for pr in range(PAIRS)]
        at.ln.xt = [hx_all[:, 2048 + pr * PIX:2048 + (pr + 1) * PIX].rearrange("p (b n) -> p b n", n=P)
                    for pr in range(PAIRS)]
        ex.ln.xh = [src0[:, pr * PIX:(pr + 1) * PIX] for pr in range(PAIRS)]
        ex.xt = src1[:, 0:4096].rearrange("p (c r n) -> p c r n", c=CHUNKS, r=PAIRS)
        ex.ln.xt = [ex.xt[:, :, pr, :] for pr in range(PAIRS)]
        norm_stats = sb("norm_stats", [P, 3, PAIRS, STATS])
        for ln in (at.ln, ex.ln):
            ln.mean, ln.squares, ln.rstd = (norm_stats[:, k, :, :] for k in range(3))
            ln.square = s_all[:, 1024:3072].rearrange("p (s b n) -> p s b n", s=2, n=P)
        for name, ln in (("at", at.ln), ("ex", ex.ln)):
            ln.tokens_ready = sem(name + "_tokens_ready")
            ln.turned = sem(name + "_turned")
            ln.summed = sem(name + "_summed")
            ln.mean_ready = sem(name + "_mean_ready")
            ln.centred = sem(name + "_centred")
            ln.squared = sem(name + "_squared")
            ln.squares_summed = sem(name + "_squares_summed")
            ln.std_ready = sem(name + "_std_ready")
            ln.rstd_ready = sem(name + "_rstd_ready")
            ln.scaled = sem(name + "_scaled")
            ln.back_in_psum = sem(name + "_back_in_psum")
            ln.normed = sem(name + "_normed")
        at.g_in_psum = sem("at_g_in_psum")
        at.g_ready = sem("at_g_ready")
        at.xw_in_psum = sem("at_xw_in_psum")
        at.xw_ready = sem("at_xw_ready")
        at.scores_in_psum = sem("at_scores_in_psum")
        at.shifted = sem("at_shifted")
        at.probs_ready = sem("at_probs_ready")
        at.pt_in_psum = sem("at_pt_in_psum")
        at.pt_ready = sem("at_pt_ready")
        at.z_in_psum = sem("at_z_in_psum")
        at.z_ready = sem("at_z_ready")
        at.projected = sem("at_projected")
        at.added = sem("at_added")
        at.windows_ready = sem("at_windows_ready")
        at.pair_windows_ready = sem("at_pair_windows_ready")
        at.exp_ready = sem("at_exp_ready")
        at.max_ready = sem("at_max_ready")
        at.sum_ready = sem("at_sum_ready")
        at.rsum_ready = sem("at_rsum_ready")
        w_attn = y_all[0:C, 0:4 * HEADS * C].rearrange("p (k n) -> p k n", k=4)
        m.identity16 = sb("identity16", [P, P], F16)
        m.mask = sb("mask", [P, BANK], F16)
        m.eps_ln = sb("eps_ln", [P, 1])
        m.bu = sb("bu", [P, 1])
        m.image_of = sb("image_of", [P, 2])
        m.w_gate = sb("w_gate", [P, 2 * EXPERTS])
        m.b_gate = sb("b_gate", [P, 1])

        ex.w1 = y_all[:, 0:8192].rearrange("p (e n) -> p e n", e=EXPERTS)
        ex.w2 = [buffer.bitcast(F32)[:, 0:EXPERTS * C].rearrange("p (e c) -> p e c", e=EXPERTS)
                 for buffer in (m.stack[:, :, :, :].rearrange("p a b n -> p (a b n)"),
                                hi_lo[:, :, :, :].rearrange("p a b n -> p (a b n)"))]
        ex.w2_bias = y_all[:, 8576:8640]
        ex.pick = hx_all[:, 0:2048].rearrange("p (g n) -> p g n", g=GROUPS)
        ex.rest = hx_all[:, 2048:4096].rearrange("p (g n) -> p g n", g=GROUPS)
        ex.pt = hx_all[:, 4096:6144].rearrange("p (c n) -> p c n", c=CHUNKS)
        ex.pooled = hat_all[:, 0:1024].rearrange("p (e b) -> p e b", e=EXPERTS)
        ex.pooled_rows = hat_all[:, 1024:1152]
        ex.hidden_rows = src0[:, 0:2048].rearrange("p (r n) -> p r n", r=4)
        ex.hidden = src0[:, 2048:4096].rearrange("p (r a k b) -> p r a k b", r=4, a=2 * MH, k=SIDE)
        ex.answer_rows = hat_all[:, 1152:1664]
        ex.answer = hat_all[:, 1664:1920]
        ex.answers = y_all[:, 8448:8576].rearrange("p (g n) -> p g n", g=GROUPS)
        ex.top = sb("top", [P, GROUPS, 2, TOPK])
        ex.neg_max = sb("neg_max", [P, GROUPS])
        ex.gate_sum = sb("gate_sum", [P, GROUPS])
        ex.gate_rsum = sb("gate_rsum", [P, GROUPS])
        ex.logits_in_psum = sem("ex_logits_in_psum")
        ex.picked = sem("ex_picked")
        ex.pt_in_psum = sem("ex_pt_in_psum")
        ex.pt_ready = sem("ex_pt_ready")
        ex.pooled_in_psum = sem("ex_pooled_in_psum")
        ex.pooled_ready = sem("ex_pooled_ready")
        ex.w_loaded = sem("ex_w_loaded")
        ex.hidden_in_psum = sem("ex_hidden_in_psum")
        ex.hidden_ready = sem("ex_hidden_ready")
        ex.answer_in_psum = sem("ex_answer_in_psum")
        ex.answer_ready = sem("ex_answer_ready")
        ex.answer_turned = sem("ex_answer_turned")
        ex.answer_sb = sem("ex_answer_sb")
        ex.joined = sem("ex_joined")
        ex.spread = sem("ex_spread")
        ex.logits_ready = sem("ex_logits_ready")
        ex.gate_max = sem("ex_gate_max")
        ex.gate_exp = sem("ex_gate_exp")
        ex.top_steps = sem("ex_top_steps")
        ex.pick_steps = sem("ex_pick_steps")
        ex.rsum_ready = sem("ex_rsum_ready")
        ex.pooled_set = sem("ex_pooled_set")
        ex.pooled_copied = sem("ex_pooled_copied")
        ex.pooled_turned = sem("ex_pooled_turned")
        ex.hidden_copied = [sem(f"ex_hidden_copied{i}") for i in range(2)]
        ex.hidden_turned = sem("ex_hidden_turned")
        ex.answer_copied = sem("ex_answer_copied")
        ex.answers_in_psum = sem("ex_answers_in_psum")

        heads_loaded = sem("heads_loaded")
        heads_cleared = sem("heads_cleared")
        heads_in_psum, heads_ready, cleared = sem("heads_in_psum"), sem("heads_ready"), sem("cleared")
        out_done = sem("out_done")
        m.residual, m.tokens_ready = sem("residual"), at.ln.tokens_ready

        block = ctx.enter_context(nc.Block())
        conv1_loads = [(convs[0].w_dc[:, :, :], a["w_dc1"]), (m.coord_bias[:, :], a["coord_bias"]),
                       (m.sel_coord[:, :, :], a["sel_coord"]), (m.sel_x[:, :], a["sel_x"])]
        loads = [(m.sel_y[:, :, :], a["sel_y"]), (m.identity[:, :], a["identity"]),
                 (convs[1].w_off[:, :, :], a["w_off2"]), (convs[1].w_dc[:, :, :], a["w_dc2"]),
                 (m.identity16[:, :], a["identity16"]), (m.mask[:, :], a["mask"]), (m.bu[:, :], a["bu"]),
                 (m.image_of[:, :], a["image_of"]),
                 (m.w_gate[:, :], a["w_gate"]), (m.b_gate[:, :], a["b_gate"])]
        NLOAD = 16 * len(loads)

        @block.sync
        def _(sp):
            sp.dma_start(convs[0].w_off[:, :, :], a["w_off1"]).then_inc(w_off_loaded, 16)
            sp.dma_start(m.b_off[:, :], a["b_off"]).then_inc(w_off_loaded, 16)
            sp.dma_start(bn[:, :, :], a["bn"]).then_inc(w_off_loaded, 16)
            sp.dma_start(pxpy, a["pxpy"]).then_inc(pxpy_loaded, 16)
            for i in range(2):
                sp.dma_start(convs[0].src[:, i, :], a["x"][:, i, :]).then_inc(m.x_loaded[i], 16)
            sp.wait_ge(pxpy_cast, 1)
            for i in range(PAIRS):
                sp.dma_start(off[PX_ROW:NCOORD, i, :], pxpy16).then_inc(m.pxpy_placed, 16)
            for dst, src in conv1_loads:
                sp.dma_start(dst, src).then_inc(m.conv1_loaded, 16)
            for i in range(2, PAIRS):
                sp.dma_start(convs[0].src[:, i, :], a["x"][:, i, :]).then_inc(m.x_loaded[i], 16)
            for dst, src in loads:
                sp.dma_start(dst, src).then_inc(loaded, 16)
            for cv in convs:
                offsets_sp(nc, sp, m, cv)
                sp.wait_ge(cv.flag_ready, 1)
                flag = nc.sync.value_load(far_flag[0:1, cv.k:cv.k + 1], min_val=0, max_val=1)
                with sp.If(flag == 0):
                    sampler_sp(nc, sp, m, cv, cv.near)
                with sp.Else():
                    sampler_sp(nc, sp, m, cv, cv.all)
            sp.wait_ge(convs[1].pair_free, 1 + PAIRS)
            sp.wait_ge(convs[1].near.y_ready, PAIRS * NY + FIRST_Y)
            sp.dma_start(w_attn, a["w_attn"]).then_inc(heads_loaded, 16)
            sp.wait_ge(heads_in_psum, 2)
            sp.dma_start(ex.w1[0:C + 1, :, :], a["w1"]).then_inc(ex.w_loaded, 16)
            for k in range(MH):
                sp.dma_start(ex.w2[k], a["w2"][:, k, :, :]).then_inc(ex.w_loaded, 16)
            sp.dma_start(ex.w2_bias, a["w2_bias"]).then_inc(ex.w_loaded, 16)
            for i in range(PAIRS):
                sp.wait_ge(ex.joined, 2 * i + 2)
                sp.dma_start(out[i], m.tokens[:, i, :]).then_inc(out_done, 16)
            sp.wait_ge(out_done, 16 * PAIRS)

        @block.gpsimd
        def _(pool):
            nc.gpsimd.memset(m.off32[:, :, :], 0.0).then_inc(prepared, 1)
            nc.gpsimd.memset(eps_bn[:, :], EPS_BN).then_inc(prepared, 1)
            nc.gpsimd.memset(m.hat_scale[:, :], HAT_SCALE).then_inc(prepared, 1)
            nc.gpsimd.memset(m.eps_ln[:, :], EPS_LN).then_inc(prepared, 1)
            pool.wait_ge(pxpy_loaded, 16)
            nc.gpsimd.tensor_copy(pxpy16, pxpy).then_inc(pxpy_cast, 1)
            nc.gpsimd.memset(m.zeros[:, :], 0.0).then_inc(prepared, 1)
            nc.gpsimd.memset(off[:, PAIRS, :], 0.0).then_inc(prepared, 1)
            pool.wait_ge(pxpy_cast, 1)
            pool.wait_ge(m.x_loaded[0], 16)
            for cv in convs:
                if cv.k:
                    pool.wait_ge(convs[0].pair_free, 1 + PAIRS)
                sampler_pool(nc, pool, m, cv, cv.near, start=True)
                if cv.k == 0:
                    nc.gpsimd.memset(convs[1].src[:, :, :], 0.0).then_inc(prepared, 1)
                pool.wait_ge(cv.flag_ready, 1)
                flag = nc.gpsimd.value_load(far_flag[0:1, cv.k:cv.k + 1], min_val=0, max_val=1)
                with pool.If(flag == 0):
                    sampler_pool(nc, pool, m, cv, cv.near)
                with pool.Else():
                    sampler_pool(nc, pool, m, cv, cv.all)
            residual(nc, pool, m, convs[1], PAIRS - 1)
            nc.gpsimd.memset(hat_all[:, 0:2048], 0.0).then_inc(cleared, 1)
            for i in range(PAIRS):
                nc.gpsimd.memset(at.xh[:, i, 0:WINDOW], 0.0).then_inc(cleared, 1)
            nc.gpsimd.memset(at.xh[:, PAIRS, :], 0.0).then_inc(cleared, 1)
            pool.wait_ge(cleared, 2 + PAIRS)
            norm_pool(nc, pool, m, at.ln)
            attention_pool(nc, pool, m, at)
            pool.wait_ge(at.added, 2 + ALL_BLOCKS)
            norm_pool(nc, pool, m, ex.ln)
            pool.wait_ge(ex.ln.scaled, PAIRS)
            nc.gpsimd.memset(ex.pooled[0:C, :, :], 0.0).then_inc(ex.pooled_set, 1)
            nc.gpsimd.memset(ex.pooled[C:C + 1, :, :], 1.0).then_inc(ex.pooled_set, 1)

        @block.scalar
        def _(act):
            act.wait_ge(w_off_loaded, 48)
            act.wait_ge(prepared, 4)
            for k in range(2):
                nc.scalar.activation(bn_tmp[:, k:k + 1], bn[:, k, 3:4], ACT.Sqrt, bias=eps_bn[:, 0:1]
                                     ).then_inc(bn_sqrt, 1)
            for cv in convs:
                offsets_act(nc, act, m, cv)
                if cv.k == 0:
                    act.wait_ge(prepared, 7)
                    act.wait_ge(bn_ready, 2)
                act.wait_ge(cv.flag_ready, 1)
                flag = nc.scalar.value_load(far_flag[0:1, cv.k:cv.k + 1], min_val=0, max_val=1)
                with act.If(flag == 0):
                    sampler_act(nc, act, m, cv, cv.near)
                with act.Else():
                    sampler_act(nc, act, m, cv, cv.all)

            def head_products():
                act.wait_ge(heads_cleared, 1)
                act.wait_ge(heads_in_psum, 2)
                for image in range(2):
                    rows = slice(C * image, C * image + C)
                    nc.scalar.activation(at.a_heads[rows, :, rows],
                                         m.ps[rows, 6, :].rearrange("p (h n) -> p h n", h=HEADS),
                                         ACT.Copy, scale=1.0 / 8.0).then_inc(heads_ready, 1)
                nc.scalar.copy(at.b_heads[:, :, :], m.ps[:, 7, 0:H4 * C].rearrange("p (h n) -> p h n", h=H4)
                               ).then_inc(heads_ready, 1)

            norm_act(nc, act, m, at.ln, {0: head_products})
            attention_act(nc, act, m, at)
            experts_act(nc, act, m, ex)

        @block.vector
        def _(dve):
            dve.wait_ge(prepared, 4)
            dve.wait_ge(bn_sqrt, 2)
            nc.vector.reciprocal(bn_tmp[:, 2:4], bn_tmp[:, 0:2]).then_inc(bn_steps, 1)
            dve.wait_ge(bn_steps, 1)
            nc.vector.tensor_tensor(bn_inv[:, :], bn[:, :, 0], bn_tmp[:, 2:4], ALU.mult).then_inc(bn_steps, 1)
            dve.wait_ge(bn_steps, 2)
            nc.vector.tensor_tensor(bn_tmp[:, 0:2], bn[:, :, 2], bn_inv[:, :], ALU.mult).then_inc(bn_steps, 1)
            dve.wait_ge(bn_steps, 3)
            nc.vector.tensor_tensor(bn_shift[:, :], bn[:, :, 1], bn_tmp[:, 0:2], ALU.subtract
                                    ).then_inc(bn_ready, 2)
            dve.wait_ge(m.pxpy_placed, 16 * PAIRS)
            for cv in convs:
                offsets_dve(nc, dve, m, cv)
                dve.wait_ge(cv.max_turned, 1)
                nc.vector.tensor_reduce(far[0:1, cv.k:cv.k + 1], m.ps[0:1, 0, 0:C + 2 * NOFF], AX.X, ALU.max
                                        ).then_inc(cv.max_steps, 1)
                dve.wait_ge(cv.max_steps, 1)
                nc.vector.tensor_scalar(far_flag[0:1, cv.k:cv.k + 1], far[0:1, cv.k:cv.k + 1], REACH, None,
                                        ALU.is_ge).then_inc(cv.flag_ready, 1)
                nc.vector.tensor_copy(far[0:1, 2 + cv.k:3 + cv.k], far[0:1, cv.k:cv.k + 1]).then_inc(cv.pair_free, 1)
                nc.vector.tensor_copy(far[0:1, 4 + cv.k:5 + cv.k], far[0:1, cv.k:cv.k + 1]
                                      ).then_inc(cv.near.sampled, S_SLOTS)
                dve.wait_ge(cv.flag_ready, 1)
                flag = nc.vector.value_load(far_flag[0:1, cv.k:cv.k + 1], min_val=0, max_val=1)
                with dve.If(flag == 0):
                    sampler_dve(nc, dve, m, cv, cv.near)
                with dve.Else():
                    sampler_dve(nc, dve, m, cv, cv.all)
            dve.wait_ge(convs[1].pair_free, 1 + PAIRS)
            dve.wait_ge(convs[1].pair_free, 1 + PAIRS)
            nc.vector.memset(at.a_heads, 0.0).then_inc(heads_cleared, 1)
            norm_dve(nc, dve, m, at.ln)
            dve.wait_ge(cleared, 1)
            attention_dve(nc, dve, m, at)
            dve.wait_ge(at.added, 2 + ALL_BLOCKS)
            nc.vector.tensor_copy(at.mark[:, 0:1], m.bu[:, 0:1]).then_inc(ex.ln.tokens_ready, PAIRS)
            experts_dve(nc, dve, m, ex)

        @block.tensor
        def _(pe):
            pe.wait_ge(w_off_loaded, 48)
            for cv in convs:
                offsets_pe(nc, pe, m, cv)
                if cv.k == 0:
                    pe.wait_ge(loaded, NLOAD)
                pe.wait_ge(cv.max_ready, PAIRS + 1)
                nc.tensor.transpose(m.ps[0:1, 0, 0:C + 2 * NOFF], m.abs_max[0:C + 2 * NOFF, PAIRS:PAIRS + 1],
                                    m.identity[0:C + 2 * NOFF, 0:C + 2 * NOFF]).then_inc(cv.max_turned, 1)
                for slot in range(2):
                    pe.wait_ge(cv.moved[slot], 96 * PAIRS // 2)
                pe.wait_ge(cv.flag_ready, 1)
                flag = nc.tensor.value_load(far_flag[0:1, cv.k:cv.k + 1], min_val=0, max_val=1)
                with pe.If(flag == 0):
                    sampler_pe(nc, pe, m, cv, cv.near)
                with pe.Else():
                    sampler_pe(nc, pe, m, cv, cv.all)

            def head_products():
                pe.wait_ge(heads_loaded, 16)
                for h in range(HEADS):
                    for image in range(2):
                        last = nc.tensor.matmul(m.ps[C * image:C * image + C, 6, h * C:(h + 1) * C],
                                                w_attn[:, 0, h * C:(h + 1) * C],
                                                w_attn[:, 1, h * C:(h + 1) * C], start=True, stop=True)
                last.then_inc(heads_in_psum, 1)
                for h in range(HEADS):
                    hg, h4 = divmod(h, H4)
                    last = nc.tensor.matmul(m.ps[C * hg:C * hg + C, 7, h4 * C:(h4 + 1) * C],
                                            w_attn[:, 2, h * C:(h + 1) * C], w_attn[:, 3, h * C:(h + 1) * C],
                                            start=True, stop=True)
                last.then_inc(heads_in_psum, 1)

            pe.wait_ge(convs[1].pair_free, 1 + PAIRS)
            norm_pe(nc, pe, m, at.ln, {("turn", 2): head_products, ("back", 0): lambda: pe.wait_ge(heads_ready, 3)})
            pe.wait_ge(at.ln.normed, PAIRS)
            pe.wait_ge(cleared, 2 + PAIRS)
            attention_pe(nc, pe, m, at)
            experts_pe(nc, pe, m, ex)


def constants():
    f32, f16 = np.float32, np.float16
    c = {}
    sel = np.zeros((P, TAPS, P), f16)
    bias = np.zeros((P, TAPS), f32)
    q = np.arange(W)
    for t in range(TAPS):
        ky, kx = divmod(t, 3)
        for image in range(2):
            for axis in range(2):
                g = slice(64 * image + 32 * axis, 64 * image + 32 * axis + 32)
                for part in range(3):
                    sel[2 * NOFF * part + NOFF * image + 2 * t + (1 - axis), t, g] = 1
                sel[[PX_ROW, PY_ROW][axis], t, g] = 1
                bias[g, t] = 2 * [kx, ky][axis] - 2 - q
    c["sel_coord"], c["coord_bias"] = sel, bias
    r = np.arange(P)
    part = (r % 64) // 32
    c["sel_x"] = (((part == 0)[:, None]) & ((r % 32)[:, None] == (r % 32)[None, :])).astype(f16) * f16(1 / HAT_SCALE)
    starts = np.array(ALIGNED + SHIFTED)
    c["sel_y"] = ((part == 1)[:, None, None] &
                  ((r % 32)[:, None, None] == (starts[:, None] + (r // 32)[None, :])[None])).astype(f16) * f16(1 / HAT_SCALE)
    c["pxpy"] = np.stack([np.tile(np.arange(W), H), np.repeat(np.arange(H), W)]).astype(f32)
    c["identity"] = np.eye(P, dtype=f32)
    c["image_of"] = np.kron(np.eye(2), np.ones((C, 1))).astype(f32)
    c["identity16"] = (np.eye(P) * MASK_SCALE).astype(f16)
    qq, kk = (np.arange(P) % TQ)[:, None], np.arange(KEYS)[None, :]
    c["mask"] = np.tile(np.where((kk > qq) & (kk <= qq + WINDOW), 0.0, MASKED), (1, TILES * HG)).astype(f16)
    return c


def layout(v):
    d = {}
    x = np.pad(v["x"], ((0, 0), (0, 0), (PADR, PADR), (PADC, PADC)))
    d["x"] = x.reshape(PAIRS, P, HP * WP).transpose(1, 0, 2)
    for k in (1, 2):
        w = v[f"L0_conv_w_off{k}"].transpose(1, 2, 3, 0).reshape(C, TAPS, NOFF)
        blocks = np.zeros((2, C, TAPS, 2, NOFF), w.dtype)
        blocks[0, :, :, 0] = w
        blocks[1, :, :, 1] = w
        d[f"w_off{k}"] = blocks.reshape(P, TAPS, 2 * NOFF)
        w = v[f"L0_conv_w_dc{k}"].transpose(1, 2, 3, 0).reshape(C, TAPS, C)
        d[f"w_dc{k}"] = np.concatenate([w, w])
    b_off = np.stack([np.tile(v[f"L0_conv_b_off{k}"], 2) for k in (1, 2)], 1)
    d["b_off"] = np.zeros((P, 2), b_off.dtype)
    d["b_off"][0:2 * NOFF] = d["b_off"][C:C + 2 * NOFF] = b_off
    d["bn"] = np.stack([np.stack([np.tile(v[f"L0_conv_{n}{k}"], 2) for n in ("g", "beta", "m", "v")], 1)
                        for k in (1, 2)], 1)
    per_head = [v[f"L1_attn_W{n}"].reshape(HEADS, C, C).transpose(1, 0, 2) for n in "qkv"]
    per_head.append(v["L1_attn_Wu"].T.reshape(HEADS, C, C).transpose(1, 0, 2))
    d["w_attn"] = np.stack(per_head, 1).reshape(C, 4, HEADS * C)
    d["bu"] = np.tile(v["L1_attn_bu"], 2)[:, None]
    gate = v["L1_ffn_gate_w"].T
    blocks = np.zeros((2, C, 2, EXPERTS), gate.dtype)
    blocks[0, :, 0] = gate
    blocks[1, :, 1] = gate
    d["w_gate"] = blocks.reshape(P, 2 * EXPERTS)
    d["b_gate"] = np.tile(v["L1_ffn_gate_b"], PER_GROUP)[:, None]
    d["w1"] = v["L1_ffn_weight1"].transpose(1, 0, 2)
    w2 = v["L1_ffn_weight2"]
    d["w2"] = w2[:, :HID].reshape(EXPERTS, MH, P, C).transpose(2, 1, 0, 3)
    d["w2_bias"] = np.tile(w2[:, HID], (PER_GROUP, 1))
    return d


def kernel(**inputs):
    import numpy as _np
    import concourse.bacc as _bacc
    from concourse import mybir as _mybir
    from concourse.bass_utils import run_bass_kernel_spmd as _run

    nc = _bacc.Bacc("TRN2", target_bir_lowering=False, num_devices=1)
    given = {n: _np.asarray(x) for n, x in inputs.items()}
    arrays, aps = {}, {}
    for name, x in {**layout(given), **constants()}.items():
        x = _np.ascontiguousarray(x)
        arrays[f"in_{name}_dram"] = x
        aps[name] = nc.dram_tensor(f"in_{name}_dram", x.shape, _mybir.dt.from_np(x.dtype), kind="ExternalInput").ap()
    out = nc.dram_tensor("out_dram", (PAIRS, P, PIX), F32, kind="ExternalOutput").ap()
    program(nc, aps, out)
    r = _run(nc, [arrays], core_ids=[0])
    return r.results[0]["out_dram"].reshape(NIMG, C, H, W)
```
